# Optimizing a Trainium2 kernel written in Bass

```python
import numpy as np
import jax
import jax.numpy as jnp

def _softmax(x, axis=-1):
    return jax.nn.softmax(x, axis=axis)

def _gelu(x):
    return jax.nn.gelu(x, approximate=True)

def _silu(x):
    return jax.nn.silu(x)

def _sigmoid(x):
    return jax.nn.sigmoid(x)

def _layernorm(x, axis=-1, eps=1e-05):
    m = jnp.mean(x, axis=axis, keepdims=True)
    v = jnp.var(x, axis=axis, keepdims=True)
    return (x - m) / jnp.sqrt(v + eps)

def _scatter_add(tgt, idx, src, axis=0):
    return tgt.at[idx].add(src)

def _segment_sum(src, seg, n):
    return jax.ops.segment_sum(src, seg, n)
kernel_name = 'mk_gnn_resnorm_d2_gnn_r16_bebf88'

def setup_inputs(seed: int=0):
    np.random.seed(seed)
    _w = jnp.asarray

    def _rec_inputs():
        import jax
        import jax.numpy as jnp
        _gk = jax.random.key(seed)
        x = -8.776e-05 + 1 * jax.random.normal(jax.random.fold_in(_gk, 1), (6250, 128), jnp.float32)
        src = jax.random.randint(jax.random.fold_in(_gk, 2), (200000,), 0, 6250, jnp.int32)
        dst = jax.random.randint(jax.random.fold_in(_gk, 3), (200000,), 0, 6250, jnp.int32)
        _o = jnp.argsort(dst, stable=True)
        src = src[_o]
        dst = dst[_o]
        edge_attr_2 = 0.000126197 + 0.999763 * jax.random.normal(jax.random.fold_in(_gk, 11), (200000, 2), jnp.float32)
        return (x, src, dst, edge_attr_2)
    x, src, dst, edge_attr_2 = _rec_inputs()

    def _L0_gnn_setup():
        import jax, jax.numpy as jnp
        import numpy as np
        N = 2500
        E = 40000
        CIN = 128
        COUT = 128
        EDGE_DIM = 2
        BN_EPS = 1e-05
        key = jax.random.key(seed)
        ks = jax.random.split(key, 9)
        din = 2 * CIN + EDGE_DIM
        x = jax.random.normal(ks[0], (N, CIN), dtype=jnp.float32)
        edge_index = jax.random.randint(ks[1], (2, E), 0, N, dtype=jnp.int64)
        edge_attr = jax.random.normal(ks[2], (E, EDGE_DIM), dtype=jnp.float32)
        W1 = jax.random.normal(ks[3], (din, COUT), dtype=jnp.float32) / np.sqrt(din)
        b1 = jax.random.normal(ks[4], (COUT,), dtype=jnp.float32) * 0.01
        gamma = jnp.ones((COUT,), dtype=jnp.float32)
        beta = jnp.zeros((COUT,), dtype=jnp.float32)
        W2 = jax.random.normal(ks[5], (COUT, COUT), dtype=jnp.float32) / np.sqrt(COUT)
        b2 = jax.random.normal(ks[6], (COUT,), dtype=jnp.float32) * 0.01
        return {'x': x, 'edge_index': edge_index, 'edge_attr': edge_attr, 'W1': W1, 'b1': b1, 'gamma': gamma, 'beta': beta, 'W2': W2, 'b2': b2}
    _L0_gnn_all = _L0_gnn_setup()
    _L0_gnn_in = {k: v for k, v in _L0_gnn_all.items() if k in ('W1', 'b1', 'gamma', 'beta', 'W2', 'b2')}
    del _L0_gnn_all

    def _L1_gnn_setup():
        import jax, jax.numpy as jnp
        import numpy as np
        N_NODES = 6250
        D = 128
        N_EDGES = 100000
        key = jax.random.key(seed)
        ks = jax.random.split(key, 10)
        x = jax.random.normal(ks[0], (N_NODES, D), dtype=jnp.float32)
        edge_index = jax.random.randint(ks[1], (2, N_EDGES), 0, N_NODES, dtype=jnp.int32)
        s = 1.0 / np.sqrt(D)
        W0 = jax.random.normal(ks[2], (D, D), dtype=jnp.float32) * s
        b0 = jnp.zeros((D,), jnp.float32)
        W1 = jax.random.normal(ks[3], (D, D), dtype=jnp.float32) * s
        b1 = jnp.zeros((D,), jnp.float32)
        W2 = jax.random.normal(ks[4], (D, D), dtype=jnp.float32) * s
        b2 = jnp.zeros((D,), jnp.float32)
        return {'x': x, 'W0': W0, 'b0': b0, 'W1': W1, 'b1': b1, 'W2': W2, 'b2': b2, 'edge_index': edge_index}
    _L1_gnn_all = _L1_gnn_setup()
    _L1_gnn_in = {k: v for k, v in _L1_gnn_all.items() if k in ('W0', 'b0', 'W1', 'b1', 'W2', 'b2')}
    del _L1_gnn_all
    return {'x': x, 'src': src, 'dst': dst, 'edge_attr_2': edge_attr_2, 'L0_gnn_W1': _L0_gnn_in['W1'], 'L0_gnn_b1': _L0_gnn_in['b1'], 'L0_gnn_gamma': _L0_gnn_in['gamma'], 'L0_gnn_beta': _L0_gnn_in['beta'], 'L0_gnn_W2': _L0_gnn_in['W2'], 'L0_gnn_b2': _L0_gnn_in['b2'], 'L1_gnn_W0': _L1_gnn_in['W0'], 'L1_gnn_b0': _L1_gnn_in['b0'], 'L1_gnn_W1': _L1_gnn_in['W1'], 'L1_gnn_b1': _L1_gnn_in['b1'], 'L1_gnn_W2': _L1_gnn_in['W2'], 'L1_gnn_b2': _L1_gnn_in['b2']}

def reference(x, src, dst, edge_attr_2, L0_gnn_W1, L0_gnn_b1, L0_gnn_gamma, L0_gnn_beta, L0_gnn_W2, L0_gnn_b2, L1_gnn_W0, L1_gnn_b0, L1_gnn_W1, L1_gnn_b1, L1_gnn_W2, L1_gnn_b2):
    import jax
    import jax.numpy as jnp

    def _L0_gnn_ref(x, edge_index, edge_attr, W1, b1, gamma, beta, W2, b2):
        import jax, jax.numpy as jnp
        import numpy as np
        N = 2500
        E = 40000
        CIN = 128
        COUT = 128
        EDGE_DIM = 2
        BN_EPS = 1e-05
        n_nodes = x.shape[0]
        row, col = (edge_index[0], edge_index[1])
        ef = jnp.concatenate([x[row], x[col], edge_attr], axis=-1)
        h = ef @ W1 + b1
        mu = jnp.mean(h, axis=0)
        var = jnp.mean((h - mu) ** 2, axis=0)
        h = (h - mu) * jax.lax.rsqrt(var + BN_EPS) * gamma + beta
        h = jax.nn.relu(h)
        msgs = h @ W2 + b2
        sums = jax.ops.segment_sum(msgs, row, num_segments=n_nodes)
        counts = jax.ops.segment_sum(jnp.ones((msgs.shape[0],), dtype=msgs.dtype), row, num_segments=n_nodes)
        out = sums / (counts + 1.0)[:, None]
        return out + x

    def _L1_gnn_ref(x, W0, b0, W1, b1, W2, b2, edge_index):
        import jax, jax.numpy as jnp
        import numpy as np
        N_NODES = 6250
        D = 128
        N_EDGES = 100000
        N = x.shape[0]
        src, dst = (edge_index[0], edge_index[1])
        loop = jnp.arange(N, dtype=src.dtype)
        src = jnp.concatenate([src, loop])
        dst = jnp.concatenate([dst, loop])
        deg = jax.ops.segment_sum(jnp.ones_like(src, jnp.float32), dst, num_segments=N)
        dinv = jnp.where(deg > 0, jax.lax.rsqrt(deg), 0.0)
        norm = dinv[src] * dinv[dst]

        def conv(h, W, b):
            h = h @ W
            msg = h[src] * norm[:, None]
            out = jax.ops.segment_sum(msg, dst, num_segments=N)
            return out + b
        h = jax.nn.relu(conv(x, W0, b0))
        h = jax.nn.relu(conv(h, W1, b1))
        return conv(h, W2, b2)
    edge_index = jnp.stack([src, dst])
    x = _layernorm(x + _L0_gnn_ref(x, edge_index, edge_attr_2, L0_gnn_W1, L0_gnn_b1, L0_gnn_gamma, L0_gnn_beta, L0_gnn_W2, L0_gnn_b2), axis=-1)
    x = _layernorm(x + _L1_gnn_ref(x, L1_gnn_W0, L1_gnn_b0, L1_gnn_W1, L1_gnn_b1, L1_gnn_W2, L1_gnn_b2, edge_index), axis=-1)
    return x

_drawn_inputs = setup_inputs


def setup_inputs(seed=0):
    import zlib

    import numpy as np

    out = dict(_drawn_inputs(seed))
    spreads = {'L0_gnn_gamma': (1.0, 0.2),
     'L0_gnn_beta': (0.0, 0.285),
     'L1_gnn_b0': (0.0, 0.1),
     'L1_gnn_b1': (0.0, 0.1),
     'L1_gnn_b2': (0.0, 0.1)}
    factors = {'edge_attr_2': 8.0, 'L0_gnn_b1': 8.0, 'L0_gnn_b2': 8.0}
    for name, (base, spread) in spreads.items():
        noise = np.random.default_rng([zlib.crc32(name.encode()), seed]).standard_normal(out[name].shape)
        drawn = base * np.exp(spread * noise) if base else spread * noise
        out[name] = jnp.asarray(drawn.astype(out[name].dtype))
    for name, factor in factors.items():
        out[name] = (out[name] * factor).astype(out[name].dtype)
    return out
```

```python
import concourse.bass as bass
from concourse import mybir
from contextlib import ExitStack

F32 = mybir.dt.float32
I32 = mybir.dt.int32
ALU = mybir.AluOpType
ACT = mybir.ActivationFunctionType
AX = mybir.AxisListType.X

NODES = 6250
EDGES = 200000
D = 128
P = 128
NODE_TILES = -(-NODES // P)
ROWS = NODE_TILES * P
EPT = 125
EDGE_TILES = EDGES // EPT
BN_EPS = 1e-5
LN_EPS = 1e-5
SKIP = 1 << 20


def build(nc, x, src, dst, attr, w1, b1, gamma, beta, w2, b2, conv_w, conv_b, ident_in, lower_in, out):
    ctx = ExitStack()
    with ctx:
        def sb(name, shape, dt=F32):
            return ctx.enter_context(nc.sbuf_tensor(name, shape, dt))

        def ps(name, shape):
            return ctx.enter_context(nc.psum_tensor(name, shape, F32))

        def sem(name):
            return ctx.enter_context(nc.semaphore(name))

        def table(name, width=D):
            return nc.dram_tensor(name, [ROWS, width], F32).ap()

        p_table, q_table = table("p_table"), table("q_table")
        msg_sum, src_count, degree = table("msg_sum"), table("src_count"), table("degree")
        inv_root = table("inv_root")
        x1_table = table("x1_table")
        g_table = [table(f"g_table{c}") for c in range(3)]
        conv_sum = [table(f"conv_sum{c}") for c in range(3)]

        w1_sb = sb("w1_sb", [P, 2, D])
        wa_sb = sb("wa_sb", [P, 2, D])
        w2_sb = sb("w2_sb", [P, D])
        cw_sb = sb("cw_sb", [P, 3, D])
        vec = sb("vec", [P, 7, D])
        B1, GAMMA, BETA, B2, CB = 0, 1, 2, 3, 4
        ident = sb("ident", [P, P])
        lower = sb("lower", [P, P])
        ones = sb("ones", [P, P])
        zeros = sb("zeros", [P, D])

        key_row_i = sb("key_row_i", [P, EPT], I32)
        key_row = sb("key_row", [P, EPT])
        src_i = sb("src_i", [P, 1], I32)
        dst_i = sb("dst_i", [P, 1], I32)
        at = sb("at", [P, 2])
        key_f = sb("key_f", [P, 1])
        equal = sb("equal", [P, EPT])
        earlier = sb("earlier", [P, EPT])
        n_earlier = sb("n_earlier", [P, 1])
        write_f = sb("write_f", [P, 1])
        write_i = sb("write_i", [P, 1], I32)
        from_src = sb("from_src", [P, D])
        from_dst = sb("from_dst", [P, D])
        row_sum = sb("row_sum", [P, D])
        new_row = sb("new_row", [P, D])
        h = [sb(f"h{n}", [P, D]) for n in range(4)]
        mean = sb("mean", [P, D])
        var = sb("var", [P, D])
        scale = sb("scale", [P, D])
        shift = sb("shift", [P, D])
        nx = sb("nx", [P, D])
        nin = sb("nin", [P, D])
        nT = sb("nT", [P, D])
        ncnt = sb("ncnt", [P, D])
        na, nb, n_out, n_out2 = (sb(f"n{c}", [P, D]) for c in "abcd")
        stat = sb("stat", [P, 4])
        root = sb("root", [P, D])

        merged = ps("merged", [P, D])
        total = ps("total", [P, D])
        nps = ps("nps", [P, D])
        npq = ps("npq", [P, D])

        loaded = sem("loaded")
        preset = sem("preset")
        step = sem("step")
        outputs = sem("outputs")
        LOADS = 0

        class Chain:
            def __init__(self, eng):
                self.eng, self.at, self.i = eng, 0, 0

            def __call__(self, ins):
                self.at = self.at + 1
                ins.then_inc(step, 1)
                self.eng.wait_ge(step, self.at)

        block = ctx.enter_context(nc.Block())

        def wait_then(eng, s, v):
            eng.wait_ge(s, v)
            eng.nop(nofuse=True)
        programs = {"sync": [], "gpsimd": [], "tensor": [], "vector": [], "scalar": []}
        chain_box = {}

        small = [(w1_sb[:, :, :], w1[0:2 * D, :].rearrange("(a p) d -> p a d", a=2)),
                 (w2_sb[:, :], w2), (ident[:, :], ident_in), (lower[:, :], lower_in)]
        small += [(wa_sb[:, a, :], w1[2 * D + a:2 * D + a + 1, :].to_broadcast([P, D])) for a in range(2)]
        small += [(cw_sb[:, c, :], conv_w[c]) for c in range(3)]
        small += [(vec[:, n, :], v.to_broadcast([P, D])) for n, v in enumerate([b1, gamma, beta, b2, *conv_b])]

        def setup_sync(eng):
            for to, of in small:
                eng.dma_start(to, of).then_inc(loaded, 16)
            eng.wait_ge(preset, 2)
            for t in (msg_sum, src_count, degree):
                what = ones if t is degree else zeros
                for n in range(NODE_TILES):
                    eng.dma_start(t[n * P:(n + 1) * P, :], what[:, :]).then_inc(loaded, 16)
            eng.wait_ge(loaded, 16 * (len(small) + 3 * NODE_TILES))
        ALL_LOADED = 16 * (len(small) + 3 * NODE_TILES)

        def setup_vector(eng):
            nc.vector.memset(ones[:], 1.0).then_inc(preset, 1)
            nc.vector.memset(zeros[:], 0.0).then_inc(preset, 1)
            eng.wait_ge(preset, 2)
            eng.wait_ge(loaded, ALL_LOADED)

        def node_pass(name, loads, transposed, weights, compute, stores, rows_last=P, before=None):
            got, ready, turned, copied, made, done, stored = (
                sem(f"{name}_{s}") for s in ("got", "ready", "turned", "copied", "made", "done", "stored"))

            def rows(t, i):
                return t[bass.ts(i, P), :]

            def sync(eng):
                with eng.Fori(0, NODE_TILES) as i:
                    for to, of in loads:
                        eng.dma_start(to, rows(of, i)).then_inc(got, 16)
                    wait_then(eng, done, i + 1)
                    for to, of in stores:
                        eng.dma_start(rows(to, i), of).then_inc(stored, 16)
                    wait_then(eng, stored, 16 * len(stores) * (i + 1))

            def vector(eng, chain):
                base = chain.at
                with eng.Fori(0, NODE_TILES) as i:
                    steps = compute.steps
                    chain.at, chain.i = base + i * steps, i
                    eng.wait_ge(got, 16 * len(loads) * (i + 1))
                    if before:
                        before(chain)
                    if transposed is not None:
                        nc.vector.memset(stat[:, 3:4], 0.0).then_inc(ready, 1)
                        eng.wait_ge(turned, i + 1)
                        nc.vector.tensor_copy(nT[:, :], nps[:, :]).then_inc(copied, 1)
                        eng.wait_ge(made, i + 1)
                    compute(chain)
                    nc.vector.memset(stat[:, 3:4], 0.0).then_inc(done, 1)
                    eng.wait_ge(done, i + 1)
                    eng.wait_ge(stored, 16 * len(stores) * (i + 1))
                chain.at = base + NODE_TILES * steps

            def tensor(eng):
                if transposed is None:
                    return
                with eng.Fori(0, NODE_TILES) as i:
                    eng.wait_ge(ready, i + 1)
                    nc.tensor.transpose(nps[:, :], transposed, ident[:, :]).then_inc(turned, 1)
                    eng.wait_ge(copied, i + 1)
                    for w, to in zip(weights, (nps, npq)):
                        last = nc.tensor.matmul(to[:, :], nT[:, :], w, start=True, stop=True)
                    last.then_inc(made, 1)

            programs["sync"].append(sync)
            programs["vector"].append(vector)
            programs["tensor"].append(tensor)
            return stored, 16 * len(stores) * NODE_TILES

        def counted(steps):
            def wrap(f):
                f.steps = steps
                return f
            return wrap

        def inverse_root(c, name, i, to, of, t):
            asked, rooted = roots[name]
            nc.vector.memset(stat[:, 3:4], 0.0).then_inc(asked, 1)
            c.eng.wait_ge(rooted, i + 1)
            c(nc.vector.reciprocal(to, t))
            c(nc.vector.tensor_tensor(t, to, to, ALU.mult))
            c(nc.vector.tensor_tensor(t, t, of, ALU.mult))
            c(nc.vector.tensor_scalar(t, t, -0.5, 1.5, ALU.mult, ALU.add))
            c(nc.vector.tensor_tensor(to, to, t, ALU.mult))
        ROOT_STEPS = 5

        def root_service(name, to, of, times):
            asked, rooted = roots[name] = (sem(f"{name}_root_asked"), sem(f"{name}_rooted"))

            def scalar(eng):
                if times == 1:
                    eng.wait_ge(asked, 1)
                    nc.scalar.activation(to, of, ACT.Sqrt).then_inc(rooted, 1)
                    return
                with eng.Fori(0, times) as i:
                    eng.wait_ge(asked, i + 1)
                    nc.scalar.activation(to, of, ACT.Sqrt).then_inc(rooted, 1)
            programs["scalar"].append(scalar)
        roots = {}

        def layer_norm(c, a, b, to, sc, name):
            c(nc.vector.tensor_reduce(out=sc[:, 0:1], in_=a, op=ALU.add, axis=AX))
            c(nc.vector.tensor_scalar(sc[:, 0:1], sc[:, 0:1], 1.0 / D, None, ALU.mult))
            c(nc.vector.tensor_scalar(a, a, sc[:, 0:1], None, ALU.subtract))
            c(nc.vector.tensor_tensor(b, a, a, ALU.mult))
            c(nc.vector.tensor_reduce(out=sc[:, 1:2], in_=b, op=ALU.add, axis=AX))
            c(nc.vector.tensor_scalar(sc[:, 1:2], sc[:, 1:2], 1.0 / D, LN_EPS, ALU.mult, ALU.add))
            inverse_root(c, name, c.i, sc[:, 2:3], sc[:, 1:2], root[:, 0:1])
            c(nc.vector.tensor_scalar(to, a, sc[:, 2:3], None, ALU.mult))
        LN_STEPS = 7 + ROOT_STEPS

        def edge_pass(name, key, src_rows=None, dst_rows=None, compute=None, sum_to=None, all_sum=False, after=None):
            got, formed, products, updated, scattered = (
                sem(f"{name}_{s}") for s in ("got", "formed", "products", "updated", "scattered"))
            gathered = [sem(f"{name}_gathered{n}") for n in range(3)]
            keys = {"src": src, "dst": dst}.get(key)
            key_i = {"src": src_i, "dst": dst_i}.get(key)
            n_loads = 3 + (keys is not None)
            gathers = [(to, tab, idx) for to, tab, idx in
                       ((from_src, src_rows, src_i), (from_dst, dst_rows, dst_i), (row_sum, sum_to, key_i)) if tab is not None]
            row_keys = keys.rearrange("(t e) a -> t (e a)", e=EPT) if keys is not None else None

            def sync(eng):
                with eng.Fori(0, EDGE_TILES) as i:
                    eng.dma_start(src_i[0:EPT, :], src[bass.ts(i, EPT), :]).then_inc(got, 16)
                    eng.dma_start(dst_i[0:EPT, :], dst[bass.ts(i, EPT), :]).then_inc(got, 16)
                    eng.dma_start(at[0:EPT, :], attr[bass.ts(i, EPT), :]).then_inc(got, 16)
                    if keys is not None:
                        eng.dma_start(key_row_i[0:EPT, :], row_keys[bass.ds(i, 1), :].to_broadcast([EPT, EPT])).then_inc(got, 16)
                    if sum_to is not None:
                        wait_then(eng, scattered, 16 * (i + 1))
                    else:
                        wait_then(eng, updated, i + 1)

            def gpsimd(eng):
                with eng.Fori(0, EDGE_TILES) as i:
                    wait_then(eng, got, 16 * n_loads * (i + 1))
                    for (to, tab, idx), landed in zip(gathers, gathered):
                        nc.gpsimd.indirect_dma_start(to[0:EPT, :], None, tab,
                                                     bass.IndirectOffsetOnAxis(ap=idx[0:EPT, 0:1], axis=0)).then_inc(landed, 16)
                    for _, landed in zip(gathers, gathered):
                        wait_then(eng, landed, 16 * (i + 1))
                    if sum_to is not None:
                        wait_then(eng, updated, i + 1)
                        nc.gpsimd.indirect_dma_start(sum_to, bass.IndirectOffsetOnAxis(ap=write_i[0:EPT, 0:1], axis=0),
                                                     new_row[0:EPT, :], None, bounds_check=ROWS - 1,
                                                     oob_is_err=False).then_inc(scattered, 16)
                        wait_then(eng, scattered, 16 * (i + 1))
                    else:
                        wait_then(eng, updated, i + 1)

            def vector(eng, chain):
                base, steps = chain.at, (compute.steps if compute else 0) + (8 if sum_to is not None else 0)
                with eng.Fori(0, EDGE_TILES) as i:
                    chain.at = base + i * steps
                    e = slice(0, EPT)
                    eng.wait_ge(got, 16 * n_loads * (i + 1))
                    if sum_to is not None:
                        chain(nc.vector.tensor_copy(key_row[e, :], key_row_i[e, :]))
                        chain(nc.vector.tensor_copy(key_f[e, :], key_i[e, :]))
                        chain(nc.vector.tensor_scalar(equal[e, :], key_row[e, :], key_f[e, 0:1], None, ALU.is_equal))
                        chain(nc.vector.tensor_tensor(earlier[e, :], equal[e, :], lower[e, 0:EPT], ALU.mult))
                        chain(nc.vector.tensor_reduce(out=n_earlier[e, :], in_=earlier[e, :], op=ALU.add, axis=AX))
                        chain(nc.vector.tensor_scalar(write_f[e, :], n_earlier[e, :], float(SKIP), None, ALU.mult))
                        chain(nc.vector.tensor_tensor(write_f[e, :], write_f[e, :], key_f[e, :], ALU.add))
                        chain(nc.vector.tensor_copy(write_i[e, :], write_f[e, :]))
                    if gathers:
                        for _, landed in zip(gathers, gathered):
                            eng.wait_ge(landed, 16 * (i + 1))
                    if compute:
                        compute(chain)
                    nc.vector.memset(stat[:, 3:4], 0.0).then_inc(formed, 1)
                    eng.wait_ge(products, i + 1)
                    if sum_to is not None:
                        nc.vector.tensor_tensor(new_row[e, :], row_sum[e, :], merged[e, :], ALU.add).then_inc(updated, 1)
                        eng.wait_ge(updated, i + 1)
                        eng.wait_ge(scattered, 16 * (i + 1))
                    else:
                        nc.vector.memset(stat[:, 2:3], 0.0).then_inc(updated, 1)
                        eng.wait_ge(updated, i + 1)
                chain.at = base + EDGE_TILES * steps
                if after:
                    eng.wait_ge(products, EDGE_TILES + 1)
                    after(chain)

            def tensor(eng):
                result = compute.result if compute else (from_src if src_rows is not None else ones)
                if all_sum:
                    nc.tensor.matmul(total[:, :], ones[:, :], zeros[:, :], start=True, stop=False)
                with eng.Fori(0, EDGE_TILES) as i:
                    eng.wait_ge(formed, i + 1)
                    if all_sum:
                        nc.tensor.matmul(total[:, :], ones[0:EPT, :], result[0:EPT, :], start=False, stop=False).then_inc(products, 1)
                    else:
                        nc.tensor.matmul(merged[0:EPT, :], equal[0:EPT, :], result[0:EPT, :], start=True, stop=True).then_inc(products, 1)
                if all_sum:
                    nc.tensor.matmul(total[:, :], ones[:, :], zeros[:, :], start=False, stop=True).then_inc(products, 1)

            programs["sync"].append(sync)
            programs["gpsimd"].append(gpsimd)
            programs["vector"].append(vector)
            programs["tensor"].append(tensor)
            return scattered, 16 * EDGE_TILES

        e = slice(0, EPT)

        def edge_h(c):
            c(nc.vector.tensor_tensor(h[0][e, :], from_src[e, :], from_dst[e, :], ALU.add))
            c(nc.vector.scalar_tensor_tensor(out=h[1][e, :], in0=wa_sb[e, 0, :], scalar=at[e, 0:1], in1=h[0][e, :], op0=ALU.mult, op1=ALU.add))
            c(nc.vector.scalar_tensor_tensor(out=h[0][e, :], in0=wa_sb[e, 1, :], scalar=at[e, 1:2], in1=h[1][e, :], op0=ALU.mult, op1=ALU.add))

        def fence(name, waits):
            def wait(eng, *_):
                for s, v in waits:
                    eng.wait_ge(s, v)
            for engine in ("sync", "gpsimd", "vector", "tensor"):
                programs[engine].append(wait)

        @counted(2)
        def project(c):
            c(nc.vector.tensor_tensor(na[:, :], nps[:, :], vec[:, B1, :], ALU.add))
            c(nc.vector.tensor_copy(nb[:, :], npq[:, :]))
        fence("tables", [node_pass("project", [(nx[:, :], x)], nx[:, :], [w1_sb[:, 0, :], w1_sb[:, 1, :]], project,
                                   [(p_table, na[:, :]), (q_table, nb[:, :])])])

        counts = [edge_pass("src_count", "src", sum_to=src_count), edge_pass("degree", "dst", sum_to=degree)]
        fence("counts", counts)

        @counted(ROOT_STEPS)
        def rooted_degree(c):
            inverse_root(c, "degree", c.i, na[:, :], ncnt[:, :], root[:, :])
        root_service("degree", root[:, :], ncnt[:, :], NODE_TILES)
        fence("degree", [node_pass("degree_root", [(ncnt[:, :], degree)], None, [], rooted_degree, [(inv_root, na[:, :])])])

        @counted(3)
        def hidden(c):
            edge_h(c)
        hidden.result = h[0]

        def take_mean(c):
            c(nc.vector.tensor_scalar(mean[:, :], total[:, :], 1.0 / EDGES, None, ALU.mult))
        edge_pass("mean", None, p_table, q_table, hidden, all_sum=True, after=take_mean)

        @counted(5)
        def squares(c):
            edge_h(c)
            c(nc.vector.tensor_tensor(h[1][e, :], h[0][e, :], mean[e, :], ALU.subtract))
            c(nc.vector.tensor_tensor(h[2][e, :], h[1][e, :], h[1][e, :], ALU.mult))
        squares.result = h[2]

        root_service("batch", root[:, :], var[:, :], 1)

        def take_scale(c):
            c(nc.vector.tensor_scalar(var[:, :], total[:, :], 1.0 / EDGES, BN_EPS, ALU.mult, ALU.add))
            inverse_root(c, "batch", 0, scale[:, :], var[:, :], root[:, :])
            c(nc.vector.tensor_tensor(scale[:, :], scale[:, :], vec[:, GAMMA, :], ALU.mult))
            c(nc.vector.tensor_tensor(var[:, :], mean[:, :], scale[:, :], ALU.mult))
            c(nc.vector.tensor_tensor(shift[:, :], vec[:, BETA, :], var[:, :], ALU.subtract))
        mean_taken = sem("mean_taken")

        def signal_mean(eng, c):
            nc.vector.memset(stat[:, 3:4], 0.0).then_inc(mean_taken, 1)
        programs["vector"].append(signal_mean)
        programs["tensor"].append(lambda eng: eng.wait_ge(mean_taken, 1))
        edge_pass("var", None, p_table, q_table, squares, all_sum=True, after=take_scale)

        @counted(6)
        def activated(c):
            edge_h(c)
            c(nc.vector.tensor_tensor(h[1][e, :], h[0][e, :], scale[e, :], ALU.mult))
            c(nc.vector.tensor_tensor(h[2][e, :], h[1][e, :], shift[e, :], ALU.add))
            c(nc.vector.tensor_scalar(h[3][e, :], h[2][e, :], 0.0, None, ALU.max))
        activated.result = h[3]
        fence("messages", [edge_pass("messages", "src", p_table, q_table, activated, sum_to=msg_sum)])

        @counted(6 + LN_STEPS)
        def first_norm(c):
            c(nc.vector.tensor_tensor(na[:, :], ncnt[:, :], vec[:, B2, :], ALU.mult))
            c(nc.vector.tensor_tensor(na[:, :], na[:, :], nps[:, :], ALU.add))
            c(nc.vector.tensor_scalar(nb[:, :], ncnt[:, :], 1.0, None, ALU.add))
            c(nc.vector.reciprocal(n_out[:, :], nb[:, :]))
            c(nc.vector.tensor_tensor(na[:, :], na[:, :], n_out[:, :], ALU.mult))
            c(nc.vector.scalar_tensor_tensor(out=nb[:, :], in0=nx[:, :], scalar=2.0, in1=na[:, :], op0=ALU.mult, op1=ALU.add))
            layer_norm(c, nb[:, :], na[:, :], n_out[:, :], stat, "first")
        root_service("first", root[:, 0:1], stat[:, 1:2], NODE_TILES)
        fence("x1", [node_pass("first_norm", [(nx[:, :], x), (nin[:, :], msg_sum), (ncnt[:, :], src_count)], nin[:, :],
                               [w2_sb[:, :]], first_norm, [(x1_table, n_out[:, :])])])

        def scaled(rows):
            @counted(1)
            def f(c):
                c(nc.vector.tensor_tensor(n_out[:, :], nps[:, :], ncnt[:, :], ALU.mult))
            return f

        def hidden_rows(layer):
            def f(c):
                c(nc.vector.tensor_tensor(nb[:, :], nin[:, :], ncnt[:, :], ALU.mult))
                c(nc.vector.tensor_tensor(nb[:, :], nb[:, :], vec[:, CB + layer, :], ALU.add))
                c(nc.vector.tensor_scalar(nin[:, :], nb[:, :], 0.0, None, ALU.max))
            return f

        for layer in range(3):
            compute = scaled(None)
            if layer:
                compute.steps += 3
            stores = [(g_table[layer], n_out[:, :]), (conv_sum[layer], n_out[:, :])]
            fence("g", [node_pass(f"conv{layer}", [(nin[:, :], conv_sum[layer - 1] if layer else x1_table), (ncnt[:, :], inv_root)],
                                  nin[:, :], [cw_sb[:, layer, :]], compute, stores,
                                  before=hidden_rows(layer - 1) if layer else None)])
            fence("sums", [edge_pass(f"sums{layer}", "dst", g_table[layer], sum_to=conv_sum[layer])])

        @counted(3 + LN_STEPS)
        def last_norm(c):
            c(nc.vector.tensor_tensor(nb[:, :], nin[:, :], ncnt[:, :], ALU.mult))
            c(nc.vector.tensor_tensor(na[:, :], nb[:, :], vec[:, CB + 2, :], ALU.add))
            c(nc.vector.tensor_tensor(nb[:, :], na[:, :], nx[:, :], ALU.add))
            layer_norm(c, nb[:, :], na[:, :], n_out[:, :], stat, "last")
        root_service("last", root[:, 0:1], stat[:, 1:2], NODE_TILES)
        node_pass("last_norm", [(nin[:, :], conv_sum[2]), (ncnt[:, :], inv_root), (nx[:, :], x1_table)], None, [], last_norm,
                  [(out, n_out[:, :])])

        @block.sync
        def _(eng):
            setup_sync(eng)
            for f in programs["sync"]:
                f(eng)

        @block.gpsimd
        def _(eng):
            eng.wait_ge(loaded, ALL_LOADED)
            for f in programs["gpsimd"]:
                f(eng)

        @block.tensor
        def _(eng):
            eng.wait_ge(preset, 2)
            eng.wait_ge(loaded, ALL_LOADED)
            for f in programs["tensor"]:
                f(eng)

        @block.scalar
        def _(eng):
            for f in programs["scalar"]:
                f(eng)

        @block.vector
        def _(eng):
            chain = Chain(eng)
            setup_vector(eng)
            for f in programs["vector"]:
                f(eng, chain)


def kernel(x, src, dst, edge_attr_2, L0_gnn_W1, L0_gnn_b1, L0_gnn_gamma, L0_gnn_beta, L0_gnn_W2, L0_gnn_b2,
           L1_gnn_W0, L1_gnn_b0, L1_gnn_W1, L1_gnn_b1, L1_gnn_W2, L1_gnn_b2):
    import numpy as np
    import concourse.bacc as bacc
    from concourse.bass_utils import run_bass_kernel_spmd

    def row(a):
        return np.ascontiguousarray(a).reshape(1, -1)

    x_rows = np.zeros((ROWS, D), np.float32)
    x_rows[:NODES] = np.asarray(x)
    arrays = {
        "x": x_rows, "src": np.asarray(src).reshape(-1, 1), "dst": np.asarray(dst).reshape(-1, 1),
        "attr": np.asarray(edge_attr_2), "w1": np.asarray(L0_gnn_W1), "b1": row(L0_gnn_b1), "gamma": row(L0_gnn_gamma),
        "beta": row(L0_gnn_beta), "w2": np.asarray(L0_gnn_W2), "b2": row(L0_gnn_b2),
        "cw0": np.asarray(L1_gnn_W0), "cw1": np.asarray(L1_gnn_W1), "cw2": np.asarray(L1_gnn_W2),
        "cb0": row(L1_gnn_b0), "cb1": row(L1_gnn_b1), "cb2": row(L1_gnn_b2),
        "ident": np.eye(P, dtype=np.float32), "lower": np.tril(np.ones((P, P), np.float32), -1),
    }
    arrays = {k: np.ascontiguousarray(v) for k, v in arrays.items()}
    nc = bacc.Bacc("TRN2", target_bir_lowering=False, num_devices=1)
    arrays = {"in_" + k: v for k, v in arrays.items()}
    t = {k[3:]: nc.dram_tensor(k, v.shape, mybir.dt.from_np(v.dtype), kind="ExternalInput").ap() for k, v in arrays.items()}
    out = nc.dram_tensor("out", (ROWS, D), F32, kind="ExternalOutput").ap()
    build(nc, t["x"], t["src"], t["dst"], t["attr"], t["w1"], t["b1"], t["gamma"], t["beta"], t["w2"], t["b2"],
          [t["cw0"], t["cw1"], t["cw2"]], [t["cb0"], t["cb1"], t["cb2"]], t["ident"], t["lower"], out)
    r = run_bass_kernel_spmd(nc, [arrays], core_ids=[0])
    return r.results[0]["out"][:NODES]
```

```python
import concourse.bass as bass
from concourse import mybir
from contextlib import ExitStack

F32 = mybir.dt.float32
I32 = mybir.dt.int32
BF16 = mybir.dt.bfloat16
F16 = mybir.dt.float16
ALU = mybir.AluOpType
ACT = mybir.ActivationFunctionType
AX = mybir.AxisListType.X

NODES, EDGES, D, P = 6250, 200000, 128, 128
B = -(-NODES // P)
ROWS = B * P
BN_EPS = LN_EPS = 1e-5
SKIP = 1 << 20
NODE_TILES = B
EPT = 125
EDGE_TILES = EDGES // EPT

TILES = -(-EDGES // P)
RT = 9
RC = -(-TILES // RT)
LEAD = 9
STRIP, HALO, STRIPS, IT, UT = 512, 8, 12, 7, 21
COLS = LEAD + RT * RC + 3
CAP = 34
SLOTS = CAP * B
SPAN = 8
PHASES = 3
CT = 17
CHUNKS = SLOTS // CT
NL = 7
GROUPS = [4, 4, 4, 4, 1]
TURNS = [8, 8, 6]
KA = 18


def general_path(nc, sem, t, out):
    x, src, dst, attr = t["x"], t["src"], t["dst"], t["attr"]
    w1, b1, gamma, beta, w2, b2 = t["w1"], t["b1"], t["gamma"], t["beta"], t["w2"], t["b2"]
    conv_w, conv_b = [t["cw0"], t["cw1"], t["cw2"]], [t["cb0"], t["cb1"], t["cb2"]]
    ident_in, lower_in = t["ident_f"], t["lower"]
    ctx = ExitStack()
    with ctx:
        def sb(name, shape, dt=F32):
            return ctx.enter_context(nc.sbuf_tensor("any_" + name, shape, dt))

        def ps(name, shape):
            return ctx.enter_context(nc.psum_tensor("any_" + name, shape, F32))

        def table(name, width=D):
            return nc.dram_tensor("any_" + name, [ROWS, width], F32).ap()

        p_table, q_table = table("p_table"), table("q_table")
        msg_sum, src_count, degree = table("msg_sum"), table("src_count"), table("degree")
        inv_root = table("inv_root")
        x1_table = table("x1_table")
        g_table = [table(f"g_table{c}") for c in range(3)]
        conv_sum = [table(f"conv_sum{c}") for c in range(3)]

        w1_sb = sb("w1_sb", [P, 2, D])
        wa_sb = sb("wa_sb", [P, 2, D])
        w2_sb = sb("w2_sb", [P, D])
        cw_sb = sb("cw_sb", [P, 3, D])
        vec = sb("vec", [P, 7, D])
        B1, GAMMA, BETA, B2, CB = 0, 1, 2, 3, 4
        ident = sb("ident", [P, P])
        lower = sb("lower", [P, P])
        ones = sb("ones", [P, P])
        zeros = sb("zeros", [P, D])

        key_row_i = sb("key_row_i", [P, EPT], I32)
        key_row = sb("key_row", [P, EPT])
        src_i = sb("src_i", [P, 1], I32)
        dst_i = sb("dst_i", [P, 1], I32)
        at = sb("at", [P, 2])
        key_f = sb("key_f", [P, 1])
        equal = sb("equal", [P, EPT])
        earlier = sb("earlier", [P, EPT])
        n_earlier = sb("n_earlier", [P, 1])
        write_f = sb("write_f", [P, 1])
        write_i = sb("write_i", [P, 1], I32)
        from_src = sb("from_src", [P, D])
        from_dst = sb("from_dst", [P, D])
        row_sum = sb("row_sum", [P, D])
        new_row = sb("new_row", [P, D])
        h = [sb(f"h{n}", [P, D]) for n in range(4)]
        mean = sb("mean", [P, D])
        var = sb("var", [P, D])
        scale = sb("scale", [P, D])
        shift = sb("shift", [P, D])
        nx = sb("nx", [P, D])
        nin = sb("nin", [P, D])
        nT = sb("nT", [P, D])
        ncnt = sb("ncnt", [P, D])
        na, nb, n_out, n_out2 = (sb(f"n{c}", [P, D]) for c in "abcd")
        stat = sb("stat", [P, 4])
        root = sb("root", [P, D])

        merged = ps("merged", [P, D])
        total = ps("total", [P, D])
        nps = ps("nps", [P, D])
        npq = ps("npq", [P, D])

        loaded = sem("any_loaded")
        preset = sem("preset")
        step = sem("step")
        outputs = sem("outputs")
        LOADS = 0

        class Chain:
            def __init__(self, eng):
                self.eng, self.at, self.i = eng, 0, 0

            def __call__(self, ins):
                self.at = self.at + 1
                ins.then_inc(step, 1)
                self.eng.wait_ge(step, self.at)

        def wait_then(eng, s, v):
            eng.wait_ge(s, v)
            eng.nop(nofuse=True)
        programs = {"sync": [], "gpsimd": [], "tensor": [], "vector": [], "scalar": []}
        chain_box = {}

        small = [(w1_sb[:, :, :], w1[0:2 * D, :].rearrange("(a p) d -> p a d", a=2)),
                 (w2_sb[:, :], w2), (ident[:, :], ident_in), (lower[:, :], lower_in)]
        small += [(wa_sb[:, a, :], w1[2 * D + a:2 * D + a + 1, :].to_broadcast([P, D])) for a in range(2)]
        small += [(cw_sb[:, c, :], conv_w[c]) for c in range(3)]
        small += [(vec[:, n, :], v.to_broadcast([P, D])) for n, v in enumerate([b1, gamma, beta, b2, *conv_b])]

        def setup_sync(eng):
            for to, of in small:
                eng.dma_start(to, of).then_inc(loaded, 16)
            eng.wait_ge(preset, 2)
            for t in (msg_sum, src_count, degree):
                what = ones if t is degree else zeros
                for n in range(NODE_TILES):
                    eng.dma_start(t[n * P:(n + 1) * P, :], what[:, :]).then_inc(loaded, 16)
            eng.wait_ge(loaded, 16 * (len(small) + 3 * NODE_TILES))
        ALL_LOADED = 16 * (len(small) + 3 * NODE_TILES)

        def setup_vector(eng):
            nc.vector.memset(ones[:], 1.0).then_inc(preset, 1)
            nc.vector.memset(zeros[:], 0.0).then_inc(preset, 1)
            eng.wait_ge(preset, 2)
            eng.wait_ge(loaded, ALL_LOADED)

        def node_pass(name, loads, transposed, weights, compute, stores, rows_last=P, before=None):
            got, done, stored = (sem(f"{name}_{s}") for s in ("got", "done", "stored"))
            if transposed is not None:
                ready, turned, copied, made = (sem(f"{name}_{s}") for s in ("ready", "turned", "copied", "made"))

            def rows(t, i):
                return t[bass.ts(i, P), :]

            def sync(eng):
                with eng.Fori(0, NODE_TILES) as i:
                    for to, of in loads:
                        eng.dma_start(to, rows(of, i)).then_inc(got, 16)
                    wait_then(eng, done, i + 1)
                    for to, of in stores:
                        eng.dma_start(rows(to, i), of).then_inc(stored, 16)
                    wait_then(eng, stored, 16 * len(stores) * (i + 1))

            def vector(eng, chain):
                base = chain.at
                with eng.Fori(0, NODE_TILES) as i:
                    steps = compute.steps
                    chain.at, chain.i = base + i * steps, i
                    eng.wait_ge(got, 16 * len(loads) * (i + 1))
                    if before:
                        before(chain)
                    if transposed is not None:
                        nc.vector.memset(stat[:, 3:4], 0.0).then_inc(ready, 1)
                        eng.wait_ge(turned, i + 1)
                        nc.vector.tensor_copy(nT[:, :], nps[:, :]).then_inc(copied, 1)
                        eng.wait_ge(made, i + 1)
                    compute(chain)
                    nc.vector.memset(stat[:, 3:4], 0.0).then_inc(done, 1)
                    eng.wait_ge(done, i + 1)
                    eng.wait_ge(stored, 16 * len(stores) * (i + 1))
                chain.at = base + NODE_TILES * steps

            def tensor(eng):
                if transposed is None:
                    return
                with eng.Fori(0, NODE_TILES) as i:
                    eng.wait_ge(ready, i + 1)
                    nc.tensor.transpose(nps[:, :], transposed, ident[:, :]).then_inc(turned, 1)
                    eng.wait_ge(copied, i + 1)
                    for w, to in zip(weights, (nps, npq)):
                        last = nc.tensor.matmul(to[:, :], nT[:, :], w, start=True, stop=True)
                    last.then_inc(made, 1)

            programs["sync"].append(sync)
            programs["vector"].append(vector)
            programs["tensor"].append(tensor)
            return stored, 16 * len(stores) * NODE_TILES

        def counted(steps):
            def wrap(f):
                f.steps = steps
                return f
            return wrap

        def inverse_root(c, name, i, to, of, t):
            asked, rooted = roots[name]
            nc.vector.memset(stat[:, 3:4], 0.0).then_inc(asked, 1)
            c.eng.wait_ge(rooted, i + 1)
            c(nc.vector.reciprocal(to, t))
            c(nc.vector.tensor_tensor(t, to, to, ALU.mult))
            c(nc.vector.tensor_tensor(t, t, of, ALU.mult))
            c(nc.vector.tensor_scalar(t, t, -0.5, 1.5, ALU.mult, ALU.add))
            c(nc.vector.tensor_tensor(to, to, t, ALU.mult))
        ROOT_STEPS = 5

        def root_service(name, to, of, times):
            asked, rooted = roots[name] = (sem(f"{name}_root_asked"), sem(f"{name}_rooted"))

            def scalar(eng):
                if times == 1:
                    eng.wait_ge(asked, 1)
                    nc.scalar.activation(to, of, ACT.Sqrt).then_inc(rooted, 1)
                    return
                with eng.Fori(0, times) as i:
                    eng.wait_ge(asked, i + 1)
                    nc.scalar.activation(to, of, ACT.Sqrt).then_inc(rooted, 1)
            programs["scalar"].append(scalar)
        roots = {}

        def layer_norm(c, a, b, to, sc, name):
            c(nc.vector.tensor_reduce(out=sc[:, 0:1], in_=a, op=ALU.add, axis=AX))
            c(nc.vector.tensor_scalar(sc[:, 0:1], sc[:, 0:1], 1.0 / D, None, ALU.mult))
            c(nc.vector.tensor_scalar(a, a, sc[:, 0:1], None, ALU.subtract))
            c(nc.vector.tensor_tensor(b, a, a, ALU.mult))
            c(nc.vector.tensor_reduce(out=sc[:, 1:2], in_=b, op=ALU.add, axis=AX))
            c(nc.vector.tensor_scalar(sc[:, 1:2], sc[:, 1:2], 1.0 / D, LN_EPS, ALU.mult, ALU.add))
            inverse_root(c, name, c.i, sc[:, 2:3], sc[:, 1:2], root[:, 0:1])
            c(nc.vector.tensor_scalar(to, a, sc[:, 2:3], None, ALU.mult))
        LN_STEPS = 7 + ROOT_STEPS

        def edge_pass(name, key, src_rows=None, dst_rows=None, compute=None, sum_to=None, all_sum=False, after=None):
            got, formed, products, updated = (sem(f"{name}_{s}") for s in ("got", "formed", "products", "updated"))
            scattered = sem(f"{name}_scattered") if sum_to is not None else None
            keys = {"src": src, "dst": dst}.get(key)
            key_i = {"src": src_i, "dst": dst_i}.get(key)
            n_loads = 3 + (keys is not None)
            gathers = [(to, tab, idx) for to, tab, idx in
                       ((from_src, src_rows, src_i), (from_dst, dst_rows, dst_i), (row_sum, sum_to, key_i)) if tab is not None]
            gathered = [sem(f"{name}_gathered{n}") for n in range(len(gathers))]
            row_keys = keys.rearrange("(t e) a -> t (e a)", e=EPT) if keys is not None else None

            def sync(eng):
                with eng.Fori(0, EDGE_TILES) as i:
                    eng.dma_start(src_i[0:EPT, :], src[bass.ts(i, EPT), :]).then_inc(got, 16)
                    eng.dma_start(dst_i[0:EPT, :], dst[bass.ts(i, EPT), :]).then_inc(got, 16)
                    eng.dma_start(at[0:EPT, :], attr[bass.ts(i, EPT), :]).then_inc(got, 16)
                    if keys is not None:
                        eng.dma_start(key_row_i[0:EPT, :], row_keys[bass.ds(i, 1), :].to_broadcast([EPT, EPT])).then_inc(got, 16)
                    if sum_to is not None:
                        wait_then(eng, scattered, 16 * (i + 1))
                    else:
                        wait_then(eng, updated, i + 1)

            def gpsimd(eng):
                with eng.Fori(0, EDGE_TILES) as i:
                    wait_then(eng, got, 16 * n_loads * (i + 1))
                    for (to, tab, idx), landed in zip(gathers, gathered):
                        nc.gpsimd.indirect_dma_start(to[0:EPT, :], None, tab,
                                                     bass.IndirectOffsetOnAxis(ap=idx[0:EPT, 0:1], axis=0)).then_inc(landed, 16)
                    for _, landed in zip(gathers, gathered):
                        wait_then(eng, landed, 16 * (i + 1))
                    if sum_to is not None:
                        wait_then(eng, updated, i + 1)
                        nc.gpsimd.indirect_dma_start(sum_to, bass.IndirectOffsetOnAxis(ap=write_i[0:EPT, 0:1], axis=0),
                                                     new_row[0:EPT, :], None, bounds_check=ROWS - 1,
                                                     oob_is_err=False).then_inc(scattered, 16)
                        wait_then(eng, scattered, 16 * (i + 1))
                    else:
                        wait_then(eng, updated, i + 1)

            def vector(eng, chain):
                base, steps = chain.at, (compute.steps if compute else 0) + (8 if sum_to is not None else 0)
                with eng.Fori(0, EDGE_TILES) as i:
                    chain.at = base + i * steps
                    e = slice(0, EPT)
                    eng.wait_ge(got, 16 * n_loads * (i + 1))
                    if sum_to is not None:
                        chain(nc.vector.tensor_copy(key_row[e, :], key_row_i[e, :]))
                        chain(nc.vector.tensor_copy(key_f[e, :], key_i[e, :]))
                        chain(nc.vector.tensor_scalar(equal[e, :], key_row[e, :], key_f[e, 0:1], None, ALU.is_equal))
                        chain(nc.vector.tensor_tensor(earlier[e, :], equal[e, :], lower[e, 0:EPT], ALU.mult))
                        chain(nc.vector.tensor_reduce(out=n_earlier[e, :], in_=earlier[e, :], op=ALU.add, axis=AX))
                        chain(nc.vector.tensor_scalar(write_f[e, :], n_earlier[e, :], float(SKIP), None, ALU.mult))
                        chain(nc.vector.tensor_tensor(write_f[e, :], write_f[e, :], key_f[e, :], ALU.add))
                        chain(nc.vector.tensor_copy(write_i[e, :], write_f[e, :]))
                    if gathers:
                        for _, landed in zip(gathers, gathered):
                            eng.wait_ge(landed, 16 * (i + 1))
                    if compute:
                        compute(chain)
                    nc.vector.memset(stat[:, 3:4], 0.0).then_inc(formed, 1)
                    eng.wait_ge(products, i + 1)
                    if sum_to is not None:
                        nc.vector.tensor_tensor(new_row[e, :], row_sum[e, :], merged[e, :], ALU.add).then_inc(updated, 1)
                        eng.wait_ge(updated, i + 1)
                        eng.wait_ge(scattered, 16 * (i + 1))
                    else:
                        nc.vector.memset(stat[:, 2:3], 0.0).then_inc(updated, 1)
                        eng.wait_ge(updated, i + 1)
                chain.at = base + EDGE_TILES * steps
                if after:
                    eng.wait_ge(products, EDGE_TILES + 1)
                    after(chain)

            def tensor(eng):
                result = compute.result if compute else (from_src if src_rows is not None else ones)
                if all_sum:
                    nc.tensor.matmul(total[:, :], ones[:, :], zeros[:, :], start=True, stop=False)
                with eng.Fori(0, EDGE_TILES) as i:
                    eng.wait_ge(formed, i + 1)
                    if all_sum:
                        nc.tensor.matmul(total[:, :], ones[0:EPT, :], result[0:EPT, :], start=False, stop=False).then_inc(products, 1)
                    else:
                        nc.tensor.matmul(merged[0:EPT, :], equal[0:EPT, :], result[0:EPT, :], start=True, stop=True).then_inc(products, 1)
                if all_sum:
                    nc.tensor.matmul(total[:, :], ones[:, :], zeros[:, :], start=False, stop=True).then_inc(products, 1)

            programs["sync"].append(sync)
            programs["gpsimd"].append(gpsimd)
            programs["vector"].append(vector)
            programs["tensor"].append(tensor)
            return scattered, 16 * EDGE_TILES

        e = slice(0, EPT)

        def edge_h(c):
            c(nc.vector.tensor_tensor(h[0][e, :], from_src[e, :], from_dst[e, :], ALU.add))
            c(nc.vector.scalar_tensor_tensor(out=h[1][e, :], in0=wa_sb[e, 0, :], scalar=at[e, 0:1], in1=h[0][e, :], op0=ALU.mult, op1=ALU.add))
            c(nc.vector.scalar_tensor_tensor(out=h[0][e, :], in0=wa_sb[e, 1, :], scalar=at[e, 1:2], in1=h[1][e, :], op0=ALU.mult, op1=ALU.add))

        def fence(name, waits):
            def wait(eng, *_):
                for s, v in waits:
                    eng.wait_ge(s, v)
            for engine in ("sync", "gpsimd", "vector", "tensor"):
                programs[engine].append(wait)

        @counted(2)
        def project(c):
            c(nc.vector.tensor_tensor(na[:, :], nps[:, :], vec[:, B1, :], ALU.add))
            c(nc.vector.tensor_copy(nb[:, :], npq[:, :]))
        fence("tables", [node_pass("project", [(nx[:, :], x)], nx[:, :], [w1_sb[:, 0, :], w1_sb[:, 1, :]], project,
                                   [(p_table, na[:, :]), (q_table, nb[:, :])])])

        counts = [edge_pass("src_count", "src", sum_to=src_count), edge_pass("degree", "dst", sum_to=degree)]
        fence("counts", counts)

        @counted(ROOT_STEPS)
        def rooted_degree(c):
            inverse_root(c, "degree", c.i, na[:, :], ncnt[:, :], root[:, :])
        root_service("degree", root[:, :], ncnt[:, :], NODE_TILES)
        fence("degree", [node_pass("degree_root", [(ncnt[:, :], degree)], None, [], rooted_degree, [(inv_root, na[:, :])])])

        @counted(3)
        def hidden(c):
            edge_h(c)
        hidden.result = h[0]

        def take_mean(c):
            c(nc.vector.tensor_scalar(mean[:, :], total[:, :], 1.0 / EDGES, None, ALU.mult))
        edge_pass("mean", None, p_table, q_table, hidden, all_sum=True, after=take_mean)

        @counted(5)
        def squares(c):
            edge_h(c)
            c(nc.vector.tensor_tensor(h[1][e, :], h[0][e, :], mean[e, :], ALU.subtract))
            c(nc.vector.tensor_tensor(h[2][e, :], h[1][e, :], h[1][e, :], ALU.mult))
        squares.result = h[2]

        root_service("batch", root[:, :], var[:, :], 1)

        def take_scale(c):
            c(nc.vector.tensor_scalar(var[:, :], total[:, :], 1.0 / EDGES, BN_EPS, ALU.mult, ALU.add))
            inverse_root(c, "batch", 0, scale[:, :], var[:, :], root[:, :])
            c(nc.vector.tensor_tensor(scale[:, :], scale[:, :], vec[:, GAMMA, :], ALU.mult))
            c(nc.vector.tensor_tensor(var[:, :], mean[:, :], scale[:, :], ALU.mult))
            c(nc.vector.tensor_tensor(shift[:, :], vec[:, BETA, :], var[:, :], ALU.subtract))
        mean_taken = sem("mean_taken")

        def signal_mean(eng, c):
            nc.vector.memset(stat[:, 3:4], 0.0).then_inc(mean_taken, 1)
        programs["vector"].append(signal_mean)
        programs["tensor"].append(lambda eng: eng.wait_ge(mean_taken, 1))
        edge_pass("var", None, p_table, q_table, squares, all_sum=True, after=take_scale)

        @counted(6)
        def activated(c):
            edge_h(c)
            c(nc.vector.tensor_tensor(h[1][e, :], h[0][e, :], scale[e, :], ALU.mult))
            c(nc.vector.tensor_tensor(h[2][e, :], h[1][e, :], shift[e, :], ALU.add))
            c(nc.vector.tensor_scalar(h[3][e, :], h[2][e, :], 0.0, None, ALU.max))
        activated.result = h[3]
        fence("messages", [edge_pass("messages", "src", p_table, q_table, activated, sum_to=msg_sum)])

        @counted(6 + LN_STEPS)
        def first_norm(c):
            c(nc.vector.tensor_tensor(na[:, :], ncnt[:, :], vec[:, B2, :], ALU.mult))
            c(nc.vector.tensor_tensor(na[:, :], na[:, :], nps[:, :], ALU.add))
            c(nc.vector.tensor_scalar(nb[:, :], ncnt[:, :], 1.0, None, ALU.add))
            c(nc.vector.reciprocal(n_out[:, :], nb[:, :]))
            c(nc.vector.tensor_tensor(na[:, :], na[:, :], n_out[:, :], ALU.mult))
            c(nc.vector.scalar_tensor_tensor(out=nb[:, :], in0=nx[:, :], scalar=2.0, in1=na[:, :], op0=ALU.mult, op1=ALU.add))
            layer_norm(c, nb[:, :], na[:, :], n_out[:, :], stat, "first")
        root_service("first", root[:, 0:1], stat[:, 1:2], NODE_TILES)
        fence("x1", [node_pass("first_norm", [(nx[:, :], x), (nin[:, :], msg_sum), (ncnt[:, :], src_count)], nin[:, :],
                               [w2_sb[:, :]], first_norm, [(x1_table, n_out[:, :])])])

        def scaled(rows):
            @counted(1)
            def f(c):
                c(nc.vector.tensor_tensor(n_out[:, :], nps[:, :], ncnt[:, :], ALU.mult))
            return f

        def hidden_rows(layer):
            def f(c):
                c(nc.vector.tensor_tensor(nb[:, :], nin[:, :], ncnt[:, :], ALU.mult))
                c(nc.vector.tensor_tensor(nb[:, :], nb[:, :], vec[:, CB + layer, :], ALU.add))
                c(nc.vector.tensor_scalar(nin[:, :], nb[:, :], 0.0, None, ALU.max))
            return f

        for layer in range(3):
            compute = scaled(None)
            if layer:
                compute.steps += 3
            stores = [(g_table[layer], n_out[:, :]), (conv_sum[layer], n_out[:, :])]
            fence("g", [node_pass(f"conv{layer}", [(nin[:, :], conv_sum[layer - 1] if layer else x1_table), (ncnt[:, :], inv_root)],
                                  nin[:, :], [cw_sb[:, layer, :]], compute, stores,
                                  before=hidden_rows(layer - 1) if layer else None)])
            fence("sums", [edge_pass(f"sums{layer}", "dst", g_table[layer], sum_to=conv_sum[layer])])

        @counted(3 + LN_STEPS)
        def last_norm(c):
            c(nc.vector.tensor_tensor(nb[:, :], nin[:, :], ncnt[:, :], ALU.mult))
            c(nc.vector.tensor_tensor(na[:, :], nb[:, :], vec[:, CB + 2, :], ALU.add))
            c(nc.vector.tensor_tensor(nb[:, :], na[:, :], nx[:, :], ALU.add))
            layer_norm(c, nb[:, :], na[:, :], n_out[:, :], stat, "last")
        root_service("last", root[:, 0:1], stat[:, 1:2], NODE_TILES)
        node_pass("last_norm", [(nin[:, :], conv_sum[2]), (ncnt[:, :], inv_root), (nx[:, :], x1_table)], None, [], last_norm,
                  [(out, n_out[:, :])])

        def sync_program(eng):
            setup_sync(eng)
            for f in programs["sync"]:
                f(eng)

        def gpsimd_program(eng):
            eng.wait_ge(loaded, ALL_LOADED)
            for f in programs["gpsimd"]:
                f(eng)

        def tensor_program(eng):
            eng.wait_ge(preset, 2)
            eng.wait_ge(loaded, ALL_LOADED)
            for f in programs["tensor"]:
                f(eng)

        def scalar_program(eng):
            for f in programs["scalar"]:
                f(eng)

        def vector_program(eng):
            chain = Chain(eng)
            setup_vector(eng)
            for f in programs["vector"]:
                f(eng, chain)
    return sync_program, gpsimd_program, tensor_program, scalar_program, vector_program


def build(nc, t, out):
    def table(name, shape, dt=F32):
        return nc.dram_tensor(name, shape, dt).ap()
    perm = table("perm", [P * SLOTS, 4]); at_dram = table("at_dram", [STRIPS + 1, P, B, STRIP], BF16)
    deg_dram = table("deg_dram", [1, ROWS]); p_dram = table("p_dram", [ROWS, D]); q_dram = table("q_dram", [ROWS, D])
    h_dram = table("h_dram", [CHUNKS, P, CT * D]); s_dram = table("s_dram", [P, B, D + 1])
    outer = ExitStack()
    with outer:
        def mk(ctx):
            return (lambda n, s, d=F32: ctx.enter_context(nc.sbuf_tensor(n, s, d)),
                    lambda n, s, d=F32: ctx.enter_context(nc.psum_tensor(n, s, d)))
        sem = lambda n: outer.enter_context(nc.semaphore(n))
        sb, _ = mk(outer)
        V = nc.vector
        iota_lo = sb("iota_lo", [P, P], F16); identb = sb("identb", [P, P], BF16)
        ones_f = sb("ones_f", [P, P])
        w1 = sb("w1", [P, 2, D]); wrep = sb("wrep", [P, D])
        vec = sb("vec", [P, 7, D])
        sgn = sb("sgn", [P, D])
        masks = sb("masks", [P, 8])
        fits = sb("fits", [P, 1], I32); misfit = sb("misfit", [P, 1]); misfit2 = sb("misfit2", [P, 1]); misfit3 = sb("misfit3", [P, 1]); top = sb("top", [P, B]); over = sb("over", [1, STRIPS + 1])
        alpha = sb("alpha", [P, D]); shift = sb("shift", [P, D]); dummy2 = sb("dummy2", [P, 1])
        one_col = sb("one_col", [P, 1]); zero_col = sb("zero_col", [P, 1])
        S = {n: sem(n) for n in "part_clear cleared src_in dst_in attr_in rec_dst rec_lo low_bits weights_done deg_part keys_done neg_done loaded filled dv set_done hot_ready rank_ready idx_done lo_ready key_ready pair_ready added strip_clear deg_ready deg_read act proj_ready proj_p proj_q proj_in proj_out1 proj_out2 phase1 deg_out misfit_ready misfit_sum fits_ready".split()}
        slot_ready = [sem(f"slot_ready{u}") for u in range(4)]
        scattered = [sem(f"scattered{u}") for u in range(4)]
        stored = [sem(f"stored{u}") for u in range(2)]
        fit_stack = ExitStack()
        fit_sem = lambda n: fit_stack.enter_context(nc.semaphore(n))
        S.update({n: fit_sem(n) for n in "copied recs_in as_done hot2 turned oht_ready mm_done h_done squared stat_done p_in p3_done stats_ready bn_sqrt bn_rooted z_done z_used sum_taken phase2 credits3 node_done chunk_used y_taken yt_ready tail_done v_a v_b ln_ask ln_root out_ready out_sent dv3 credits dv2 s_out nd pe_n act_n root_a root_b x_in bias_done g_taken".split()})
        rec_in = [fit_sem(f"rec_in{u}") for u in range(2)]
        gathered = [fit_sem(f"gathered{u}") for u in range(2)]
        h_out = [fit_sem(f"h_out{u}") for u in range(2)]
        h_in = [fit_sem(f"h_in{u}") for u in range(2)]
        a_in = [fit_sem(f"a_in{u}") for u in range(7)]
        fit_stack.close()
        general = general_path(nc, sem, t, out)

        def put(eng, s, v):
            eng.wait_ge(s, v)
            eng.nop(nofuse=True)

        def barrier(eng, s):
            eng.sem_inc(s, 1)
            eng.wait_ge(s, 5)

        def newton(link, to, of, t):
            link(V.reciprocal(to, t))
            link(V.tensor_tensor(t, to, to, ALU.mult))
            link(V.tensor_tensor(t, t, of, ALU.mult))
            link(V.tensor_scalar(t, t, -0.5, 1.5, ALU.mult, ALU.add))
            link(V.tensor_tensor(to, to, t, ALU.mult))

        one = ExitStack()
        with one:
            sb, ps = mk(one)
            src_i = sb("src_i", [P, COLS], I32); dst_i = sb("dst_i", [P, COLS], I32); first_i = sb("first_i", [P, COLS], I32)
            blk = sb("blk", [P, COLS + 2 * RT]); neg_lo = sb("neg_lo", [P, COLS]); key = sb("key", [P, COLS])
            place = sb("place", [P, COLS]); idx_all = src_i
            rec = sb("rec", [P, COLS, 4])
            offs = sb("offs", [1, STRIPS * IT + 2, 24], I32)
            iotak = sb("iotak", [P, B]); iota_key = sb("iota_key", [P, SPAN * B], F16)
            upper = sb("upper", [P, P], BF16); onesb = sb("onesb", [P, P], BF16); zerob = sb("zerob", [P, STRIP], BF16)
            hot = [sb(f"hot{u}", [P, (RT + 1) * B], BF16) for u in range(2)]
            ranks = [sb(f"ranks{u}", [P, RT * B]) for u in range(2)]; own = ranks
            base = [sb(f"base{u}", [P, B]) for u in range(2)]
            r_f = sb("r_f", [P, 2 * RT]); r_i = sb("r_i", [P, 2 * RT], I32); rhi = sb("rhi", [P, 2 * RT], I32); t_f = sb("t_f", [P, 2 * RT])
            strip = [sb(f"strip{u}", [P, B, STRIP + 2 * HALO], BF16) for u in range(2)]
            sq = [sb(f"sq{u}", [P, P], BF16) for u in range(3)]
            hot_lo = [sb(f"hot_lo{u}", [P, P], BF16) for u in range(NL)]
            hot_key = [sb(f"hot_key{u}", [P, SPAN * B], BF16) for u in range(NL)]
            ix_slot = [sb(f"ix_slot{u}", [P, RT], I32) for u in range(4)]
            rec_slot = [sb(f"rec_slot{u}", [P, RT, 4]) for u in range(4)]
            deg = [sb(f"deg{u}", [1, STRIP]) for u in range(1)]
            dummy = sb("dummy1", [P, 1])
            pr = [ps(f"pr{u}", [P, 512]) for u in range(2)]
            pk = [ps(f"pk{u}", [P, 512]) for u in range(3)]
            pd = ps("pd", [P, 512])
            px = [ps(f"px{u}", [P, 512]) for u in range(2)]
            xT = strip[0][:].rearrange("p b d -> p (b d)").bitcast(F32)[:, 0:ROWS]
            pq = strip[1][:].rearrange("p b d -> p (b d)").bitcast(F32)
            pT, qT = pq[:, 0:ROWS], pq[:, ROWS:2 * ROWS]
            stage = strip[0][:].rearrange("p b d -> p (b d)").bitcast(F32)[:, ROWS:]
            least, above = stage[:, 0:COLS], stage[:, COLS:2 * COLS]
            attr_stage = stage[:, 2 * COLS:2 * COLS + 2 * RT * RC].rearrange("p (t c) -> p t c", c=2)
            low = key[:].bitcast(I32)
            loads = [(w1[:], t["w1"][0:2 * D, :].rearrange("(a p) d -> p a d", a=2)), (wrep[:], t["wrep"]), (masks[:], t["masks"]),
                     (first_i[:], t["d0_row"].to_broadcast([P, COLS])), (least, t["least"].to_broadcast([P, COLS])),
                     (above, t["above"].to_broadcast([P, COLS])), (iota_lo[:], t["iota_lo"]), (iota_key[:], t["iota_key"])]
            loads += [(vec[:, n, :], t[k].to_broadcast([P, D])) for n, k in enumerate(("b1", "gamma", "beta", "b2", "cb0", "cb1", "cb2"))]
            LOADED = 16 * len(loads)
            UPT = IT * UT

            def sp_1(sp):
                for to, of in ((src_i[:], t["src_t"]), (iotak[:], t["iotak"]), (hot_lo[0][:].bitcast(F16), t["upper"]), (hot_lo[1][:].bitcast(F16), t["ident_h"])):
                    sp.dma_start(to, of).then_inc(S["src_in"], 16)
                sp.dma_start(dst_i[:], t["dst_t"]).then_inc(S["dst_in"], 16)
                sp.dma_start(attr_stage, t["attr_t"]).then_inc(S["attr_in"], 16)
                sp.dma_start(perm.rearrange("(p t) c -> p (t c)", p=P), t["empty"]).then_inc(S["filled"], 16)
                for to, of in loads:
                    sp.dma_start(to, of).then_inc(S["loaded"], 16)
                sp.wait_ge(S["rec_dst"], 3)

                def step(n, slot, have_prev, half):
                    if have_prev is not None:
                        put(sp, scattered[slot], have_prev)
                    put(sp, S["idx_done"], half)
                    sp.dma_start(ix_slot[slot][:], idx_all[:, bass.ds(LEAD + n * RT, RT)]).then_inc(slot_ready[slot], 16)
                    sp.dma_start(rec_slot[slot][:], rec[:, bass.ds(LEAD + n * RT, RT), :]).then_inc(slot_ready[slot], 16)
                for u in range(4):
                    step(u, u, None, u // 2 + 1)
                with sp.Fori(1, RC // 4) as c:
                    for u in range(4):
                        step(c * 4 + u, u, c * (16 * RT), c * 2 + (u // 2 + 1))
                for u in range(RC % 4):
                    step(RC // 4 * 4 + u, u, RC // 4 * 16 * RT, RC // 2)
                for u in range(4):
                    sp.wait_ge(slot_ready[u], 32 * (RC // 4 + (u < RC % 4)))
                sp.wait_ge(S["deg_read"], STRIPS + 2)

            def pool_1(pool):
                pool.wait_ge(S["filled"], 16)

                def step(slot, times):
                    put(pool, slot_ready[slot], times * 32)
                    for k in range(RT):
                        nc.gpsimd.indirect_dma_start(perm, bass.IndirectOffsetOnAxis(ap=ix_slot[slot][:, k:k + 1], axis=0),
                                                     rec_slot[slot][:, k, :], None, bounds_check=P * SLOTS - 1,
                                                     oob_is_err=False).then_inc(scattered[slot], 16)
                with pool.Fori(0, RC // 4) as c:
                    for u in range(4):
                        step(u, c + 1)
                for u in range(RC % 4):
                    step(u, RC // 4 + 1)
                for u in range(4):
                    pool.wait_ge(scattered[u], 16 * RT * (RC // 4 + (u < RC % 4)))

            def pe_1(pe):
                pe.wait_ge(S["set_done"], 1)
                with pe.Fori(0, RC // 2) as c:
                    for u in range(2):
                        pe.wait_ge(S["hot_ready"], c * 2 + u + 1)
                        nc.tensor.matmul(pr[u][:, 0:490], upper[:], hot[u][:], start=True, stop=False)
                        for dl in range(1, RT + 1):
                            last = nc.tensor.matmul(pr[u][:, dl * B:490], onesb[:], hot[u][:, 0:(RT + 1 - dl) * B], start=False, stop=dl == RT)
                        last.then_inc(S["rank_ready"], 1)
                pe.wait_ge(S["proj_in"], 16)
                pe.wait_ge(S["weights_done"], 1)

                def project(g, par, nb, need):
                    if need is not None:
                        pe.wait_ge(S["proj_p"], need)
                        pe.wait_ge(S["proj_q"], need)
                    bp, bq = ((pk[0], pk[1]), (px[0], px[1]))[par]
                    for w, bank in ((0, bp), (1, bq)):
                        for m in range(nb):
                            last = nc.tensor.matmul(bank[:, m * P:(m + 1) * P], xT[:, bass.ds((g * 4 + m) * P, P)] if not isinstance(g, int) else xT[:, (g * 4 + m) * P:(g * 4 + m + 1) * P],
                                                    w1[:, w, :], start=True, stop=True)
                    last.then_inc(S["proj_ready"], 1)
                project(0, 0, 4, None); project(1, 1, 4, None)
                for g in range(2, 13):
                    project(g, g % 2, 4 if g < 12 else 1, g - 1)

                def degree_begin():
                    nc.tensor.matmul(pd[:, :], onesb[:], zerob[:], start=True, stop=False)

                def degree_step(buf, i, width=STRIP):
                    for m in range(7):
                        last = nc.tensor.matmul(pd[:, 0:width], onesb[:], strip[buf][:, bass.ds(i * 7 + m, 1), HALO:HALO + width], start=False, stop=False)
                    last.then_inc(S["deg_part"], 1)

                def degree_end():
                    nc.tensor.matmul(pd[:, :], onesb[:], zerob[:], start=False, stop=True).then_inc(S["deg_ready"], 1)

                def tiles(n0, first):
                    for u in range(UT):
                        pe.wait_ge(S["lo_ready"], n0 + u + 1)
                        pe.wait_ge(S["key_ready"], n0 + u + 1)
                        if not first or u >= 3:
                            pe.wait_ge(S["added"], n0 + u - 2)
                        nc.tensor.matmul(pk[u % 3][:, 0:SPAN * B], hot_lo[u % NL][:], hot_key[u % NL][:], start=True, stop=True).then_inc(S["pair_ready"], 1)
                pe.wait_ge(S["proj_p"], 13)
                pe.wait_ge(S["proj_q"], 13)
                tiles(0, True)
                with pe.Fori(1, IT) as i:
                    tiles(i * UT, False)
                with pe.Fori(0, (STRIPS - 2) // 2) as jj:
                    for h in range(2):
                        j = jj * 2 + 1 + h
                        pe.wait_ge(S["added"], j * UPT)
                        pe.wait_ge(S["deg_read"], j)
                        degree_begin()
                        with pe.Fori(0, IT) as i:
                            degree_step(h, i)
                            tiles(j * UPT + i * UT, False)
                        degree_end()
                for j, its in ((STRIPS - 1, IT), (STRIPS, 2)):
                    pe.wait_ge(S["added"], j * UPT)
                    pe.wait_ge(S["deg_read"], j)
                    degree_begin()
                    if j == STRIPS - 1:
                        with pe.Fori(0, its) as i:
                            degree_step(1 - j % 2, i)
                            tiles(i * UT + j * UPT, False)
                    else:
                        with pe.Fori(0, its) as i:
                            tiles(i * UT + j * UPT, False)
                        with pe.Fori(0, IT) as i:
                            degree_step(1 - j % 2, i)
                    degree_end()
                pe.wait_ge(S["added"], (STRIPS * IT + 2) * UT)
                pe.wait_ge(S["deg_read"], STRIPS + 1)
                degree_begin()
                with pe.Fori(0, IT) as i:
                    degree_step(0, i, P)
                degree_end()
                pe.wait_ge(S["misfit_ready"], 1)
                nc.tensor.matmul(px[0][:, 0:1], ones_f[:], misfit[:], start=True, stop=True).then_inc(S["misfit_sum"], 1)

            def act_1(act):
                act.dma_start(xT, t["xT"]).then_inc(S["proj_in"], 16)
                act.wait_ge(S["dst_in"], 16)
                nc.scalar.activation(rec[:, :, 0], dst_i[:], ACT.Copy).then_inc(S["rec_dst"], 1)
                act.wait_ge(S["attr_in"], 16)
                nc.scalar.activation(rec[:, LEAD:LEAD + RT * RC, 2:4], attr_stage, ACT.Copy).then_inc(S["rec_dst"], 1)
                act.wait_ge(S["low_bits"], 1)
                nc.scalar.activation(neg_lo[:], low, ACT.Copy, scale=-1.0).then_inc(S["neg_done"], 1)
                nc.scalar.activation(rec[:, :, 1], low, ACT.Copy).then_inc(S["rec_dst"], 1)
                act.wait_ge(S["keys_done"], 1)
                act.wait_ge(S["loaded"], LOADED)
                act.wait_ge(S["neg_done"], 1)
                for g in range(13):
                    act.wait_ge(S["proj_ready"], g + 1)
                    w = (4 if g < 12 else 1) * P
                    nc.scalar.activation(qT[:, g * 512:g * 512 + w], (pk[1], px[1])[g % 2][:, 0:w], ACT.Copy).then_inc(S["proj_q"], 1)
                act.wait_ge(S["proj_q"], 13)
                act.wait_ge(S["proj_p"], 13)
                act.dma_start(q_dram.rearrange("(b p) d -> p b d", p=P), qT.rearrange("p (b d) -> p b d", b=B)).then_inc(S["proj_out1"], 16)
                act.dma_start(p_dram.rearrange("(b p) d -> p b d", p=P), pT.rearrange("p (b d) -> p b d", b=B)).then_inc(S["proj_out2"], 16)

                def tiles(n0, col0, first):
                    def square(u):
                        if not first or u >= NL:
                            act.wait_ge(S["pair_ready"], n0 + u - NL + 1)
                        if not first or u >= 3:
                            act.wait_ge(S["lo_ready"], n0 + u - 2)
                        nc.scalar.activation(sq[u % 3][:], iota_lo[:], ACT.Square, bias=neg_lo[:, bass.ds(col0 + u, 1)] if not isinstance(col0, int) else neg_lo[:, col0 + u:col0 + u + 1]).then_inc(S["act"], 1)
                    square(0)
                    for u in range(UT):
                        if u + 1 < UT:
                            square(u + 1)
                        act.wait_ge(S["act"], n0 + u + 1)
                        nc.scalar.activation(hot_lo[u % NL][:], sq[u % 3][:], ACT.Relu, bias=one_col[:, 0:1], scale=-1.0).then_inc(S["lo_ready"], 1)

                def store(buf, j):
                    act.dma_start(at_dram[bass.ds(j, 1)].rearrange("a p b d -> (a p) b d") if not isinstance(j, int) else at_dram[j],
                                  strip[buf][:, :, HALO:HALO + STRIP]).then_inc(stored[buf], 16)
                def degree_out(j, w=STRIP):
                    put(act, S["deg_read"], j + 2)
                    act.dma_start(deg_dram[0:1, bass.ds(j * STRIP, w)], deg[0][:, 0:w]).then_inc(S["deg_out"], 16)
                tiles(0, 0, True)
                with act.Fori(1, IT) as i:
                    tiles(i * UT, i * UT, False)
                def clear_part(buf, j, i, stores):
                    act.wait_ge(stored[buf], stores)
                    act.wait_ge(S["deg_part"], (j - 1) * 7 + i + 1)
                    piece = strip[buf][:].rearrange("p (g b) d -> p g (b d)", g=7).bitcast(F32)[:, bass.ds(i, 1), :]
                    nc.scalar.activation(piece, zero_col[:, 0:1].unsqueeze(2).to_broadcast([P, 1, B // 7 * (STRIP + 2 * HALO) // 2]), ACT.Copy).then_inc(S["part_clear"], 1)

                def clear_end(buf, j, blocks):
                    act.wait_ge(S["part_clear"], j * 7)
                    for m in range(blocks):
                        last = nc.scalar.activation(strip[buf][:, bass.ds(j * 4 + 4 + m, 1), HALO + P * m:HALO + P * (m + 1)], identb[:].unsqueeze(1), ACT.Copy)
                    last.then_inc(S["cleared"], 1)
                act.wait_ge(S["added"], UPT)
                store(0, 0)
                with act.Fori(0, IT) as i:
                    tiles(UPT + i * UT, P + i * UT, False)
                    clear_part(0, 1, i, 16)
                clear_end(0, 1, 4)
                def strip_pair(jj):
                    for h in range(2):
                        j = jj * 2 + h
                        put(act, S["added"], j * UPT)
                        store(1 - h, j - 1)
                        degree_out(j - 2)
                        with act.Fori(0, IT) as i:
                            tiles(j * UPT + i * UT, j * P + i * UT, False)
                            clear_part(1 - h, j, i, (jj + h) * 16)
                        clear_end(1 - h, j, 1 if isinstance(j, int) and j == STRIPS - 1 else 4)
                with act.Fori(1, STRIPS // 2 - 1) as jj:
                    strip_pair(jj)
                strip_pair(STRIPS // 2 - 1)
                act.wait_ge(S["added"], STRIPS * UPT)
                store(1, STRIPS - 1)
                degree_out(STRIPS - 2)
                with act.Fori(0, 2) as i:
                    tiles(i * UT + STRIPS * UPT, i * UT + STRIPS * P, False)
                act.wait_ge(S["added"], (STRIPS * IT + 2) * UT)
                act.dma_start(at_dram[STRIPS, :, :, 0:P], strip[0][:, :, HALO:HALO + P]).then_inc(stored[0], 16)
                degree_out(STRIPS - 1)
                degree_out(STRIPS, P)
                act.wait_ge(S["deg_out"], 1 + 16 * (STRIPS + 1))
                act.wait_ge(stored[0], 16 * 7)
                act.wait_ge(stored[1], 16 * 6)

            def dve_1(dve):
                c = [0]

                def link(ins):
                    c[0] += 1
                    ins.then_inc(S["dv"], 1)
                    dve.wait_ge(S["dv"], c[0])
                for to, v in ((zerob, 0.0), (onesb, 1.0), (one_col, 1.0), (zero_col, 0.0), (ones_f, 1.0), (hot[0], 0.0), (hot[1], 0.0), (base[0], 0.0)):
                    link(V.memset(to[:], v))
                link(V.memset(blk[:, COLS:], float(B)))
                dve.wait_ge(S["src_in"], 64)
                link(V.tensor_copy(upper[:], hot_lo[0][:].bitcast(F16)))
                link(V.tensor_copy(identb[:], hot_lo[1][:].bitcast(F16)))
                link(V.tensor_scalar(low, src_i[:], 7, None, ALU.arith_shift_right))
                link(V.tensor_copy(blk[:, 0:COLS], low))
                V.tensor_scalar(low, src_i[:], P - 1, None, ALU.bitwise_and).then_inc(S["low_bits"], 1)
                link(V.tensor_scalar(place[:], blk[:, 0:COLS], float(B) - 0.5, float(SKIP), ALU.is_gt, ALU.mult))
                link(V.scalar_tensor_tensor(out=place[:], in0=blk[:, 0:COLS], scalar=float(CAP), in1=place[:], op0=ALU.mult, op1=ALU.add))
                V.memset(dummy[:], 0.0).then_inc(S["set_done"], 1)
                dve.wait_ge(S["set_done"], 1)
                V.memset(dummy[:], 0.0).then_inc(S["deg_read"], 1)
                dve.wait_ge(S["deg_read"], 1)
                V.memset(dummy[:], 0.0).then_inc(S["deg_out"], 1)
                dve.wait_ge(S["deg_out"], 1)
                c0 = c[0]
                STEPS = 13

                def hot_make(u, cols):
                    return V.tensor_tensor(hot[u][:, 0:RT * B].rearrange("p (t k) -> p t k", t=RT),
                                           blk[:, cols].unsqueeze(2).to_broadcast([P, RT, B]), iotak[:].unsqueeze(1).to_broadcast([P, RT, B]), ALU.is_equal)
                for u in range(2):
                    hot_make(u, slice(LEAD + u * RT, LEAD + u * RT + RT)).then_inc(S["hot_ready"], 1)
                with dve.Fori(0, RC // 2) as cc:
                    def after(n):
                        dve.wait_ge(S["dv"], cc * STEPS + (c0 + n))

                    def op(ins):
                        ins.then_inc(S["dv"], 1)

                    def c3(ap):
                        return ap.rearrange("p (t k) -> p t k", t=RT)
                    cols = bass.ds(cc * (2 * RT) + LEAD, 2 * RT)
                    dve.wait_ge(S["rank_ready"], cc * 2 + 1)
                    op(V.tensor_tensor(c3(ranks[0][:]), c3(pr[0][:, 0:RT * B]), base[0][:].unsqueeze(1).to_broadcast([P, RT, B]), ALU.add))
                    op(V.tensor_tensor(base[1][:], base[0][:], pr[0][:, RT * B:490], ALU.add))
                    after(1); op(V.tensor_tensor(own[0][:], ranks[0][:], hot[0][:, 0:RT * B], ALU.mult))
                    dve.wait_ge(S["rank_ready"], cc * 2 + 2)
                    after(2); op(V.tensor_tensor(c3(ranks[1][:]), c3(pr[1][:, 0:RT * B]), base[1][:].unsqueeze(1).to_broadcast([P, RT, B]), ALU.add))
                    op(V.tensor_tensor(base[0][:], base[1][:], pr[1][:, RT * B:490], ALU.add))
                    after(3); op(V.tensor_reduce(out=r_f[:, 0:RT], in_=c3(own[0][:]), op=ALU.add, axis=AX))
                    after(4); op(V.tensor_tensor(own[1][:], ranks[1][:], hot[1][:, 0:RT * B], ALU.mult))
                    hot_make(0, bass.ds(cc * (2 * RT) + (LEAD + 2 * RT), RT)).then_inc(S["hot_ready"], 1)
                    after(7); op(V.tensor_reduce(out=r_f[:, RT:], in_=c3(own[1][:]), op=ALU.add, axis=AX))
                    hot_make(1, bass.ds(cc * (2 * RT) + (LEAD + 3 * RT), RT)).then_inc(S["hot_ready"], 1)
                    after(8); op(V.tensor_scalar(t_f[:], r_f[:], float(CAP * P) - 0.5, float(1 << 30), ALU.is_gt, ALU.mult))
                    after(9); op(V.tensor_tensor(r_i[:], r_f[:], t_f[:], ALU.add))
                    after(10); op(V.tensor_scalar(rhi[:], r_i[:], 7, None, ALU.arith_shift_right))
                    after(11); op(V.scalar_tensor_tensor(out=t_f[:], in0=rhi[:], scalar=float(1 - P * SLOTS), in1=place[:, cols], op0=ALU.mult, op1=ALU.add))
                    after(12); op(V.scalar_tensor_tensor(out=idx_all[:, cols], in0=r_i[:], scalar=float(SLOTS), in1=t_f[:], op0=ALU.mult, op1=ALU.add))
                    after(13); V.memset(dummy[:], 0.0).then_inc(S["idx_done"], 1)
                    dve.wait_ge(S["hot_ready"], cc * 2 + 4)
                    dve.wait_ge(S["idx_done"], cc + 1)
                c[0] = c0 + STEPS * (RC // 2)
                link(V.tensor_reduce(out=misfit2[:], in_=base[0][:], op=ALU.max, axis=AX))
                link(V.tensor_scalar(misfit[:], misfit2[:], float(CAP * P), None, ALU.is_gt))
                link(V.memset(offs[:], 0))
                dve.wait_ge(S["loaded"], LOADED)
                dve.wait_ge(S["rec_dst"], 3)
                dve.wait_ge(S["neg_done"], 1)
                link(V.tensor_scalar(sgn[:], vec[:, 1, :], 0.0, 2.0, ALU.is_ge, ALU.mult))
                link(V.tensor_scalar(sgn[:], sgn[:], -1.0, None, ALU.add))
                link(V.tensor_tensor(w1[:, 0, :], w1[:, 0, :], sgn[:], ALU.mult))
                link(V.tensor_tensor(w1[:, 1, :], w1[:, 1, :], sgn[:], ALU.mult))
                link(V.tensor_tensor(wrep[:], wrep[:], sgn[:], ALU.mult))
                link(V.tensor_tensor(vec[:, 0, :], vec[:, 0, :], sgn[:], ALU.mult))
                V.memset(dummy[:], 0.0).then_inc(S["weights_done"], 1)
                dve.wait_ge(S["weights_done"], 1)
                link(V.tensor_tensor(key[:], rec[:, :, 0], first_i[:], ALU.subtract))
                link(V.tensor_tensor(least, least, rec[:, :, 0], ALU.is_gt))
                link(V.tensor_tensor(above, above, rec[:, :, 0], ALU.is_le))
                link(V.tensor_tensor(least, least, above, ALU.add))
                link(V.scalar_tensor_tensor(out=above, in0=key[:], scalar=0.0, in1=least, op0=ALU.is_lt, op1=ALU.add))
                link(V.scalar_tensor_tensor(out=least, in0=key[:], scalar=float(SPAN - 1), in1=above, op0=ALU.is_gt, op1=ALU.add))
                link(V.scalar_tensor_tensor(out=above, in0=blk[:, 0:COLS], scalar=float(B), in1=least, op0=ALU.is_lt, op1=ALU.mult))
                link(V.tensor_reduce(out=misfit3[:], in_=above, op=ALU.max, axis=AX))
                link(V.tensor_tensor(misfit[:], misfit[:], misfit3[:], ALU.add))
                link(V.scalar_tensor_tensor(out=key[:], in0=blk[:, 0:COLS], scalar=float(SPAN), in1=key[:], op0=ALU.mult, op1=ALU.add))
                for j in range(STRIPS + 1):
                    w = IT if j < STRIPS else 2
                    link(V.tensor_scalar(offs[:, j * IT:j * IT + w, 0:UT], first_i[0:1, j * P:j * P + w * UT].rearrange("a (i u) -> a i u", u=UT),
                                         float(HALO - STRIP * j), 0.0, ALU.add, ALU.max))
                link(V.tensor_scalar(offs[:, :, 0:UT], offs[:, :, 0:UT], float(STRIP + HALO), None, ALU.min))
                V.memset(dummy[:], 0.0).then_inc(S["keys_done"], 1)
                dve.wait_ge(S["keys_done"], 1)
                for g in range(13):
                    nb = 4 if g < 12 else 1
                    dve.wait_ge(S["proj_ready"], g + 1)
                    V.tensor_tensor(pT[:, g * 512:g * 512 + nb * P].rearrange("p (b d) -> p b d", b=nb),
                                    (pk[0], px[0])[g % 2][:, 0:nb * P].rearrange("p (b d) -> p b d", b=nb),
                                    vec[:, 0:1, :].to_broadcast([P, nb, D]), ALU.add).then_inc(S["proj_p"], 1)

                def clear_strip(buf, j, last=False):
                    V.memset(strip[buf][:], 0.0).then_inc(S["strip_clear"], 1)
                    dve.wait_ge(S["strip_clear"], j * 2 + 1)
                    for m in range(1 if last else 4):
                        ins = V.tensor_copy(strip[buf][:, bass.ds(j * 4 + m, 1), HALO + P * m:HALO + P * (m + 1)] if not isinstance(j, int) else
                                            strip[buf][:, j * 4 + m:j * 4 + m + 1, HALO + P * m:HALO + P * (m + 1)], identb[:].unsqueeze(1))
                    ins.then_inc(S["strip_clear"], 1)
                    dve.wait_ge(S["strip_clear"], j * 2 + 2)
                    dve.nop(nofuse=True)

                def keyhot(n0, col0, u, first):
                    if not (first and u < NL):
                        dve.wait_ge(S["pair_ready"], n0 + u - NL + 1)
                    V.tensor_scalar(hot_key[u % NL][:], iota_key[:], key[:, bass.ds(col0 + u, 1)] if not isinstance(col0, int) else key[:, col0 + u:col0 + u + 1], None, ALU.is_equal).then_inc(S["key_ready"], 1)

                def tiles(buf, n0, col0, first, it):
                    row = offs[0:1, bass.ds(it, 1), :] if not isinstance(it, int) else offs[0:1, it:it + 1, :]
                    _, at_col = nc.values_load_multi_w_load_instructions(row.rearrange("a b c -> a (b c)"), engines=[mybir.EngineType.DVE],
                                                                         min_val=0, max_val=STRIP + HALO, skip_runtime_bounds_check_because="clamped above")
                    for u in range(2):
                        keyhot(n0, col0, u, first)
                    for u in range(UT):
                        if u + 2 < UT:
                            keyhot(n0, col0, u + 2, first)
                        dve.wait_ge(S["pair_ready"], n0 + u + 1)
                        if not (first and u == 0):
                            dve.wait_ge(S["added"], n0 + u)
                        w = strip[buf][:, :, bass.ds(at_col[u], SPAN)]
                        V.tensor_tensor(w, w, pk[u % 3][:, 0:SPAN * B].rearrange("p (b s) -> p b s", b=B), ALU.add).then_inc(S["added"], 1)

                def take_degree(j, w=STRIP):
                    dve.wait_ge(S["deg_ready"], j + 1)
                    dve.wait_ge(S["deg_out"], j * 16 + 1)
                    V.tensor_reduce(out=over[:, bass.ds(j, 1)], in_=pd[0:1, 0:w], op=ALU.max, axis=AX)
                    V.tensor_copy(deg[0][:, 0:w], pd[0:1, 0:w]).then_inc(S["deg_read"], 1)
                    dve.wait_ge(S["deg_read"], j + 2)
                dve.wait_ge(S["proj_ready"], 13)
                clear_strip(0, 0)
                tiles(0, 0, 0, True, 0)
                with dve.Fori(1, IT) as i:
                    tiles(0, i * UT, i * UT, False, i)
                dve.wait_ge(S["proj_out1"], 16); dve.wait_ge(S["proj_out2"], 16)
                clear_strip(1, 1)
                with dve.Fori(0, IT) as i:
                    tiles(1, i * UT + UPT, i * UT + P, False, i + IT)
                with dve.Fori(1, STRIPS // 2) as jj:
                    for h in range(2):
                        j = jj * 2 + h
                        take_degree(j - 2)
                        put(dve, S["cleared"], j - 1)
                        with dve.Fori(0, IT) as i:
                            tiles(h, j * UPT + i * UT, j * P + i * UT, False, j * IT + i)
                take_degree(STRIPS - 2)
                put(dve, S["cleared"], STRIPS - 1)
                with dve.Fori(0, 2) as i:
                    tiles(0, i * UT + STRIPS * UPT, i * UT + STRIPS * P, False, i + STRIPS * IT)
                take_degree(STRIPS - 1)
                take_degree(STRIPS, P)
                link(V.tensor_reduce(out=top[0:1, 0:1], in_=over[:], op=ALU.max, axis=AX))
                link(V.scalar_tensor_tensor(out=misfit[0:1, :], in0=top[0:1, 0:1], scalar=255.0, in1=misfit[0:1, :], op0=ALU.is_gt, op1=ALU.add))
                V.memset(dummy[:], 0.0).then_inc(S["misfit_ready"], 1)
                dve.wait_ge(S["misfit_sum"], 1)
                V.tensor_scalar(fits[:], px[0][:, 0:1], 0.5, None, ALU.is_lt).then_inc(S["fits_ready"], 1)
                dve.wait_ge(S["fits_ready"], 1)

            phase_one = (sp_1, pool_1, pe_1, act_1, dve_1)

        two = ExitStack()
        with two:
            sb, ps = mk(two)
            p3 = sb("p3", [P, B, 3, D], BF16)
            s_all = sb("s_all", [P, B, 130])
            p_stage = s_all[:].rearrange("p b d -> p (b d)")[:, 0:ROWS].rearrange("p (b d) -> p b d", b=B)
            recs = sb("recs", [P, SLOTS, 4]); gi_all = sb("gi_all", [P, SLOTS], I32)
            gi = [sb(f"gi{u}", [P, CT], I32) for u in range(2)]
            hotb = sb("hotb", [P, CT, P], BF16)
            parts = sb("parts", [P, 20, 32], BF16)
            res = [sb(f"res{u}", [P, CT, 2]) for u in range(2)]
            turn_sb = [sb(f"turn_sb{u}", [P, 22, P], BF16) for u in range(2)]
            G = [sb(f"G{u}", [P, CT, D]) for u in range(2)]
            H = [sb(f"H{u}", [P, CT, D]) for u in range(2)]
            sqb = [sb(f"sqb{u}", [P, 512]) for u in range(2)]
            zb = [sb(f"zb{u}", [P, CT, 130]) for u in range(2)]
            hotf = [sb(f"hotf{u}", [P, CT, P]) for u in range(2)]
            wsz = sb("wsz", [P, 4, D], BF16)
            wt = [sb(f"wt{u}", [P, D]) for u in range(4)]
            neg_g = sb("neg_g", [P, D]); bt = [sb(f"bt{u}", [P, D]) for u in range(4)]
            zero_f = sb("zero_f", [P, 512])
            tb = [ps(f"tb{u}", [P, 1024], BF16) for u in range(3)]
            ph = [ps(f"ph{u}", [P, 512]) for u in range(2)]
            st = [ps(f"st{u}", [P, 512]) for u in range(2)]
            pS = ps("pS", [P, 512])
            rec_rows = perm.rearrange("(p t) c -> p t c", p=P)
            START = [0, 8, 16]

            def drive(eng, front, back):
                front(0, 0, 0)
                with eng.Fori(0, CHUNKS // 2 - 1) as k:
                    front(k * 2 + 1, 1, k)
                    back(k * 2, 0, k)
                    front(k * 2 + 2, 0, k + 1)
                    back(k * 2 + 1, 1, k)
                front(CHUNKS - 1, 1, CHUNKS // 2 - 1)
                back(CHUNKS - 2, 0, CHUNKS // 2 - 1)
                back(CHUNKS - 1, 1, CHUNKS // 2 - 1)

            def sp_2(sp):
                sp.dma_start(p_stage, p_dram.rearrange("(b p) d -> p b d", p=P)).then_inc(S["p_in"], 16)
                sp.dma_start(recs[:], rec_rows).then_inc(S["recs_in"], 16)
                sp.wait_ge(S["credits"], 1)
                sp.wait_ge(S["copied"], 1)

                def front(q, par, r):
                    if not isinstance(r, int):
                        put(sp, gathered[par], r * (16 * CT))
                    sp.dma_start(gi[par][:], gi_all[:, bass.ds(q * CT, CT)]).then_inc(rec_in[par], 16)

                def back(q, par, r):
                    put(sp, S["h_done"], q * 5 + 15)
                    sp.dma_start(h_dram[bass.ds(q, 1)].rearrange("a p c -> (a p) c"), H[par][:].rearrange("p t d -> p (t d)")).then_inc(h_out[par], 16)
                front(0, 0, 0)
                front(1, 1, 0)
                with sp.Fori(0, CHUNKS // 2 - 1) as k:
                    for par in range(2):
                        front(k * 2 + 2 + par, par, k + 1)
                        back(k * 2 + par, par, k)
                for par in range(2):
                    back(CHUNKS - 2 + par, par, CHUNKS // 2 - 1)
                for u in range(2):
                    sp.wait_ge(h_out[u], 16 * (CHUNKS // 2) + 1)
                with sp.Fori(0, CHUNKS // 2) as k:
                    for par in range(2):
                        q = k * 2 + par
                        put(sp, S["z_done"], q + 1)
                        sp.dma_start(G[par][:].rearrange("p t d -> p (t d)"), h_dram[bass.ds(q, 1)].rearrange("a p c -> (a p) c")).then_inc(h_in[par], 16)
                sp.wait_ge(S["sum_taken"], B + 1)
                sp.dma_start(s_dram, s_all[:, :, 0:D + 1]).then_inc(S["s_out"], 16)
                sp.wait_ge(S["s_out"], 16)

            def pool_2(pool):
                pool.wait_ge(S["credits"], 1)

                def front(q, par, r):
                    put(pool, rec_in[par], r * 16 + 16)
                    for k in range(CT):
                        if k % 4 == 0:
                            put(pool, S["h_done"], q * 5 + (k // 4 + 1))
                        nc.gpsimd.indirect_dma_start(G[par][:, k, :], None, q_dram,
                                                     bass.IndirectOffsetOnAxis(ap=gi[par][:, k:k + 1], axis=0)).then_inc(gathered[par], 16)
                drive(pool, front, lambda *a: None)
                for u in range(2):
                    pool.wait_ge(gathered[u], 16 * CT * (CHUNKS // 2))

            def pe_2(pe):
                pe.wait_ge(S["p3_done"], 1)
                for u in range(2):
                    nc.tensor.matmul(st[u][:, :], ones_f[:], zero_f[:], start=True, stop=False)

                def front(q, par, r):
                    pe.wait_ge(S["hot2"], q + 1)
                    pe.wait_ge(S["as_done"], q + 3)
                    for g in range(3):
                        pe.wait_ge(S["oht_ready"], q * 3 + g + 1)
                        for k in range(TURNS[g]):
                            n = START[g] + k
                            of = hotb[:, n, :] if n < CT else parts[:, (n - CT) * 4:(n - CT) * 4 + 4, :].rearrange("p a b -> p (a b)")
                            last = nc.tensor.transpose(tb[g][:, k * P:(k + 1) * P], of, identb[:])
                        last.then_inc(S["turned"], 1)

                def back(q, par, r):
                    pe.wait_ge(S["oht_ready"], q * 3 + 6)
                    b = r

                    def sums(g):
                        w = GROUPS[g] * P
                        pe.wait_ge(S["squared"], q * 5 + g + 11)
                        nc.tensor.matmul(st[0][:, 0:w], ones_f[:], H[par][:, 4 * g:4 * g + GROUPS[g], :].rearrange("p a b -> p (a b)"), start=False, stop=False)
                        nc.tensor.matmul(st[1][:, 0:w], ones_f[:], sqb[(par + g) % 2][:, 0:w], start=False, stop=False).then_inc(S["stat_done"], 1)
                    for g in range(5):
                        pe.wait_ge(S["h_done"], q * 5 + g + 9)
                        bank = ph[(par + g) % 2]
                        for k in range(GROUPS[g]):
                            n = 4 * g + k
                            to = bank[:, k * P:(k + 1) * P]
                            nc.tensor.matmul(to, turn_sb[par][:, CT + g, :], wsz[:, k, :], start=True, stop=False)
                            for m in range(3):
                                last = nc.tensor.matmul(to, turn_sb[par][:, n, :], p3[:, bass.ds(b, 1), m, :].rearrange("p a d -> p (a d)"), start=False, stop=m == 2)
                        last.then_inc(S["mm_done"], 1)
                        if g:
                            sums(g - 1)
                    sums(4)
                drive(pe, front, back)
                for u in range(2):
                    last = nc.tensor.matmul(st[u][:, :], ones_f[:], zero_f[:], start=False, stop=True)
                last.then_inc(S["stats_ready"], 1)
                with pe.Fori(0, B) as k:
                    pe.wait_ge(S["sum_taken"], k + 1)
                    for par in range(2):
                        pe.wait_ge(S["z_done"], k * 2 + par + 3)
                        for n in range(CT):
                            last = nc.tensor.matmul(pS[:, 0:D + 1], hotf[par][:, n, :], zb[par][:, n, 0:D + 1],
                                                    start=par == 0 and n == 0, stop=par == 1 and n == CT - 1)
                        last.then_inc(S["z_used"], 1)

            def act_2(act):
                act.wait_ge(S["recs_in"], 16)
                nc.scalar.activation(gi_all[:], recs[:, :, 0], ACT.Copy).then_inc(S["copied"], 1)
                act.wait_ge(S["credits"], 1)

                def front(q, par, r):
                    act.wait_ge(S["mm_done"], q * 5 + 5)
                    for g in range(3):
                        act.wait_ge(S["turned"], q * 3 + g + 4)
                        w = TURNS[g] * P
                        nc.scalar.activation(turn_sb[par][:, START[g]:START[g] + TURNS[g], :].rearrange("p a b -> p (a b)"), tb[g][:, 0:w], ACT.Copy).then_inc(S["oht_ready"], 1)

                def back(q, par, r):
                    for g in range(5):
                        w = GROUPS[g] * P
                        act.wait_ge(S["h_done"], q * 5 + g + 11)
                        act.wait_ge(S["stat_done"], q * 5 + g + 9)
                        nc.scalar.activation(sqb[(par + g) % 2][:, 0:w], H[par][:, 4 * g:4 * g + GROUPS[g], :].rearrange("p a b -> p (a b)"), ACT.Square).then_inc(S["squared"], 1)
                drive(act, front, back)
                act.wait_ge(S["bn_sqrt"], 1)
                nc.scalar.activation(bt[1][:], bt[0][:], ACT.Sqrt).then_inc(S["bn_rooted"], 1)
                with act.Fori(0, B) as k:
                    act.wait_ge(S["z_used"], k * 2 + 4)
                    nc.scalar.activation(s_all[:, bass.ds(k, 1), 0:D + 1].rearrange("p a d -> p (a d)"), pS[:, 0:D + 1], ACT.Copy).then_inc(S["sum_taken"], 1)

            def dve_2(dve):
                c = [0]

                def link(ins):
                    c[0] += 1
                    ins.then_inc(S["dv2"], 1)
                    dve.wait_ge(S["dv2"], c[0])
                for n, k in (("as_done", 2), ("h_done", 10), ("turned", 3), ("oht_ready", 3), ("mm_done", 10), ("stat_done", 10),
                             ("squared", 10), ("z_done", 2), ("z_used", 2), ("sum_taken", 1), ("hout0", 1), ("hout1", 1)):
                    handle = {"hout0": h_out[0], "hout1": h_out[1]}.get(n) or S[n]
                    for _ in range(k):
                        V.memset(dummy2[:], 0.0).then_inc(handle, 1)
                        dve.wait_ge(handle, _ + 1)
                link(V.memset(parts[:], 0.0)); link(V.memset(zero_f[:], 0.0))
                for u in range(2):
                    link(V.memset(zb[u][:], 1.0))
                link(V.memset(dummy2[:], 0.0))
                V.memset(dummy2[:], 0.0).then_inc(S["credits"], 1)
                dve.wait_ge(S["credits"], 1)

                def split3(outs, of, r0, r1):
                    link(V.tensor_copy(outs[0], of))
                    link(V.tensor_tensor(r0, of, outs[0], ALU.subtract))
                    link(V.tensor_copy(outs[1], r0))
                    link(V.tensor_tensor(r1, r0, outs[1], ALU.subtract))
                    link(V.tensor_copy(outs[2], r1))
                wb = [hotb[:, u, :] for u in range(3)]
                split3(wb, wrep[:], wt[0][:], wt[1][:])
                link(V.tensor_scalar(wt[2][:], wb[0], masks[:, 0:1], None, ALU.mult))
                link(V.scalar_tensor_tensor(out=wt[3][:], in0=wb[1], scalar=masks[:, 1:2], in1=wt[2][:], op0=ALU.mult, op1=ALU.add))
                link(V.scalar_tensor_tensor(out=wt[2][:], in0=wb[2], scalar=masks[:, 2:3], in1=wt[3][:], op0=ALU.mult, op1=ALU.add))
                for k in range(4):
                    link(V.tensor_scalar(wsz[:, k, :], wt[2][:], masks[:, 3 + k:4 + k], None, ALU.mult))
                dve.wait_ge(S["recs_in"], 16)
                dve.wait_ge(S["p_in"], 16)
                for b7 in range(0, B, 7):
                    blocks = slice(b7, b7 + 7)
                    split3([p3[:, blocks, m, :] for m in range(3)], p_stage[:, blocks, :], H[0][:, 0:7, :], H[1][:, 0:7, :])
                V.memset(dummy2[:], 0.0).then_inc(S["p3_done"], 1)
                dve.wait_ge(S["p3_done"], 1)
                c0 = c[0]

                def front(q, par, r):
                    k = [0]

                    def lk(ins, wait=True):
                        k[0] += 1
                        ins.then_inc(S["dv2"], 1)
                        if wait:
                            dve.wait_ge(S["dv2"], q * 4 + (c0 + k[0]))
                    dve.wait_ge(S["turned"], q * 3 + 3)
                    a = recs[:, bass.ds(q * CT, CT), 2:4]
                    a3 = lambda ap: ap.unsqueeze(2).to_broadcast([P, CT, 3, 2])
                    p4 = lambda i: parts[:, 0:CT, 6 * i:6 * i + 6].rearrange("p t (j c) -> p t j c", j=3)
                    lk(V.tensor_copy(p4(0), a3(a)), False)
                    V.tensor_tensor(hotb[:], iota_lo[:].unsqueeze(1).to_broadcast([P, CT, P]), recs[:, bass.ds(q * CT, CT), 1:2].to_broadcast([P, CT, P]), ALU.is_equal).then_inc(S["hot2"], 1)
                    dve.wait_ge(S["dv2"], q * 4 + (c0 + 1))
                    lk(V.tensor_tensor(res[0][:], a, parts[:, 0:CT, 0:2], ALU.subtract))
                    lk(V.tensor_copy(p4(1), a3(res[0][:])))
                    lk(V.tensor_tensor(res[1][:], res[0][:], parts[:, 0:CT, 6:8], ALU.subtract))
                    V.tensor_copy(p4(2), a3(res[1][:])).then_inc(S["as_done"], 1)

                def back(q, par, r):
                    dve.wait_ge(gathered[par], r * (16 * CT) + 16 * CT)
                    dve.wait_ge(h_out[par], r * 16 + 1)
                    dve.wait_ge(S["stat_done"], q * 5 + 5)
                    for g in range(5):
                        w = GROUPS[g] * P
                        dve.wait_ge(S["mm_done"], q * 5 + g + 11)
                        sl = lambda T: T[par][:, 4 * g:4 * g + GROUPS[g], :].rearrange("p a b -> p (a b)")
                        V.tensor_tensor(sl(H), ph[(par + g) % 2][:, 0:w], sl(G), ALU.add).then_inc(S["h_done"], 1)
                drive(dve, front, back)
                c[0] = c0 + 4 * CHUNKS
                dve.wait_ge(S["stats_ready"], 1)
                mean, e2, t2 = bt[2], bt[3], neg_g
                for u, to in ((0, mean), (1, e2)):
                    link(V.tensor_copy(to[:], st[u][:, 0:P]))
                    for k in range(1, 4):
                        link(V.tensor_tensor(to[:], to[:], st[u][:, k * P:(k + 1) * P], ALU.add))
                    link(V.tensor_scalar(to[:], to[:], 1.0 / EDGES, None, ALU.mult))
                link(V.tensor_tensor(t2[:], mean[:], mean[:], ALU.mult))
                link(V.tensor_tensor(e2[:], e2[:], t2[:], ALU.subtract))
                link(V.tensor_scalar(bt[0][:], e2[:], 0.0, BN_EPS, ALU.max, ALU.add))
                V.memset(dummy2[:], 0.0).then_inc(S["bn_sqrt"], 1)
                dve.wait_ge(S["bn_rooted"], 1)
                newton(link, alpha[:], bt[0][:], bt[1][:])
                link(V.tensor_tensor(bt[1][:], vec[:, 1, :], sgn[:], ALU.mult))
                link(V.tensor_scalar(bt[1][:], bt[1][:], 1e-20, None, ALU.max))
                link(V.tensor_tensor(alpha[:], alpha[:], bt[1][:], ALU.mult))
                link(V.reciprocal(bt[1][:], alpha[:]))
                link(V.tensor_tensor(bt[1][:], bt[1][:], vec[:, 2, :], ALU.mult))
                link(V.tensor_tensor(neg_g[:], mean[:], bt[1][:], ALU.subtract))
                link(V.tensor_tensor(bt[1][:], mean[:], alpha[:], ALU.mult))
                link(V.tensor_tensor(shift[:], vec[:, 2, :], bt[1][:], ALU.subtract))
                with dve.Fori(0, CHUNKS // 2) as k:
                    for par in range(2):
                        q = k * 2 + par
                        dve.wait_ge(h_in[par], k * 16 + 16)
                        dve.wait_ge(S["z_used"], q + 1)
                        V.tensor_tensor(zb[par][:, :, 0:D], G[par][:], neg_g[:].unsqueeze(1).to_broadcast([P, CT, D]), ALU.max)
                        V.tensor_tensor(hotf[par][:], iota_lo[:].unsqueeze(1).to_broadcast([P, CT, P]),
                                        recs[:, bass.ds(q * CT, CT), 1:2].to_broadcast([P, CT, P]), ALU.is_equal).then_inc(S["z_done"], 1)
            phase_two = (sp_2, pool_2, pe_2, act_2, dve_2)

        three = ExitStack()
        with three:
            sb, ps = mk(three)
            x1 = sb("x1", [P, B, D])
            dinv_row = sb("dinv_row", [P, ROWS]); dinv_col = sb("dinv_col", [P, B]); dc = [sb(f"dc{u}", [P, B]) for u in range(2)]
            g3 = [sb(f"g3_{u}", [P, B, 3, D], BF16) for u in range(2)]
            ring_raw = sb("ring_raw", [P, 25600], BF16)
            ring = [ring_raw[:, u * 3584:(u + 1) * 3584].rearrange("p (b d) -> p b d", b=7) for u in range(7)]
            flat = ring_raw[:].bitcast(F32)
            s_in = flat[:, 0:B * 130].rearrange("p (b d) -> p b d", b=B)
            x_in = flat[:, B * 130:B * 130 + ROWS].rearrange("p (b d) -> p b d", b=B)
            sc = [g3[u][:].rearrange("p b m d -> p (b m d)").bitcast(F32)[:, 0:ROWS] for u in range(2)]
            w2 = sb("w2", [P, D]); cw = sb("cw", [P, 3, D]); cb = sb("cb", [P, 3]); ident_f = sb("ident_f", [P, P])
            vrow = sb("vrow", [P, D]); shT = sb("shT", [P, D])
            ta, tcn, tsq = (sb(n, [P, 4, D]) for n in ("ta", "tcn", "tsq"))
            tT = sb("tT", [P, 512]); yt = sb("yt", [P, 512]); hT = sb("hT", [P, 512])
            sm = [sb(f"sm{u}", [P, 4]) for u in range(6)]
            pa = ps("pa", [P, 512]); pb = ps("pb", [P, 512]); pg = ps("pg", [P, 512])
            py = [ps(f"py{u}", [P, 512]) for u in range(2)]
            dummy3 = sb("dummy3", [P, 1])
            NG = 13
            widths = [(j, 4) for j in range(12)] + [(12, 1)]
            loads3 = [(w2[:], t["w2"]), (ident_f[:], t["ident_f"]), (dinv_row[:], deg_dram.to_broadcast([P, ROWS])),
                      (dc[0][:], deg_dram.rearrange("a (b p) -> p (a b)", p=P)), (s_in[:, :, 0:D + 1], s_dram),
                      (x_in, t["x"].rearrange("(b p) d -> p b d", p=P)), (cb[:], t["cbT"])]
            loads3 += [(cw[:, c, :], t[f"cw{c}"]) for c in range(3)]

            def fl(ap):
                return ap.rearrange("p a b -> p (a b)")

            def sp_3(sp):
                for to, of in loads3:
                    sp.dma_start(to, of, allow_slow_non_contiguous=True).then_inc(S["x_in"], 16)
                sp.wait_ge(S["node_done"], NG)
                sp.wait_ge(S["credits3"], 1)

                def strip_loads(c, j, w):
                    for i in range(7):
                        put(sp, S["chunk_used"], (j + 13 * c) * 7 + i + 1)
                        sp.dma_start(ring[i][:, :, 0:w], at_dram[bass.ds(j, 1), :, 7 * i:7 * i + 7, 0:w].rearrange("a p b d -> (a p) b d")).then_inc(a_in[i], 16)
                for c in range(3):
                    with sp.Fori(0, 12) as j:
                        strip_loads(c, j, STRIP)
                    strip_loads(c, 12, P)

            def pool_3(pool):
                pool.wait_ge(S["node_done"], NG)

            def pe_3(pe):
                pe.wait_ge(S["x_in"], 16 * len(loads3))
                pe.wait_ge(S["v_a"], 1)
                nc.tensor.transpose(pa[:, 0:P], shift[:], ident_f[:]).then_inc(S["v_b"], 1)
                pe.wait_ge(S["v_a"], 2)
                nc.tensor.matmul(pb[:, 0:P], shT[:], w2[:], start=True, stop=True).then_inc(S["v_b"], 1)
                def group(j, nb):
                    def four(of_fn, rhs, to, transpose):
                        for m in range(nb):
                            sl = slice(m * P, (m + 1) * P)
                            if transpose:
                                last = nc.tensor.transpose(to[:, sl], of_fn(m), ident_f[:])
                            else:
                                last = nc.tensor.matmul(to[:, sl], of_fn(m), rhs, start=True, stop=True)
                        last.then_inc(S["pe_n"], 1)
                    pe.wait_ge(S["nd"], j * 3 + 1)
                    four(lambda m: ta[:, m, :], None, pa, True)
                    pe.wait_ge(S["act_n"], j * 2 + 1)
                    four(lambda m: tT[:, m * P:(m + 1) * P], w2[:], pb, False)
                    pe.wait_ge(S["nd"], j * 3 + 2)
                    four(lambda m: ta[:, m, :], None, pa, True)
                    pe.wait_ge(S["act_n"], j * 2 + 2)
                    four(lambda m: tT[:, m * P:(m + 1) * P], cw[:, 0, :], pg, False)
                with pe.Fori(0, 12) as j:
                    group(j, 4)
                group(12, 1)
                pe.wait_ge(S["credits3"], 1)

                def tail(c, n, nb):
                    pe.wait_ge(S["bias_done"], n + 1)
                    pe.wait_ge(S["g_taken"], n + 1)
                    for m in range(nb):
                        sl = slice(m * P, (m + 1) * P)
                        if c < 2:
                            last = nc.tensor.matmul(pg[:, sl], hT[:, sl], cw[:, c + 1, :], start=True, stop=True)
                        else:
                            last = nc.tensor.transpose(pg[:, sl], hT[:, sl], ident_f[:])
                    last.then_inc(S["tail_done"], 1)

                def strip(c, j, par, w, has_tail):
                    n = j + 13 * c
                    pe.wait_ge(S["y_taken"], n + 1)
                    for i in range(7):
                        pe.wait_ge(a_in[i], (n + 1) * 16)
                        for m in range(7):
                            for k in range(3):
                                last = nc.tensor.matmul(py[par][:, 0:w], g3[c % 2][:, 7 * i + m, k, :], ring[i][:, m, 0:w],
                                                        start=i == m == k == 0, stop=i == m == 6 and k == 2)
                        last.then_inc(S["chunk_used"], 1)
                        if i == 1 and has_tail:
                            tail(c, n - 1, 4)
                for c in range(3):
                    pe.wait_ge(S["g_taken"], 13 * c + 1)
                    strip(c, 0, c % 2, STRIP, False)
                    with pe.Fori(0, 5) as k:
                        for h in range(2):
                            strip(c, k * 2 + (1 + h), (c + 1 + h) % 2, STRIP, True)
                    strip(c, 11, (c + 11) % 2, STRIP, True)
                    strip(c, 12, (c + 12) % 2, P, True)
                    tail(c, 13 * c + 12, 1)

            def act_3(act):
                act.wait_ge(S["root_a"], 1)
                nc.scalar.activation(sc[0], dinv_row[:], ACT.Sqrt)
                nc.scalar.activation(dc[1][:], dc[0][:], ACT.Sqrt).then_inc(S["root_b"], 1)
                act.wait_ge(S["v_b"], 1)
                nc.scalar.activation(shT[:], pa[:, 0:P], ACT.Copy).then_inc(S["v_a"], 1)

                def group(j, nb):
                    w = nb * P
                    act.wait_ge(S["pe_n"], j * 4 + 1)
                    nc.scalar.activation(tT[:, 0:w], pa[:, 0:w], ACT.Copy).then_inc(S["act_n"], 1)
                    act.wait_ge(S["ln_ask"], j + 1)
                    nc.scalar.activation(sm[3][:], sm[2][:], ACT.Sqrt).then_inc(S["ln_root"], 1)
                    act.wait_ge(S["pe_n"], j * 4 + 3)
                    nc.scalar.activation(tT[:, 0:w], pa[:, 0:w], ACT.Copy).then_inc(S["act_n"], 1)
                with act.Fori(0, 12) as j:
                    group(j, 4)
                group(12, 1)

                def post(c, j, nb):
                    n = j + 13 * c
                    w = nb * P
                    act.wait_ge(S["yt_ready"], n + 1)
                    nc.scalar.activation(hT[:, 0:w], yt[:, 0:w], ACT.Relu if c < 2 else ACT.Identity, bias=cb[:, c:c + 1]).then_inc(S["bias_done"], 1)
                    if c == 2:
                        act.wait_ge(S["ln_ask"], j + 14)
                        nc.scalar.activation(sm[3][:], sm[2][:], ACT.Sqrt).then_inc(S["ln_root"], 1)
                        put(act, S["out_ready"], j + 1)
                        act.dma_start(out[bass.ds(j * 512, w), :].rearrange("(b p) d -> p b d", p=P), ta[:, 0:nb, :]).then_inc(S["out_sent"], 16)
                for c in range(3):
                    with act.Fori(0, 12) as j:
                        post(c, j, 4)
                    post(c, 12, 1)
                act.wait_ge(S["out_sent"], 16 * 13 + 1)

            def dve_3(dve):
                c3 = [0]

                def link(ins):
                    c3[0] += 1
                    ins.then_inc(S["dv3"], 1)
                    dve.wait_ge(S["dv3"], c3[0])
                dve.wait_ge(S["x_in"], 16 * len(loads3))
                for n, k in (("chunk_used", 7), ("y_taken", 2), ("g_taken", 0), ("out_sent", 1)):
                    for _ in range(k):
                        V.memset(dummy3[:], 0.0).then_inc(S[n], 1)
                        dve.wait_ge(S[n], _ + 1)
                V.memset(dummy3[:], 0.0).then_inc(S["root_a"], 1)
                dve.wait_ge(S["root_a"], 1)
                V.memset(dummy3[:], 0.0).then_inc(S["v_a"], 1)
                dve.wait_ge(S["v_a"], 1)
                dve.wait_ge(S["root_b"], 1)
                newton(link, sc[1], dinv_row[:], sc[0])
                link(V.tensor_copy(dinv_row[:], sc[1]))
                newton(link, dinv_col[:], dc[0][:], dc[1][:])
                dve.wait_ge(S["v_b"], 2)
                link(V.tensor_tensor(vrow[:], pb[:, 0:P], vec[:, 3, :], ALU.add))
                base0 = c3[0]

                def bc(ap, nb):
                    return ap[:, 0:nb].unsqueeze(2).to_broadcast([P, nb, D])

                def norm(lk, nb, ask_at):
                    A, C, Q = ta[:, 0:nb, :], tcn[:, 0:nb, :], tsq[:, 0:nb, :]
                    lk(V.tensor_reduce(out=sm[0][:, 0:nb], in_=A, op=ALU.add, axis=AX))
                    lk(V.tensor_scalar(sm[0][:, 0:nb], sm[0][:, 0:nb], 1.0 / D, None, ALU.mult))
                    lk(V.tensor_tensor(C, A, bc(sm[0], nb), ALU.subtract))
                    lk(V.tensor_tensor(Q, C, C, ALU.mult))
                    lk(V.tensor_reduce(out=sm[1][:, 0:nb], in_=Q, op=ALU.add, axis=AX))
                    V.tensor_scalar(sm[2][:, 0:nb], sm[1][:, 0:nb], 1.0 / D, LN_EPS, ALU.mult, ALU.add).then_inc(S["ln_ask"], 1)
                    dve.wait_ge(S["ln_root"], ask_at)
                    newton(lk, sm[4][:, 0:nb], sm[2][:, 0:nb], sm[3][:, 0:nb])
                NORM = 10

                def scale_split(lk, to, j, nb):
                    G0, R0, R1 = ta[:, 0:nb, :], tcn[:, 0:nb, :], tsq[:, 0:nb, :]
                    dst = lambda m: to[:, bass.ds(j * 4, nb), m, :]
                    lk(V.tensor_tensor(G0, pg[:, 0:nb * P].rearrange("p (a b) -> p a b", a=nb), dinv_col[:, bass.ds(j * 4, nb)].unsqueeze(2).to_broadcast([P, nb, D]), ALU.mult))
                    lk(V.tensor_copy(dst(0), G0))
                    lk(V.tensor_tensor(R0, G0, dst(0), ALU.subtract))
                    lk(V.tensor_copy(dst(1), R0))
                    lk(V.tensor_tensor(R1, R0, dst(1), ALU.subtract))
                    lk(V.tensor_copy(dst(2), R1))
                SPLIT = 6
                K = 8 + NORM + SPLIT

                def group(j, nb):
                    k = [0]

                    def lk(ins):
                        k[0] += 1
                        ins.then_inc(S["dv3"], 1)
                        dve.wait_ge(S["dv3"], j * K + (base0 + k[0]))
                    A = ta[:, 0:nb, :]
                    blocks = bass.ds(j * 4, nb)
                    cnt = s_in[:, blocks, D:D + 1]
                    V.tensor_tensor(A, s_in[:, blocks, 0:D], alpha[:].unsqueeze(1).to_broadcast([P, nb, D]), ALU.mult).then_inc(S["nd"], 1)
                    lk(V.tensor_tensor(tcn[:, 0:nb, :], cnt.to_broadcast([P, nb, D]), vrow[:].unsqueeze(1).to_broadcast([P, nb, D]), ALU.mult))
                    lk(V.tensor_scalar(sm[5][:, 0:nb], cnt.rearrange("p a b -> p (a b)"), 1.0, None, ALU.add))
                    lk(V.reciprocal(sm[4][:, 0:nb], sm[5][:, 0:nb]))
                    dve.wait_ge(S["pe_n"], j * 4 + 2)
                    lk(V.tensor_tensor(tsq[:, 0:nb, :], tcn[:, 0:nb, :], pb[:, 0:nb * P].rearrange("p (a b) -> p a b", a=nb), ALU.add))
                    lk(V.tensor_tensor(tcn[:, 0:nb, :], tsq[:, 0:nb, :], bc(sm[4], nb), ALU.mult))
                    lk(V.scalar_tensor_tensor(out=A, in0=x_in[:, blocks, :], scalar=2.0, in1=tcn[:, 0:nb, :], op0=ALU.mult, op1=ALU.add))
                    norm(lk, nb, j + 1)
                    V.tensor_tensor(A, tcn[:, 0:nb, :], bc(sm[4], nb), ALU.mult).then_inc(S["nd"], 1)
                    dve.wait_ge(S["nd"], j * 3 + 2)
                    lk(V.tensor_copy(x1[:, blocks, :], A))
                    dve.wait_ge(S["pe_n"], j * 4 + 4)
                    scale_split(lk, g3[0], j, nb)
                    lk(V.memset(dummy3[:], 0.0))
                    V.memset(dummy3[:], 0.0).then_inc(S["nd"], 1)
                    dve.wait_ge(S["nd"], j * 3 + 3)
                    assert k[0] == K, k
                with dve.Fori(0, 12) as j:
                    group(j, 4)
                group(12, 1)
                for _ in range(NG):
                    V.memset(dummy3[:], 0.0).then_inc(S["node_done"], 1)
                    dve.wait_ge(S["node_done"], _ + 1)
                V.memset(dummy3[:], 0.0).then_inc(S["g_taken"], 1)
                dve.wait_ge(S["g_taken"], 1)
                V.memset(dummy3[:], 0.0).then_inc(S["credits3"], 1)
                dve.wait_ge(S["credits3"], 1)
                base1 = base0 + 13 * K

                def post(c, j, par, nb):
                    n = j + 13 * c
                    w = nb * P
                    k = [0]
                    per = SPLIT if c < 2 else NORM + 1
                    start = base1 + (c * 13 * SPLIT)

                    def lk(ins):
                        k[0] += 1
                        ins.then_inc(S["dv3"], 1)
                        dve.wait_ge(S["dv3"], j * per + (start + k[0]))
                    dve.wait_ge(S["chunk_used"], n * 7 + 14)
                    V.tensor_tensor(yt[:, 0:w], py[par][:, 0:w], dinv_row[:, bass.ds(j * 512, w)], ALU.mult).then_inc(S["yt_ready"], 1)
                    dve.wait_ge(S["yt_ready"], n + 1)
                    V.memset(dummy3[:], 0.0).then_inc(S["y_taken"], 1)
                    dve.wait_ge(S["tail_done"], n + 1)
                    if c < 2:
                        scale_split(lk, g3[(c + 1) % 2], j, nb)
                    else:
                        dve.wait_ge(S["out_sent"], j * 16 + 1)
                        lk(V.tensor_tensor(ta[:, 0:nb, :], x1[:, bass.ds(j * 4, nb), :], pg[:, 0:w].rearrange("p (a b) -> p a b", a=nb), ALU.add))
                        norm(lk, nb, j + 14)
                        V.tensor_tensor(ta[:, 0:nb, :], tcn[:, 0:nb, :], bc(sm[4], nb), ALU.mult).then_inc(S["out_ready"], 1)
                        dve.wait_ge(S["out_ready"], j + 1)
                    V.memset(dummy3[:], 0.0).then_inc(S["g_taken"], 1)
                    dve.wait_ge(S["g_taken"], n + 2)
                    assert k[0] == per, (k, per)
                for c in range(3):
                    post(c, 0, c % 2, 4)
                    with dve.Fori(0, 5) as k:
                        for h in range(2):
                            post(c, k * 2 + (1 + h), (c + 1 + h) % 2, 4)
                    post(c, 11, (c + 11) % 2, 4)
                    post(c, 12, (c + 12) % 2, 1)
            phase_three = (sp_3, pool_3, pe_3, act_3, dve_3)

        block = outer.enter_context(nc.Block())

        def run(eng, n, engine):
            phase_one[n](eng)
            barrier(eng, S["phase1"])
            eng.wait_ge(S["fits_ready"], 1)
            eng.nop(nofuse=True)
            fit = nc.values_load(fits[0:1, 0:1], engines=[engine], min_val=0, max_val=1, skip_runtime_bounds_check_because="a comparison's result")
            with eng.If(fit == 1):
                phase_two[n](eng)
                barrier(eng, S["phase2"])
                phase_three[n](eng)
            with eng.Else():
                general[n](eng)

        @block.sync
        def _(sp):
            run(sp, 0, mybir.EngineType.SP)

        @block.gpsimd
        def _(pool):
            run(pool, 1, mybir.EngineType.Pool)

        @block.tensor
        def _(pe):
            run(pe, 2, mybir.EngineType.PE)

        @block.scalar
        def _(act):
            run(act, 3, mybir.EngineType.Activation)

        @block.vector
        def _(dve):
            run(dve, 4, mybir.EngineType.DVE)


def host_arrays(x, src, dst, edge_attr_2, L0_gnn_W1, L0_gnn_b1, L0_gnn_gamma, L0_gnn_beta, L0_gnn_W2, L0_gnn_b2,
                L1_gnn_W0, L1_gnn_b0, L1_gnn_W1, L1_gnn_b1, L1_gnn_W2, L1_gnn_b2):
    import numpy as np

    def cols(a, pad, lead):
        a = np.asarray(a)
        o = np.full((COLS * P,) + a.shape[1:], pad, a.dtype)
        o[:LEAD * P] = lead
        o[LEAD * P:LEAD * P + EDGES] = a
        return np.ascontiguousarray(np.moveaxis(o.reshape((COLS, P) + a.shape[1:]), 0, 1))

    def row(a):
        return np.asarray(a).reshape(1, -1)
    xr = np.zeros((ROWS, D), np.float32)
    xr[:NODES] = np.asarray(x)
    dst_t = cols(dst, NODES - 1, 0)
    p = np.arange(P)
    wrep = np.asarray(L0_gnn_W1)[2 * D + p % 2]
    masks = np.zeros((P, 8), np.float32)
    for j in range(3):
        masks[:, j] = (p % 32 < 18) & ((p % 32) // 2 % 3 == j)
    for k in range(4):
        masks[:, 3 + k] = p // 32 == k
    c = np.arange(COLS)
    above = (STRIP * (c // P + 1)).astype(np.float32)[None]
    least = (STRIP * np.maximum(-(-(c - (IT * UT - 1)) // P), 0)).astype(np.float32)[None]
    return dict(
        src_t=cols(src, B * P, B * P), dst_t=dst_t, d0_row=np.ascontiguousarray(dst_t[0:1]),
        attr_t=np.ascontiguousarray(cols(edge_attr_2, 0, 0)[:, LEAD:LEAD + RT * RC]),
        iotak=np.tile(np.arange(B, dtype=np.float32), (P, 1)), iota_lo=np.tile(np.arange(P, dtype=np.float32), (P, 1)).astype(np.float16),
        iota_key=np.tile(np.arange(SPAN * B, dtype=np.float32), (P, 1)).astype(np.float16),
        upper=np.triu(np.ones((P, P), np.float32), 1).astype(np.float16), ident_h=np.eye(P, dtype=np.float16),
        ident_f=np.eye(P, dtype=np.float32), empty=np.tile(np.array([ROWS - 1, -1, 0, 0], np.float32), (P, SLOTS)),
        x=xr, xT=np.ascontiguousarray(xr.T), w1=np.asarray(L0_gnn_W1), wrep=wrep, masks=masks,
        b1=row(L0_gnn_b1), gamma=row(L0_gnn_gamma), beta=row(L0_gnn_beta), b2=row(L0_gnn_b2), w2=np.asarray(L0_gnn_W2),
        cw0=np.asarray(L1_gnn_W0), cw1=np.asarray(L1_gnn_W1), cw2=np.asarray(L1_gnn_W2),
        cb0=row(L1_gnn_b0), cb1=row(L1_gnn_b1), cb2=row(L1_gnn_b2),
        lower=np.tril(np.ones((P, P), np.float32), -1), src=np.asarray(src).reshape(-1, 1), dst=np.asarray(dst).reshape(-1, 1), attr=np.asarray(edge_attr_2),
        least=least, above=above,
        cbT=np.ascontiguousarray(np.stack([np.asarray(L1_gnn_b0), np.asarray(L1_gnn_b1), np.asarray(L1_gnn_b2)], 1)))


def kernel(**inputs):
    import numpy as np
    import concourse.bacc as bacc
    from concourse.bass_utils import run_bass_kernel_spmd
    arrays = {"in_" + k: np.ascontiguousarray(v) for k, v in host_arrays(**inputs).items()}
    nc = bacc.Bacc("TRN2", target_bir_lowering=False, num_devices=1)
    t = {k[3:]: nc.dram_tensor(k, v.shape, mybir.dt.from_np(v.dtype), kind="ExternalInput").ap() for k, v in arrays.items()}
    out = nc.dram_tensor("out", (ROWS, D), F32, kind="ExternalOutput").ap()
    build(nc, t, out)
    r = run_bass_kernel_spmd(nc, [arrays], core_ids=[0])
    return r.results[0]["out"][:NODES]
```

```python
import concourse.bass as bass
from concourse import mybir
from contextlib import ExitStack

F32 = mybir.dt.float32
I32 = mybir.dt.int32
BF16 = mybir.dt.bfloat16
F16 = mybir.dt.float16
ALU = mybir.AluOpType
ACT = mybir.ActivationFunctionType
AX = mybir.AxisListType.X

NODES, EDGES, D, P = 6250, 200000, 128, 128
B = -(-NODES // P)
ROWS = B * P
BN_EPS = LN_EPS = 1e-5
SKIP = 1 << 20
NODE_TILES = B
EPT = 125
EDGE_TILES = EDGES // EPT

TILES = -(-EDGES // P)
RT = 9
RC = -(-TILES // RT)
LEAD = 9
STRIP, HALO, STRIPS = 512, 8, 12
IT, UT = 7, 21
COLS = LEAD + RT * RC + 3
CAP = 34
SLOTS = CAP * B
SPAN = 8
CT = 17
CHUNKS = SLOTS // CT
PT = 9
NL = 7
NP = 36
GROUPS = [4, 4, 4, 4, 1]
TURNS = [8, 8, 6]


def general_path(nc, sem, t, out):
    x, src, dst, attr = t["x"], t["src"], t["dst"], t["attr"]
    w1, b1, gamma, beta, w2, b2 = t["w1"], t["b1"], t["gamma"], t["beta"], t["w2"], t["b2"]
    conv_w, conv_b = [t["cw0"], t["cw1"], t["cw2"]], [t["cb0"], t["cb1"], t["cb2"]]
    ident_in, lower_in = t["ident_f"], t["lower"]
    ctx = ExitStack()
    with ctx:
        def sb(name, shape, dt=F32):
            return ctx.enter_context(nc.sbuf_tensor("any_" + name, shape, dt))

        def ps(name, shape):
            return ctx.enter_context(nc.psum_tensor("any_" + name, shape, F32))

        def table(name, width=D):
            return nc.dram_tensor("any_" + name, [ROWS, width], F32).ap()

        p_table, q_table = table("p_table"), table("q_table")
        msg_sum, src_count, degree = table("msg_sum"), table("src_count"), table("degree")
        inv_root = table("inv_root")
        x1_table = table("x1_table")
        g_table = [table(f"g_table{c}") for c in range(3)]
        conv_sum = [table(f"conv_sum{c}") for c in range(3)]

        w1_sb = sb("w1_sb", [P, 2, D])
        wa_sb = sb("wa_sb", [P, 2, D])
        w2_sb = sb("w2_sb", [P, D])
        cw_sb = sb("cw_sb", [P, 3, D])
        vec = sb("vec", [P, 7, D])
        B1, GAMMA, BETA, B2, CB = 0, 1, 2, 3, 4
        ident = sb("ident", [P, P])
        lower = sb("lower", [P, P])
        ones = sb("ones", [P, P])
        zeros = sb("zeros", [P, D])

        key_row_i = sb("key_row_i", [P, EPT], I32)
        key_row = sb("key_row", [P, EPT])
        src_i = sb("src_i", [P, 1], I32)
        dst_i = sb("dst_i", [P, 1], I32)
        at = sb("at", [P, 2])
        key_f = sb("key_f", [P, 1])
        equal = sb("equal", [P, EPT])
        earlier = sb("earlier", [P, EPT])
        n_earlier = sb("n_earlier", [P, 1])
        write_f = sb("write_f", [P, 1])
        write_i = sb("write_i", [P, 1], I32)
        from_src = sb("from_src", [P, D])
        from_dst = sb("from_dst", [P, D])
        row_sum = sb("row_sum", [P, D])
        new_row = sb("new_row", [P, D])
        h = [sb(f"h{n}", [P, D]) for n in range(4)]
        mean = sb("mean", [P, D])
        var = sb("var", [P, D])
        scale = sb("scale", [P, D])
        shift = sb("shift", [P, D])
        nx = sb("nx", [P, D])
        nin = sb("nin", [P, D])
        nT = sb("nT", [P, D])
        ncnt = sb("ncnt", [P, D])
        na, nb, n_out, n_out2 = (sb(f"n{c}", [P, D]) for c in "abcd")
        stat = sb("stat", [P, 4])
        root = sb("root", [P, D])

        merged = ps("merged", [P, D])
        total = ps("total", [P, D])
        nps = ps("nps", [P, D])
        npq = ps("npq", [P, D])

        loaded = sem("any_loaded")
        preset = sem("preset")
        step = sem("step")
        outputs = sem("outputs")
        LOADS = 0

        class Chain:
            def __init__(self, eng):
                self.eng, self.at, self.i = eng, 0, 0

            def __call__(self, ins):
                self.at = self.at + 1
                ins.then_inc(step, 1)
                self.eng.wait_ge(step, self.at)

        def wait_then(eng, s, v):
            eng.wait_ge(s, v)
            eng.nop(nofuse=True)
        programs = {"sync": [], "gpsimd": [], "tensor": [], "vector": [], "scalar": []}
        chain_box = {}

        small = [(w1_sb[:, :, :], w1[0:2 * D, :].rearrange("(a p) d -> p a d", a=2)),
                 (w2_sb[:, :], w2), (ident[:, :], ident_in), (lower[:, :], lower_in)]
        small += [(wa_sb[:, a, :], w1[2 * D + a:2 * D + a + 1, :].to_broadcast([P, D])) for a in range(2)]
        small += [(cw_sb[:, c, :], conv_w[c]) for c in range(3)]
        small += [(vec[:, n, :], v.to_broadcast([P, D])) for n, v in enumerate([b1, gamma, beta, b2, *conv_b])]

        def setup_sync(eng):
            for to, of in small:
                eng.dma_start(to, of).then_inc(loaded, 16)
            eng.wait_ge(preset, 2)
            for t in (msg_sum, src_count, degree):
                what = ones if t is degree else zeros
                for n in range(NODE_TILES):
                    eng.dma_start(t[n * P:(n + 1) * P, :], what[:, :]).then_inc(loaded, 16)
            eng.wait_ge(loaded, 16 * (len(small) + 3 * NODE_TILES))
        ALL_LOADED = 16 * (len(small) + 3 * NODE_TILES)

        def setup_vector(eng):
            nc.vector.memset(ones[:], 1.0).then_inc(preset, 1)
            nc.vector.memset(zeros[:], 0.0).then_inc(preset, 1)
            eng.wait_ge(preset, 2)
            eng.wait_ge(loaded, ALL_LOADED)

        def node_pass(name, loads, transposed, weights, compute, stores, rows_last=P, before=None):
            got, done, stored = (sem(f"{name}_{s}") for s in ("got", "done", "stored"))
            if transposed is not None:
                ready, turned, copied, made = (sem(f"{name}_{s}") for s in ("ready", "turned", "copied", "made"))

            def rows(t, i):
                return t[bass.ts(i, P), :]

            def sync(eng):
                with eng.Fori(0, NODE_TILES) as i:
                    for to, of in loads:
                        eng.dma_start(to, rows(of, i)).then_inc(got, 16)
                    wait_then(eng, done, i + 1)
                    for to, of in stores:
                        eng.dma_start(rows(to, i), of).then_inc(stored, 16)
                    wait_then(eng, stored, 16 * len(stores) * (i + 1))

            def vector(eng, chain):
                base = chain.at
                with eng.Fori(0, NODE_TILES) as i:
                    steps = compute.steps
                    chain.at, chain.i = base + i * steps, i
                    eng.wait_ge(got, 16 * len(loads) * (i + 1))
                    if before:
                        before(chain)
                    if transposed is not None:
                        nc.vector.memset(stat[:, 3:4], 0.0).then_inc(ready, 1)
                        eng.wait_ge(turned, i + 1)
                        nc.vector.tensor_copy(nT[:, :], nps[:, :]).then_inc(copied, 1)
                        eng.wait_ge(made, i + 1)
                    compute(chain)
                    nc.vector.memset(stat[:, 3:4], 0.0).then_inc(done, 1)
                    eng.wait_ge(done, i + 1)
                    eng.wait_ge(stored, 16 * len(stores) * (i + 1))
                chain.at = base + NODE_TILES * steps

            def tensor(eng):
                if transposed is None:
                    return
                with eng.Fori(0, NODE_TILES) as i:
                    eng.wait_ge(ready, i + 1)
                    nc.tensor.transpose(nps[:, :], transposed, ident[:, :]).then_inc(turned, 1)
                    eng.wait_ge(copied, i + 1)
                    for w, to in zip(weights, (nps, npq)):
                        last = nc.tensor.matmul(to[:, :], nT[:, :], w, start=True, stop=True)
                    last.then_inc(made, 1)

            programs["sync"].append(sync)
            programs["vector"].append(vector)
            programs["tensor"].append(tensor)
            return stored, 16 * len(stores) * NODE_TILES

        def counted(steps):
            def wrap(f):
                f.steps = steps
                return f
            return wrap

        def inverse_root(c, name, i, to, of, t):
            before = roots[name]
            nc.vector.memset(stat[:, 3:4], 0.0).then_inc(root_asked, 1)
            c.eng.wait_ge(rooted, i + (before + 1))
            c(nc.vector.reciprocal(to, t))
            c(nc.vector.tensor_tensor(t, to, to, ALU.mult))
            c(nc.vector.tensor_tensor(t, t, of, ALU.mult))
            c(nc.vector.tensor_scalar(t, t, -0.5, 1.5, ALU.mult, ALU.add))
            c(nc.vector.tensor_tensor(to, to, t, ALU.mult))
        ROOT_STEPS = 5

        def root_service(name, to, of, times):
            before = roots[name] = roots["all"]
            roots["all"] += times

            def scalar(eng):
                with eng.Fori(0, times) as i:
                    eng.wait_ge(root_asked, i + (before + 1))
                    nc.scalar.activation(to, of, ACT.Sqrt).then_inc(rooted, 1)
            programs["scalar"].append(scalar)
        roots = {"all": 0}
        root_asked, rooted = sem("root_asked"), sem("rooted")

        def layer_norm(c, a, b, to, sc, name):
            c(nc.vector.tensor_reduce(out=sc[:, 0:1], in_=a, op=ALU.add, axis=AX))
            c(nc.vector.tensor_scalar(sc[:, 0:1], sc[:, 0:1], 1.0 / D, None, ALU.mult))
            c(nc.vector.tensor_scalar(a, a, sc[:, 0:1], None, ALU.subtract))
            c(nc.vector.tensor_tensor(b, a, a, ALU.mult))
            c(nc.vector.tensor_reduce(out=sc[:, 1:2], in_=b, op=ALU.add, axis=AX))
            c(nc.vector.tensor_scalar(sc[:, 1:2], sc[:, 1:2], 1.0 / D, LN_EPS, ALU.mult, ALU.add))
            inverse_root(c, name, c.i, sc[:, 2:3], sc[:, 1:2], root[:, 0:1])
            c(nc.vector.tensor_scalar(to, a, sc[:, 2:3], None, ALU.mult))
        LN_STEPS = 7 + ROOT_STEPS

        def edge_pass(name, key, src_rows=None, dst_rows=None, compute=None, sum_to=None, all_sum=False, after=None):
            got, formed, products, updated = (sem(f"{name}_{s}") for s in ("got", "formed", "products", "updated"))
            scattered = sem(f"{name}_scattered") if sum_to is not None else None
            keys = {"src": src, "dst": dst}.get(key)
            key_i = {"src": src_i, "dst": dst_i}.get(key)
            n_loads = 3 + (keys is not None)
            gathers = [(to, tab, idx) for to, tab, idx in
                       ((from_src, src_rows, src_i), (from_dst, dst_rows, dst_i), (row_sum, sum_to, key_i)) if tab is not None]
            gathered = [sem(f"{name}_gathered{n}") for n in range(len(gathers))]
            row_keys = keys.rearrange("(t e) a -> t (e a)", e=EPT) if keys is not None else None

            def sync(eng):
                with eng.Fori(0, EDGE_TILES) as i:
                    eng.dma_start(src_i[0:EPT, :], src[bass.ts(i, EPT), :]).then_inc(got, 16)
                    eng.dma_start(dst_i[0:EPT, :], dst[bass.ts(i, EPT), :]).then_inc(got, 16)
                    eng.dma_start(at[0:EPT, :], attr[bass.ts(i, EPT), :]).then_inc(got, 16)
                    if keys is not None:
                        eng.dma_start(key_row_i[0:EPT, :], row_keys[bass.ds(i, 1), :].to_broadcast([EPT, EPT])).then_inc(got, 16)
                    if sum_to is not None:
                        wait_then(eng, scattered, 16 * (i + 1))
                    else:
                        wait_then(eng, updated, i + 1)

            def gpsimd(eng):
                with eng.Fori(0, EDGE_TILES) as i:
                    wait_then(eng, got, 16 * n_loads * (i + 1))
                    for (to, tab, idx), landed in zip(gathers, gathered):
                        nc.gpsimd.indirect_dma_start(to[0:EPT, :], None, tab,
                                                     bass.IndirectOffsetOnAxis(ap=idx[0:EPT, 0:1], axis=0)).then_inc(landed, 16)
                    for _, landed in zip(gathers, gathered):
                        wait_then(eng, landed, 16 * (i + 1))
                    if sum_to is not None:
                        wait_then(eng, updated, i + 1)
                        nc.gpsimd.indirect_dma_start(sum_to, bass.IndirectOffsetOnAxis(ap=write_i[0:EPT, 0:1], axis=0),
                                                     new_row[0:EPT, :], None, bounds_check=ROWS - 1,
                                                     oob_is_err=False).then_inc(scattered, 16)
                        wait_then(eng, scattered, 16 * (i + 1))
                    else:
                        wait_then(eng, updated, i + 1)

            def vector(eng, chain):
                base, steps = chain.at, (compute.steps if compute else 0) + (8 if sum_to is not None else 0)
                with eng.Fori(0, EDGE_TILES) as i:
                    chain.at = base + i * steps
                    e = slice(0, EPT)
                    eng.wait_ge(got, 16 * n_loads * (i + 1))
                    if sum_to is not None:
                        chain(nc.vector.tensor_copy(key_row[e, :], key_row_i[e, :]))
                        chain(nc.vector.tensor_copy(key_f[e, :], key_i[e, :]))
                        chain(nc.vector.tensor_scalar(equal[e, :], key_row[e, :], key_f[e, 0:1], None, ALU.is_equal))
                        chain(nc.vector.tensor_tensor(earlier[e, :], equal[e, :], lower[e, 0:EPT], ALU.mult))
                        chain(nc.vector.tensor_reduce(out=n_earlier[e, :], in_=earlier[e, :], op=ALU.add, axis=AX))
                        chain(nc.vector.tensor_scalar(write_f[e, :], n_earlier[e, :], float(SKIP), None, ALU.mult))
                        chain(nc.vector.tensor_tensor(write_f[e, :], write_f[e, :], key_f[e, :], ALU.add))
                        chain(nc.vector.tensor_copy(write_i[e, :], write_f[e, :]))
                    if gathers:
                        for _, landed in zip(gathers, gathered):
                            eng.wait_ge(landed, 16 * (i + 1))
                    if compute:
                        compute(chain)
                    nc.vector.memset(stat[:, 3:4], 0.0).then_inc(formed, 1)
                    eng.wait_ge(products, i + 1)
                    if sum_to is not None:
                        nc.vector.tensor_tensor(new_row[e, :], row_sum[e, :], merged[e, :], ALU.add).then_inc(updated, 1)
                        eng.wait_ge(updated, i + 1)
                        eng.wait_ge(scattered, 16 * (i + 1))
                    else:
                        nc.vector.memset(stat[:, 2:3], 0.0).then_inc(updated, 1)
                        eng.wait_ge(updated, i + 1)
                chain.at = base + EDGE_TILES * steps
                if after:
                    eng.wait_ge(products, EDGE_TILES + 1)
                    after(chain)

            def tensor(eng):
                result = compute.result if compute else (from_src if src_rows is not None else ones)
                if all_sum:
                    nc.tensor.matmul(total[:, :], ones[:, :], zeros[:, :], start=True, stop=False)
                with eng.Fori(0, EDGE_TILES) as i:
                    eng.wait_ge(formed, i + 1)
                    if all_sum:
                        nc.tensor.matmul(total[:, :], ones[0:EPT, :], result[0:EPT, :], start=False, stop=False).then_inc(products, 1)
                    else:
                        nc.tensor.matmul(merged[0:EPT, :], equal[0:EPT, :], result[0:EPT, :], start=True, stop=True).then_inc(products, 1)
                if all_sum:
                    nc.tensor.matmul(total[:, :], ones[:, :], zeros[:, :], start=False, stop=True).then_inc(products, 1)

            programs["sync"].append(sync)
            programs["gpsimd"].append(gpsimd)
            programs["vector"].append(vector)
            programs["tensor"].append(tensor)
            return scattered, 16 * EDGE_TILES

        e = slice(0, EPT)

        def edge_h(c):
            c(nc.vector.tensor_tensor(h[0][e, :], from_src[e, :], from_dst[e, :], ALU.add))
            c(nc.vector.scalar_tensor_tensor(out=h[1][e, :], in0=wa_sb[e, 0, :], scalar=at[e, 0:1], in1=h[0][e, :], op0=ALU.mult, op1=ALU.add))
            c(nc.vector.scalar_tensor_tensor(out=h[0][e, :], in0=wa_sb[e, 1, :], scalar=at[e, 1:2], in1=h[1][e, :], op0=ALU.mult, op1=ALU.add))

        def fence(name, waits):
            def wait(eng, *_):
                for s, v in waits:
                    eng.wait_ge(s, v)
            for engine in ("sync", "gpsimd", "vector", "tensor"):
                programs[engine].append(wait)

        @counted(2)
        def project(c):
            c(nc.vector.tensor_tensor(na[:, :], nps[:, :], vec[:, B1, :], ALU.add))
            c(nc.vector.tensor_copy(nb[:, :], npq[:, :]))
        fence("tables", [node_pass("project", [(nx[:, :], x)], nx[:, :], [w1_sb[:, 0, :], w1_sb[:, 1, :]], project,
                                   [(p_table, na[:, :]), (q_table, nb[:, :])])])

        counts = [edge_pass("src_count", "src", sum_to=src_count), edge_pass("degree", "dst", sum_to=degree)]
        fence("counts", counts)

        @counted(ROOT_STEPS)
        def rooted_degree(c):
            inverse_root(c, "degree", c.i, na[:, :], ncnt[:, :], root[:, :])
        root_service("degree", root[:, :], ncnt[:, :], NODE_TILES)
        fence("degree", [node_pass("degree_root", [(ncnt[:, :], degree)], None, [], rooted_degree, [(inv_root, na[:, :])])])

        @counted(3)
        def hidden(c):
            edge_h(c)
        hidden.result = h[0]

        def take_mean(c):
            c(nc.vector.tensor_scalar(mean[:, :], total[:, :], 1.0 / EDGES, None, ALU.mult))
        edge_pass("mean", None, p_table, q_table, hidden, all_sum=True, after=take_mean)

        @counted(5)
        def squares(c):
            edge_h(c)
            c(nc.vector.tensor_tensor(h[1][e, :], h[0][e, :], mean[e, :], ALU.subtract))
            c(nc.vector.tensor_tensor(h[2][e, :], h[1][e, :], h[1][e, :], ALU.mult))
        squares.result = h[2]

        root_service("batch", root[:, :], var[:, :], 1)

        def take_scale(c):
            c(nc.vector.tensor_scalar(var[:, :], total[:, :], 1.0 / EDGES, BN_EPS, ALU.mult, ALU.add))
            inverse_root(c, "batch", 0, scale[:, :], var[:, :], root[:, :])
            c(nc.vector.tensor_tensor(scale[:, :], scale[:, :], vec[:, GAMMA, :], ALU.mult))
            c(nc.vector.tensor_tensor(var[:, :], mean[:, :], scale[:, :], ALU.mult))
            c(nc.vector.tensor_tensor(shift[:, :], vec[:, BETA, :], var[:, :], ALU.subtract))
        mean_taken = sem("mean_taken")

        def signal_mean(eng, c):
            nc.vector.memset(stat[:, 3:4], 0.0).then_inc(mean_taken, 1)
        programs["vector"].append(signal_mean)
        programs["tensor"].append(lambda eng: eng.wait_ge(mean_taken, 1))
        edge_pass("var", None, p_table, q_table, squares, all_sum=True, after=take_scale)

        @counted(6)
        def activated(c):
            edge_h(c)
            c(nc.vector.tensor_tensor(h[1][e, :], h[0][e, :], scale[e, :], ALU.mult))
            c(nc.vector.tensor_tensor(h[2][e, :], h[1][e, :], shift[e, :], ALU.add))
            c(nc.vector.tensor_scalar(h[3][e, :], h[2][e, :], 0.0, None, ALU.max))
        activated.result = h[3]
        fence("messages", [edge_pass("messages", "src", p_table, q_table, activated, sum_to=msg_sum)])

        @counted(6 + LN_STEPS)
        def first_norm(c):
            c(nc.vector.tensor_tensor(na[:, :], ncnt[:, :], vec[:, B2, :], ALU.mult))
            c(nc.vector.tensor_tensor(na[:, :], na[:, :], nps[:, :], ALU.add))
            c(nc.vector.tensor_scalar(nb[:, :], ncnt[:, :], 1.0, None, ALU.add))
            c(nc.vector.reciprocal(n_out[:, :], nb[:, :]))
            c(nc.vector.tensor_tensor(na[:, :], na[:, :], n_out[:, :], ALU.mult))
            c(nc.vector.scalar_tensor_tensor(out=nb[:, :], in0=nx[:, :], scalar=2.0, in1=na[:, :], op0=ALU.mult, op1=ALU.add))
            layer_norm(c, nb[:, :], na[:, :], n_out[:, :], stat, "first")
        root_service("first", root[:, 0:1], stat[:, 1:2], NODE_TILES)
        fence("x1", [node_pass("first_norm", [(nx[:, :], x), (nin[:, :], msg_sum), (ncnt[:, :], src_count)], nin[:, :],
                               [w2_sb[:, :]], first_norm, [(x1_table, n_out[:, :])])])

        def scaled(rows):
            @counted(1)
            def f(c):
                c(nc.vector.tensor_tensor(n_out[:, :], nps[:, :], ncnt[:, :], ALU.mult))
            return f

        def hidden_rows(layer):
            def f(c):
                c(nc.vector.tensor_tensor(nb[:, :], nin[:, :], ncnt[:, :], ALU.mult))
                c(nc.vector.tensor_tensor(nb[:, :], nb[:, :], vec[:, CB + layer, :], ALU.add))
                c(nc.vector.tensor_scalar(nin[:, :], nb[:, :], 0.0, None, ALU.max))
            return f

        for layer in range(3):
            compute = scaled(None)
            if layer:
                compute.steps += 3
            stores = [(g_table[layer], n_out[:, :]), (conv_sum[layer], n_out[:, :])]
            fence("g", [node_pass(f"conv{layer}", [(nin[:, :], conv_sum[layer - 1] if layer else x1_table), (ncnt[:, :], inv_root)],
                                  nin[:, :], [cw_sb[:, layer, :]], compute, stores,
                                  before=hidden_rows(layer - 1) if layer else None)])
            fence("sums", [edge_pass(f"sums{layer}", "dst", g_table[layer], sum_to=conv_sum[layer])])

        @counted(3 + LN_STEPS)
        def last_norm(c):
            c(nc.vector.tensor_tensor(nb[:, :], nin[:, :], ncnt[:, :], ALU.mult))
            c(nc.vector.tensor_tensor(na[:, :], nb[:, :], vec[:, CB + 2, :], ALU.add))
            c(nc.vector.tensor_tensor(nb[:, :], na[:, :], nx[:, :], ALU.add))
            layer_norm(c, nb[:, :], na[:, :], n_out[:, :], stat, "last")
        root_service("last", root[:, 0:1], stat[:, 1:2], NODE_TILES)
        node_pass("last_norm", [(nin[:, :], conv_sum[2]), (ncnt[:, :], inv_root), (nx[:, :], x1_table)], None, [], last_norm,
                  [(out, n_out[:, :])])

        def sync_program(eng):
            setup_sync(eng)
            for f in programs["sync"]:
                f(eng)

        def gpsimd_program(eng):
            eng.wait_ge(loaded, ALL_LOADED)
            for f in programs["gpsimd"]:
                f(eng)

        def tensor_program(eng):
            eng.wait_ge(preset, 2)
            eng.wait_ge(loaded, ALL_LOADED)
            for f in programs["tensor"]:
                f(eng)

        def scalar_program(eng):
            for f in programs["scalar"]:
                f(eng)

        def vector_program(eng):
            chain = Chain(eng)
            setup_vector(eng)
            for f in programs["vector"]:
                f(eng, chain)
    return sync_program, gpsimd_program, tensor_program, scalar_program, vector_program


def build(nc, t, out):
    def table(name, shape, dt=F32):
        return nc.dram_tensor(name, shape, dt).ap()
    perm = table("perm", [P * SLOTS, 4]); at_dram = table("at_dram", [STRIPS + 1, P, B, STRIP], BF16)
    deg_dram = table("deg_dram", [1, ROWS]); p_dram = table("p_dram", [ROWS, D]); q_dram = table("q_dram", [ROWS, D])
    h_dram = table("h_dram", [CHUNKS, P, CT * D]); early_dram = table("early_dram", [NP, P, CT * D]); dinv_dram = table("dinv_dram", [1, ROWS])
    outer = ExitStack()
    with outer:
        def mk(ctx):
            return (lambda n, s, d=F32: ctx.enter_context(nc.sbuf_tensor(n, s, d)),
                    lambda n, s, d=F32: ctx.enter_context(nc.psum_tensor(n, s, d)))
        sem = lambda n: outer.enter_context(nc.semaphore(n))
        sb, _ = mk(outer)
        V = nc.vector
        iota_lo = sb("iota_lo", [P, P], F16); identb = sb("identb", [P, P], BF16)
        ones_f = sb("ones_f", [P, P])
        w1 = sb("w1", [P, 2, D]); wrep = sb("wrep", [P, D])
        vec = sb("vec", [P, 7, D])
        sgn = sb("sgn", [P, D])
        masks = sb("masks", [P, 8])
        fits = sb("fits", [P, 1], I32); misfit = sb("misfit", [P, 1]); misfit2 = sb("misfit2", [P, 1]); misfit3 = sb("misfit3", [P, 1]); top = sb("top", [P, B]); over = sb("over", [1, STRIPS + 1])
        alpha = sb("alpha", [P, D]); shift = sb("shift", [P, D]); dummy2 = sb("dummy2", [P, 1])
        one_col = sb("one_col", [P, 1]); zero_col = sb("zero_col", [P, 1])
        S = {n: sem(n) for n in "part_clear cleared src_in dst_in attr_in rec_dst rec_lo low_bits weights_done deg_part keys_done neg_done loaded filled dv set_done hot_ready rank_ready idx_done lo_ready key_ready pair_ready added strip_clear deg_ready deg_read act proj_ready proj_p proj_q proj_in proj_out1 proj_out2 phase1 deg_out misfit_ready misfit_sum fits_ready".split()}
        slot_ready = [sem(f"slot_ready{u}") for u in range(4)]
        scattered = [sem(f"scattered{u}") for u in range(4)]
        stored = [sem(f"stored{u}") for u in range(2)]
        early_in, early_done, early_out = ([sem(f"early_{n}{u}") for u in range(2)] for n in ("in", "done", "out"))
        fit_stack = ExitStack()
        fit_sem = lambda n: fit_stack.enter_context(nc.semaphore(n))
        S.update({n: fit_sem(n) for n in "copied less_bound less_bound2 own_done bound_ready recs_in early_back0 early_back1 as_done hot2 turned oht_ready mm_done h_done squared summed stat_done p_in p3_done stats_ready bn_sqrt bn_rooted z_done z_used sum_taken phase2 credits3 node_done dinv_made dinv_out dinv_in s_scaled s_turned s_copied s_made x_normed x_turned x_copied x_made chunk_used y_taken yt_ready tail_done ln_ask ln_root out_ready out_sent dv3 credits dv2 s_out nd pe_n act_n root_a root_b x_in bias_done g_taken".split()})
        rec_in = [fit_sem(f"rec_in{u}") for u in range(2)]
        gathered = [fit_sem(f"gathered{u}") for u in range(2)]
        h_out = [fit_sem(f"h_out{u}") for u in range(2)]
        h_in = [fit_sem(f"h_in{u}") for u in range(2)]
        a_in = [fit_sem(f"a_in{u}") for u in range(7)]
        fit_stack.close()
        general = general_path(nc, sem, t, out)

        def put(eng, s, v):
            eng.wait_ge(s, v)
            eng.nop(nofuse=True)

        def barrier(eng, s):
            eng.sem_inc(s, 1)
            eng.wait_ge(s, 5)

        def newton(link, to, of, t):
            link(V.reciprocal(to, t))
            link(V.tensor_tensor(t, to, to, ALU.mult))
            link(V.tensor_tensor(t, t, of, ALU.mult))
            link(V.tensor_scalar(t, t, -0.5, 1.5, ALU.mult, ALU.add))
            link(V.tensor_tensor(to, to, t, ALU.mult))

        one = ExitStack()
        with one:
            sb, ps = mk(one)
            src_i = sb("src_i", [P, COLS], I32); dst_i = sb("dst_i", [P, COLS], I32); first_i = sb("first_i", [P, COLS], I32)
            blk = sb("blk", [P, COLS + 2 * RT]); neg_lo = sb("neg_lo", [P, COLS]); key = sb("key", [P, COLS])
            place = sb("place", [P, COLS]); idx_all = src_i
            rec = sb("rec", [P, COLS, 4])
            offs = sb("offs", [1, STRIPS * IT + 2, 24], I32)
            iotak = sb("iotak", [P, B]); iota_key = sb("iota_key", [P, SPAN * B], F16)
            upper = sb("upper", [P, P], BF16); onesb = sb("onesb", [P, P], BF16); zerob = sb("zerob", [P, STRIP], BF16)
            hot = [sb(f"hot{u}", [P, (RT + 1) * B], BF16) for u in range(2)]
            ranks = [sb(f"ranks{u}", [P, RT * B]) for u in range(2)]; own = ranks
            base = [sb(f"base{u}", [P, B]) for u in range(2)]
            r_f = sb("r_f", [P, 2 * RT]); r_i = sb("r_i", [P, 2 * RT], I32); rhi = sb("rhi", [P, 2 * RT], I32); t_f = sb("t_f", [P, 2 * RT])
            strip = [sb(f"strip{u}", [P, B, STRIP + 2 * HALO], BF16) for u in range(2)]
            sq = [sb(f"sq{u}", [P, P], BF16) for u in range(3)]
            hot_lo = [sb(f"hot_lo{u}", [P, P], BF16) for u in range(NL)]
            hot_key = [sb(f"hot_key{u}", [P, SPAN * B], BF16) for u in range(NL)]
            ix_slot = [sb(f"ix_slot{u}", [P, RT], I32) for u in range(4)]
            rec_slot = [sb(f"rec_slot{u}", [P, RT, 4]) for u in range(4)]
            deg = [sb(f"deg{u}", [1, STRIP]) for u in range(1)]
            dummy = sb("dummy1", [P, 1])
            pr = [ps(f"pr{u}", [P, 512]) for u in range(2)]
            pk = [ps(f"pk{u}", [P, 512]) for u in range(3)]
            pd = ps("pd", [P, 512])
            px = [ps(f"px{u}", [P, 512]) for u in range(2)]
            xT = strip[0][:].rearrange("p b d -> p (b d)").bitcast(F32)[:, 0:ROWS]
            pq = strip[1][:].rearrange("p b d -> p (b d)").bitcast(F32)
            pT, qT = pq[:, 0:ROWS], pq[:, ROWS:2 * ROWS]
            stage = strip[0][:].rearrange("p b d -> p (b d)").bitcast(F32)[:, ROWS:]
            least, above = stage[:, 0:COLS], stage[:, COLS:2 * COLS]
            attr_stage = stage[:, 2 * COLS:2 * COLS + 2 * RT * RC].rearrange("p (t c) -> p t c", c=2)
            low = key[:].bitcast(I32)
            rec_f = rec[:].rearrange("p t c -> p (t c)")
            early = [rec_f[:, u * CT * D:(u + 1) * CT * D] for u in range(2)]
            early_rec = [rec_f[:, 2 * CT * D + u * CT * 4:2 * CT * D + (u + 1) * CT * 4] for u in range(2)]
            loads = [(w1[:], t["w1"][0:2 * D, :].rearrange("(a p) d -> p a d", a=2)), (wrep[:], t["wrep"]), (masks[:], t["masks"]),
                     (first_i[:], t["d0_row"].to_broadcast([P, COLS])), (least, t["least"].to_broadcast([P, COLS])),
                     (above, t["above"].to_broadcast([P, COLS])), (iota_lo[:], t["iota_lo"]), (iota_key[:], t["iota_key"])]
            loads += [(vec[:, n, :], t[k].to_broadcast([P, D])) for n, k in enumerate(("b1", "gamma", "beta", "b2", "cb0", "cb1", "cb2"))]
            LOADED = 16 * len(loads)
            UPT = IT * UT

            def sp_1(sp):
                for to, of in ((src_i[:], t["src_t"]), (iotak[:], t["iotak"]), (hot_lo[0][:].bitcast(F16), t["upper"]), (hot_lo[1][:].bitcast(F16), t["ident_h"])):
                    sp.dma_start(to, of).then_inc(S["src_in"], 16)
                sp.dma_start(dst_i[:], t["dst_t"]).then_inc(S["dst_in"], 16)
                sp.dma_start(attr_stage, t["attr_t"]).then_inc(S["attr_in"], 16)
                sp.dma_start(perm.rearrange("(p t) c -> p (t c)", p=P), t["empty"]).then_inc(S["filled"], 16)
                for to, of in loads:
                    sp.dma_start(to, of).then_inc(S["loaded"], 16)
                sp.wait_ge(S["rec_dst"], 3)

                def step(n, slot, have_prev, half):
                    if have_prev is not None:
                        put(sp, scattered[slot], have_prev)
                    put(sp, S["idx_done"], half)
                    sp.dma_start(ix_slot[slot][:], idx_all[:, bass.ds(LEAD + n * RT, RT)]).then_inc(slot_ready[slot], 16)
                    sp.dma_start(rec_slot[slot][:], rec[:, bass.ds(LEAD + n * RT, RT), :]).then_inc(slot_ready[slot], 16)
                for u in range(4):
                    step(u, u, None, u // 2 + 1)
                with sp.Fori(1, RC // 4) as c:
                    for u in range(4):
                        step(c * 4 + u, u, c * (16 * RT), c * 2 + (u // 2 + 1))
                for u in range(RC % 4):
                    step(RC // 4 * 4 + u, u, RC // 4 * 16 * RT, RC // 2)
                for u in range(4):
                    sp.wait_ge(slot_ready[u], 32 * (RC // 4 + (u < RC % 4)))
                for u in range(4):
                    sp.wait_ge(scattered[u], 16 * RT * (RC // 4 + (u < RC % 4)))

                def early_records(u, k):
                    sp.dma_start(early_rec[u], perm.rearrange("(p t) c -> p (t c)", p=P)[:, bass.ds(k * (2 * CT * 4), CT * 4)]).then_inc(early_in[u], 16)

                def early_store(u, k, times):
                    put(sp, early_done[u], times * (16 * CT))
                    sp.dma_start(early_dram[bass.ds(k, 1)].rearrange("a p c -> (a p) c"), early[u]).then_inc(early_out[u], 16)
                early_records(0, 0)
                early_records(1, 1)
                with sp.Fori(0, NP // 2 - 1) as c:
                    for u in range(2):
                        early_store(u, c * 2 + u, c + 1)
                        early_records(u, c * 2 + u + 2)
                for u in range(2):
                    early_store(u, NP - 2 + u, NP // 2)
                for u in range(2):
                    sp.wait_ge(early_out[u], 16 * (NP // 2))
                sp.wait_ge(S["deg_read"], STRIPS + 2)

            def pool_1(pool):
                pool.wait_ge(S["filled"], 16)

                def step(slot, times):
                    put(pool, slot_ready[slot], times * 32)
                    for k in range(RT):
                        nc.gpsimd.indirect_dma_start(perm, bass.IndirectOffsetOnAxis(ap=ix_slot[slot][:, k:k + 1], axis=0),
                                                     rec_slot[slot][:, k, :], None, bounds_check=P * SLOTS - 1,
                                                     oob_is_err=False).then_inc(scattered[slot], 16)
                with pool.Fori(0, RC // 4) as c:
                    for u in range(4):
                        step(u, c + 1)
                for u in range(RC % 4):
                    step(u, RC // 4 + 1)
                for u in range(4):
                    pool.wait_ge(scattered[u], 16 * RT * (RC // 4 + (u < RC % 4)))
                pool.wait_ge(S["proj_out1"], 16)

                def early_gather(u, times):
                    put(pool, early_in[u], times * 16 + 16)
                    if not isinstance(times, int):
                        put(pool, early_out[u], times * 16)
                    for k in range(CT):
                        nc.gpsimd.indirect_dma_start(early[u][:, k * D:(k + 1) * D], None, q_dram,
                                                     bass.IndirectOffsetOnAxis(ap=early_rec[u].bitcast(I32)[:, 4 * k:4 * k + 1], axis=0)).then_inc(early_done[u], 16)
                early_gather(0, 0)
                early_gather(1, 0)
                with pool.Fori(1, NP // 2) as c:
                    for u in range(2):
                        early_gather(u, c)
                for u in range(2):
                    pool.wait_ge(early_done[u], 16 * CT * (NP // 2))

            def pe_1(pe):
                pe.wait_ge(S["set_done"], 1)
                with pe.Fori(0, RC // 2) as c:
                    for u in range(2):
                        pe.wait_ge(S["hot_ready"], c * 2 + u + 1)
                        nc.tensor.matmul(pr[u][:, 0:490], upper[:], hot[u][:], start=True, stop=False)
                        for dl in range(1, RT + 1):
                            last = nc.tensor.matmul(pr[u][:, dl * B:490], onesb[:], hot[u][:, 0:(RT + 1 - dl) * B], start=False, stop=dl == RT)
                        last.then_inc(S["rank_ready"], 1)
                pe.wait_ge(S["proj_in"], 16)
                pe.wait_ge(S["weights_done"], 1)

                def project(g, par, nb, need):
                    if need is not None:
                        pe.wait_ge(S["proj_p"], need)
                        pe.wait_ge(S["proj_q"], need)
                    bp, bq = ((pk[0], pk[1]), (px[0], px[1]))[par]
                    for w, bank in ((0, bp), (1, bq)):
                        for m in range(nb):
                            last = nc.tensor.matmul(bank[:, m * P:(m + 1) * P], xT[:, bass.ds((g * 4 + m) * P, P)] if not isinstance(g, int) else xT[:, (g * 4 + m) * P:(g * 4 + m + 1) * P],
                                                    w1[:, w, :], start=True, stop=True)
                    last.then_inc(S["proj_ready"], 1)
                project(0, 0, 4, None); project(1, 1, 4, None)
                for g in range(2, 13):
                    project(g, g % 2, 4 if g < 12 else 1, g - 1)

                def degree_begin():
                    nc.tensor.matmul(pd[:, :], onesb[:], zerob[:], start=True, stop=False)

                def degree_step(buf, i, width=STRIP):
                    for m in range(7):
                        last = nc.tensor.matmul(pd[:, 0:width], onesb[:], strip[buf][:, bass.ds(i * 7 + m, 1), HALO:HALO + width], start=False, stop=False)
                    last.then_inc(S["deg_part"], 1)

                def degree_end():
                    nc.tensor.matmul(pd[:, :], onesb[:], zerob[:], start=False, stop=True).then_inc(S["deg_ready"], 1)

                def tiles(n0, first):
                    for u in range(UT):
                        pe.wait_ge(S["lo_ready"], n0 + u + 1)
                        pe.wait_ge(S["key_ready"], n0 + u + 1)
                        if not first or u >= 3:
                            pe.wait_ge(S["added"], n0 + u - 2)
                        nc.tensor.matmul(pk[u % 3][:, 0:SPAN * B], hot_lo[u % NL][:], hot_key[u % NL][:], start=True, stop=True).then_inc(S["pair_ready"], 1)
                pe.wait_ge(S["proj_p"], 13)
                pe.wait_ge(S["proj_q"], 13)
                tiles(0, True)
                with pe.Fori(1, IT) as i:
                    tiles(i * UT, False)
                with pe.Fori(0, (STRIPS - 2) // 2) as jj:
                    for h in range(2):
                        j = jj * 2 + 1 + h
                        pe.wait_ge(S["added"], j * UPT)
                        pe.wait_ge(S["deg_read"], j)
                        degree_begin()
                        with pe.Fori(0, IT) as i:
                            degree_step(h, i)
                            tiles(j * UPT + i * UT, False)
                        degree_end()
                for j, its in ((STRIPS - 1, IT), (STRIPS, 2)):
                    pe.wait_ge(S["added"], j * UPT)
                    pe.wait_ge(S["deg_read"], j)
                    degree_begin()
                    if j == STRIPS - 1:
                        with pe.Fori(0, its) as i:
                            degree_step(1 - j % 2, i)
                            tiles(i * UT + j * UPT, False)
                    else:
                        with pe.Fori(0, its) as i:
                            tiles(i * UT + j * UPT, False)
                        with pe.Fori(0, IT) as i:
                            degree_step(1 - j % 2, i)
                    degree_end()
                pe.wait_ge(S["added"], (STRIPS * IT + 2) * UT)
                pe.wait_ge(S["deg_read"], STRIPS + 1)
                degree_begin()
                with pe.Fori(0, IT) as i:
                    degree_step(0, i, P)
                degree_end()
                pe.wait_ge(S["misfit_ready"], 1)
                nc.tensor.matmul(px[0][:, 0:1], ones_f[:], misfit[:], start=True, stop=True).then_inc(S["misfit_sum"], 1)

            def act_1(act):
                act.dma_start(xT, t["xT"]).then_inc(S["proj_in"], 16)
                act.wait_ge(S["dst_in"], 16)
                nc.scalar.activation(rec[:].bitcast(I32)[:, :, 0], dst_i[:], ACT.Copy).then_inc(S["rec_dst"], 1)
                act.wait_ge(S["attr_in"], 16)
                nc.scalar.activation(rec[:, LEAD:LEAD + RT * RC, 2:4], attr_stage, ACT.Copy).then_inc(S["rec_dst"], 1)
                act.wait_ge(S["low_bits"], 1)
                nc.scalar.activation(neg_lo[:], low, ACT.Copy, scale=-1.0).then_inc(S["neg_done"], 1)
                nc.scalar.activation(rec[:, :, 1], low, ACT.Copy).then_inc(S["rec_dst"], 1)
                act.wait_ge(S["keys_done"], 1)
                act.wait_ge(S["loaded"], LOADED)
                act.wait_ge(S["neg_done"], 1)
                for g in range(13):
                    act.wait_ge(S["proj_ready"], g + 1)
                    w = (4 if g < 12 else 1) * P
                    nc.scalar.activation(qT[:, g * 512:g * 512 + w], (pk[1], px[1])[g % 2][:, 0:w], ACT.Copy).then_inc(S["proj_q"], 1)
                act.wait_ge(S["proj_q"], 13)
                act.wait_ge(S["proj_p"], 13)
                act.dma_start(q_dram.rearrange("(b p) d -> p b d", p=P), qT.rearrange("p (b d) -> p b d", b=B)).then_inc(S["proj_out1"], 16)
                act.dma_start(p_dram.rearrange("(b p) d -> p b d", p=P), pT.rearrange("p (b d) -> p b d", b=B)).then_inc(S["proj_out2"], 16)

                def tiles(n0, col0, first):
                    def square(u):
                        if not first or u >= NL:
                            act.wait_ge(S["pair_ready"], n0 + u - NL + 1)
                        if not first or u >= 3:
                            act.wait_ge(S["lo_ready"], n0 + u - 2)
                        nc.scalar.activation(sq[u % 3][:], iota_lo[:], ACT.Square, bias=neg_lo[:, bass.ds(col0 + u, 1)] if not isinstance(col0, int) else neg_lo[:, col0 + u:col0 + u + 1]).then_inc(S["act"], 1)
                    square(0)
                    for u in range(UT):
                        if u + 1 < UT:
                            square(u + 1)
                        act.wait_ge(S["act"], n0 + u + 1)
                        nc.scalar.activation(hot_lo[u % NL][:], sq[u % 3][:], ACT.Relu, bias=one_col[:, 0:1], scale=-1.0).then_inc(S["lo_ready"], 1)

                def store(buf, j):
                    act.dma_start(at_dram[bass.ds(j, 1)].rearrange("a p b d -> (a p) b d") if not isinstance(j, int) else at_dram[j],
                                  strip[buf][:, :, HALO:HALO + STRIP]).then_inc(stored[buf], 16)
                def degree_out(j, w=STRIP):
                    put(act, S["deg_read"], j + 2)
                    act.dma_start(deg_dram[0:1, bass.ds(j * STRIP, w)], deg[0][:, 0:w]).then_inc(S["deg_out"], 16)
                tiles(0, 0, True)
                with act.Fori(1, IT) as i:
                    tiles(i * UT, i * UT, False)
                def clear_part(buf, j, i, stores):
                    act.wait_ge(stored[buf], stores)
                    act.wait_ge(S["deg_part"], (j - 1) * 7 + i + 1)
                    piece = strip[buf][:].rearrange("p (g b) d -> p g (b d)", g=7).bitcast(F32)[:, bass.ds(i, 1), :]
                    nc.scalar.activation(piece, zero_col[:, 0:1].unsqueeze(2).to_broadcast([P, 1, B // 7 * (STRIP + 2 * HALO) // 2]), ACT.Copy).then_inc(S["part_clear"], 1)

                def clear_end(buf, j, blocks):
                    act.wait_ge(S["part_clear"], j * 7)
                    for m in range(blocks):
                        last = nc.scalar.activation(strip[buf][:, bass.ds(j * 4 + 4 + m, 1), HALO + P * m:HALO + P * (m + 1)], identb[:].unsqueeze(1), ACT.Copy)
                    last.then_inc(S["cleared"], 1)
                act.wait_ge(S["added"], UPT)
                store(0, 0)
                with act.Fori(0, IT) as i:
                    tiles(UPT + i * UT, P + i * UT, False)
                    clear_part(0, 1, i, 16)
                clear_end(0, 1, 4)
                def strip_pair(jj):
                    for h in range(2):
                        j = jj * 2 + h
                        put(act, S["added"], j * UPT)
                        store(1 - h, j - 1)
                        degree_out(j - 2)
                        with act.Fori(0, IT) as i:
                            tiles(j * UPT + i * UT, j * P + i * UT, False)
                            clear_part(1 - h, j, i, (jj + h) * 16)
                        clear_end(1 - h, j, 1 if isinstance(j, int) and j == STRIPS - 1 else 4)
                with act.Fori(1, STRIPS // 2 - 1) as jj:
                    strip_pair(jj)
                strip_pair(STRIPS // 2 - 1)
                act.wait_ge(S["added"], STRIPS * UPT)
                store(1, STRIPS - 1)
                degree_out(STRIPS - 2)
                with act.Fori(0, 2) as i:
                    tiles(i * UT + STRIPS * UPT, i * UT + STRIPS * P, False)
                act.wait_ge(S["added"], (STRIPS * IT + 2) * UT)
                act.dma_start(at_dram[STRIPS, :, :, 0:P], strip[0][:, :, HALO:HALO + P]).then_inc(stored[0], 16)
                degree_out(STRIPS - 1)
                degree_out(STRIPS, P)
                act.wait_ge(S["deg_out"], 1 + 16 * (STRIPS + 1))
                act.wait_ge(stored[0], 16 * 7)
                act.wait_ge(stored[1], 16 * 6)

            def dve_1(dve):
                c = [0]

                def link(ins):
                    c[0] += 1
                    ins.then_inc(S["dv"], 1)
                    dve.wait_ge(S["dv"], c[0])
                for to, v in ((zerob, 0.0), (onesb, 1.0), (one_col, 1.0), (zero_col, 0.0), (ones_f, 1.0), (hot[0], 0.0), (hot[1], 0.0), (base[0], 0.0)):
                    link(V.memset(to[:], v))
                link(V.memset(blk[:, COLS:], float(B)))
                dve.wait_ge(S["src_in"], 64)
                link(V.tensor_copy(upper[:], hot_lo[0][:].bitcast(F16)))
                link(V.tensor_copy(identb[:], hot_lo[1][:].bitcast(F16)))
                link(V.tensor_scalar(low, src_i[:], 7, None, ALU.arith_shift_right))
                link(V.tensor_copy(blk[:, 0:COLS], low))
                V.tensor_scalar(low, src_i[:], P - 1, None, ALU.bitwise_and).then_inc(S["low_bits"], 1)
                link(V.tensor_scalar(place[:], blk[:, 0:COLS], float(B) - 0.5, float(SKIP), ALU.is_gt, ALU.mult))
                link(V.scalar_tensor_tensor(out=place[:], in0=blk[:, 0:COLS], scalar=float(CAP), in1=place[:], op0=ALU.mult, op1=ALU.add))
                V.memset(dummy[:], 0.0).then_inc(S["set_done"], 1)
                dve.wait_ge(S["set_done"], 1)
                V.memset(dummy[:], 0.0).then_inc(S["deg_read"], 1)
                dve.wait_ge(S["deg_read"], 1)
                V.memset(dummy[:], 0.0).then_inc(S["deg_out"], 1)
                dve.wait_ge(S["deg_out"], 1)
                c0 = c[0]
                STEPS = 13

                def hot_make(u, cols):
                    return V.tensor_tensor(hot[u][:, 0:RT * B].rearrange("p (t k) -> p t k", t=RT),
                                           blk[:, cols].unsqueeze(2).to_broadcast([P, RT, B]), iotak[:].unsqueeze(1).to_broadcast([P, RT, B]), ALU.is_equal)
                for u in range(2):
                    hot_make(u, slice(LEAD + u * RT, LEAD + u * RT + RT)).then_inc(S["hot_ready"], 1)
                with dve.Fori(0, RC // 2) as cc:
                    def after(n):
                        dve.wait_ge(S["dv"], cc * STEPS + (c0 + n))

                    def op(ins):
                        ins.then_inc(S["dv"], 1)

                    def c3(ap):
                        return ap.rearrange("p (t k) -> p t k", t=RT)
                    cols = bass.ds(cc * (2 * RT) + LEAD, 2 * RT)
                    dve.wait_ge(S["rank_ready"], cc * 2 + 1)
                    op(V.tensor_tensor(c3(ranks[0][:]), c3(pr[0][:, 0:RT * B]), base[0][:].unsqueeze(1).to_broadcast([P, RT, B]), ALU.add))
                    op(V.tensor_tensor(base[1][:], base[0][:], pr[0][:, RT * B:490], ALU.add))
                    after(1); op(V.tensor_tensor(own[0][:], ranks[0][:], hot[0][:, 0:RT * B], ALU.mult))
                    dve.wait_ge(S["rank_ready"], cc * 2 + 2)
                    after(2); op(V.tensor_tensor(c3(ranks[1][:]), c3(pr[1][:, 0:RT * B]), base[1][:].unsqueeze(1).to_broadcast([P, RT, B]), ALU.add))
                    op(V.tensor_tensor(base[0][:], base[1][:], pr[1][:, RT * B:490], ALU.add))
                    after(3); op(V.tensor_reduce(out=r_f[:, 0:RT], in_=c3(own[0][:]), op=ALU.add, axis=AX))
                    after(4); op(V.tensor_tensor(own[1][:], ranks[1][:], hot[1][:, 0:RT * B], ALU.mult))
                    hot_make(0, bass.ds(cc * (2 * RT) + (LEAD + 2 * RT), RT)).then_inc(S["hot_ready"], 1)
                    after(7); op(V.tensor_reduce(out=r_f[:, RT:], in_=c3(own[1][:]), op=ALU.add, axis=AX))
                    hot_make(1, bass.ds(cc * (2 * RT) + (LEAD + 3 * RT), RT)).then_inc(S["hot_ready"], 1)
                    after(8); op(V.tensor_scalar(t_f[:], r_f[:], float(CAP * P) - 0.5, float(1 << 30), ALU.is_gt, ALU.mult))
                    after(9); op(V.tensor_tensor(r_i[:], r_f[:], t_f[:], ALU.add))
                    after(10); op(V.tensor_scalar(rhi[:], r_i[:], 7, None, ALU.arith_shift_right))
                    after(11); op(V.scalar_tensor_tensor(out=t_f[:], in0=rhi[:], scalar=float(1 - P * SLOTS), in1=place[:, cols], op0=ALU.mult, op1=ALU.add))
                    after(12); op(V.scalar_tensor_tensor(out=idx_all[:, cols], in0=r_i[:], scalar=float(SLOTS), in1=t_f[:], op0=ALU.mult, op1=ALU.add))
                    after(13); V.memset(dummy[:], 0.0).then_inc(S["idx_done"], 1)
                    dve.wait_ge(S["hot_ready"], cc * 2 + 4)
                    dve.wait_ge(S["idx_done"], cc + 1)
                c[0] = c0 + STEPS * (RC // 2)
                link(V.tensor_reduce(out=misfit2[:], in_=base[0][:], op=ALU.max, axis=AX))
                link(V.tensor_scalar(misfit[:], misfit2[:], float(CAP * P), None, ALU.is_gt))
                link(V.memset(offs[:], 0))
                dve.wait_ge(S["loaded"], LOADED)
                dve.wait_ge(S["rec_dst"], 3)
                dve.wait_ge(S["neg_done"], 1)
                link(V.tensor_scalar(sgn[:], vec[:, 1, :], 0.0, 2.0, ALU.is_ge, ALU.mult))
                link(V.tensor_scalar(sgn[:], sgn[:], -1.0, None, ALU.add))
                link(V.tensor_tensor(w1[:, 0, :], w1[:, 0, :], sgn[:], ALU.mult))
                link(V.tensor_tensor(w1[:, 1, :], w1[:, 1, :], sgn[:], ALU.mult))
                link(V.tensor_tensor(wrep[:], wrep[:], sgn[:], ALU.mult))
                link(V.tensor_tensor(vec[:, 0, :], vec[:, 0, :], sgn[:], ALU.mult))
                V.memset(dummy[:], 0.0).then_inc(S["weights_done"], 1)
                dve.wait_ge(S["weights_done"], 1)
                link(V.tensor_tensor(key[:], dst_i[:], first_i[:], ALU.subtract))
                link(V.tensor_tensor(least, least, dst_i[:], ALU.is_gt))
                link(V.tensor_tensor(above, above, dst_i[:], ALU.is_le))
                link(V.tensor_tensor(least, least, above, ALU.add))
                link(V.scalar_tensor_tensor(out=above, in0=key[:], scalar=0.0, in1=least, op0=ALU.is_lt, op1=ALU.add))
                link(V.scalar_tensor_tensor(out=least, in0=key[:], scalar=float(SPAN - 1), in1=above, op0=ALU.is_gt, op1=ALU.add))
                link(V.scalar_tensor_tensor(out=above, in0=blk[:, 0:COLS], scalar=float(B), in1=least, op0=ALU.is_lt, op1=ALU.mult))
                link(V.tensor_reduce(out=misfit3[:], in_=above, op=ALU.max, axis=AX))
                link(V.tensor_tensor(misfit[:], misfit[:], misfit3[:], ALU.add))
                link(V.scalar_tensor_tensor(out=key[:], in0=blk[:, 0:COLS], scalar=float(SPAN), in1=key[:], op0=ALU.mult, op1=ALU.add))
                for j in range(STRIPS + 1):
                    w = IT if j < STRIPS else 2
                    link(V.tensor_scalar(offs[:, j * IT:j * IT + w, 0:UT], first_i[0:1, j * P:j * P + w * UT].rearrange("a (i u) -> a i u", u=UT),
                                         float(HALO - STRIP * j), 0.0, ALU.add, ALU.max))
                link(V.tensor_scalar(offs[:, :, 0:UT], offs[:, :, 0:UT], float(STRIP + HALO), None, ALU.min))
                V.memset(dummy[:], 0.0).then_inc(S["keys_done"], 1)
                dve.wait_ge(S["keys_done"], 1)
                for g in range(13):
                    nb = 4 if g < 12 else 1
                    dve.wait_ge(S["proj_ready"], g + 1)
                    V.tensor_tensor(pT[:, g * 512:g * 512 + nb * P].rearrange("p (b d) -> p b d", b=nb),
                                    (pk[0], px[0])[g % 2][:, 0:nb * P].rearrange("p (b d) -> p b d", b=nb),
                                    vec[:, 0:1, :].to_broadcast([P, nb, D]), ALU.add).then_inc(S["proj_p"], 1)

                def clear_strip(buf, j, last=False):
                    V.memset(strip[buf][:], 0.0).then_inc(S["strip_clear"], 1)
                    dve.wait_ge(S["strip_clear"], j * 2 + 1)
                    for m in range(1 if last else 4):
                        ins = V.tensor_copy(strip[buf][:, bass.ds(j * 4 + m, 1), HALO + P * m:HALO + P * (m + 1)] if not isinstance(j, int) else
                                            strip[buf][:, j * 4 + m:j * 4 + m + 1, HALO + P * m:HALO + P * (m + 1)], identb[:].unsqueeze(1))
                    ins.then_inc(S["strip_clear"], 1)
                    dve.wait_ge(S["strip_clear"], j * 2 + 2)
                    dve.nop(nofuse=True)

                def keyhot(n0, col0, u, first):
                    if not (first and u < NL):
                        dve.wait_ge(S["pair_ready"], n0 + u - NL + 1)
                    V.tensor_scalar(hot_key[u % NL][:], iota_key[:], key[:, bass.ds(col0 + u, 1)] if not isinstance(col0, int) else key[:, col0 + u:col0 + u + 1], None, ALU.is_equal).then_inc(S["key_ready"], 1)

                def tiles(buf, n0, col0, first, it):
                    row = offs[0:1, bass.ds(it, 1), :] if not isinstance(it, int) else offs[0:1, it:it + 1, :]
                    _, at_col = nc.values_load_multi_w_load_instructions(row.rearrange("a b c -> a (b c)"), engines=[mybir.EngineType.DVE],
                                                                         min_val=0, max_val=STRIP + HALO, skip_runtime_bounds_check_because="clamped above")
                    for u in range(2):
                        keyhot(n0, col0, u, first)
                    for u in range(UT):
                        if u + 2 < UT:
                            keyhot(n0, col0, u + 2, first)
                        dve.wait_ge(S["pair_ready"], n0 + u + 1)
                        if not (first and u == 0):
                            dve.wait_ge(S["added"], n0 + u)
                        w = strip[buf][:, :, bass.ds(at_col[u], SPAN)]
                        V.tensor_tensor(w, w, pk[u % 3][:, 0:SPAN * B].rearrange("p (b s) -> p b s", b=B), ALU.add).then_inc(S["added"], 1)

                def take_degree(j, w=STRIP):
                    dve.wait_ge(S["deg_ready"], j + 1)
                    dve.wait_ge(S["deg_out"], j * 16 + 1)
                    V.tensor_reduce(out=over[:, bass.ds(j, 1)], in_=pd[0:1, 0:w], op=ALU.max, axis=AX)
                    V.tensor_copy(deg[0][:, 0:w], pd[0:1, 0:w]).then_inc(S["deg_read"], 1)
                    dve.wait_ge(S["deg_read"], j + 2)
                dve.wait_ge(S["proj_ready"], 13)
                clear_strip(0, 0)
                tiles(0, 0, 0, True, 0)
                with dve.Fori(1, IT) as i:
                    tiles(0, i * UT, i * UT, False, i)
                dve.wait_ge(S["proj_out1"], 16); dve.wait_ge(S["proj_out2"], 16)
                clear_strip(1, 1)
                with dve.Fori(0, IT) as i:
                    tiles(1, i * UT + UPT, i * UT + P, False, i + IT)
                with dve.Fori(1, STRIPS // 2) as jj:
                    for h in range(2):
                        j = jj * 2 + h
                        take_degree(j - 2)
                        put(dve, S["cleared"], j - 1)
                        with dve.Fori(0, IT) as i:
                            tiles(h, j * UPT + i * UT, j * P + i * UT, False, j * IT + i)
                take_degree(STRIPS - 2)
                put(dve, S["cleared"], STRIPS - 1)
                with dve.Fori(0, 2) as i:
                    tiles(0, i * UT + STRIPS * UPT, i * UT + STRIPS * P, False, i + STRIPS * IT)
                take_degree(STRIPS - 1)
                take_degree(STRIPS, P)
                link(V.tensor_reduce(out=top[0:1, 0:1], in_=over[:], op=ALU.max, axis=AX))
                link(V.scalar_tensor_tensor(out=misfit[0:1, :], in0=top[0:1, 0:1], scalar=255.0, in1=misfit[0:1, :], op0=ALU.is_gt, op1=ALU.add))
                V.memset(dummy[:], 0.0).then_inc(S["misfit_ready"], 1)
                dve.wait_ge(S["misfit_sum"], 1)
                V.tensor_scalar(fits[:], px[0][:, 0:1], 0.5, None, ALU.is_lt).then_inc(S["fits_ready"], 1)
                dve.wait_ge(S["fits_ready"], 1)

            phase_one = (sp_1, pool_1, pe_1, act_1, dve_1)

        sb, _ = mk(outer)
        ring_raw = sb("ring_raw", [P, 2 * (B * 130 + SLOTS * 4)], BF16)
        ring_f = ring_raw[:].bitcast(F32)
        s_all = ring_f[:, 0:B * 130].rearrange("p (b d) -> p b d", b=B)
        recs = ring_f[:, B * 130:B * 130 + SLOTS * 4].rearrange("p (t c) -> p t c", c=4)
        x_in = ring_f[:, B * 130:B * 130 + ROWS].rearrange("p (b d) -> p b d", b=B)
        two = ExitStack()
        with two:
            sb, ps = mk(two)
            p3 = sb("p3", [P, B, 3, D], BF16)
            p_stage = ring_f[:, 0:ROWS].rearrange("p (b d) -> p b d", b=B)
            gi_all = sb("gi_all", [P, SLOTS], I32)
            gi = [sb(f"gi{u}", [P, CT], I32) for u in range(2)]
            hotb = sb("hotb", [P, CT, P], BF16)
            parts = sb("parts", [P, 20, 32], BF16)
            res = [sb(f"res{u}", [P, CT, 2]) for u in range(2)]
            turn_sb = [sb(f"turn_sb{u}", [P, 22, P], BF16) for u in range(2)]
            G = [sb(f"G{u}", [P, CT, D]) for u in range(2)]
            H = [sb(f"H{u}", [P, CT, D]) for u in range(2)]
            col_sum = [sb(f"col_sum{u}", [P, 2, D]) for u in range(2)]
            zb = [sb(f"zb{u}", [P, CT, 130]) for u in range(2)]
            hotf = [sb(f"hotf{u}", [P, CT, P]) for u in range(2)]
            wsz = sb("wsz", [P, 4, D], BF16)
            wt = [sb(f"wt{u}", [P, D]) for u in range(4)]
            neg_g = sb("neg_g", [P, D]); bt = [sb(f"bt{u}", [P, D]) for u in range(4)]
            zero_f = sb("zero_f", [P, 512])
            tb = [ps(f"tb{u}", [P, 1024], BF16) for u in range(3)]
            ph = [ps(f"ph{u}", [P, 512]) for u in range(2)]
            st = ps("st", [P, 512])
            pS = ps("pS", [P, 512])
            rec_rows = perm.rearrange("(p t) c -> p t c", p=P)
            START = [0, 8, 16]

            def drive(eng, front, back):
                front(0, 0, 0)
                for lo, hi in ((0, NP), (NP, CHUNKS // 2 - 1)):
                    with eng.Fori(lo, hi) as k:
                        front(k * 2 + 1, 1, k)
                        back(k * 2, 0, k, lo == 0)
                        front(k * 2 + 2, 0, k + 1)
                        back(k * 2 + 1, 1, k)
                front(CHUNKS - 1, 1, CHUNKS // 2 - 1)
                back(CHUNKS - 2, 0, CHUNKS // 2 - 1)
                back(CHUNKS - 1, 1, CHUNKS // 2 - 1)

            def sp_2(sp):
                sp.dma_start(p_stage, p_dram.rearrange("(b p) d -> p b d", p=P)).then_inc(S["p_in"], 16)
                sp.dma_start(recs, rec_rows).then_inc(S["recs_in"], 16)
                sp.wait_ge(S["credits"], 1)
                sp.wait_ge(S["copied"], 1)

                def early_rows(k, u):
                    sp.dma_start(zb[u][:, :, 0:D], early_dram[bass.ds(k, 1)].rearrange("a p (t d) -> (a p) t d", t=CT)).then_inc(S[f"early_back{u}"], 16)

                def indices(q, u):
                    sp.dma_start(gi[u][:], gi_all[:, bass.ds(q * CT, CT)]).then_inc(rec_in[u], 16)

                def back(q, par):
                    put(sp, S["h_done"], q * 5 + 15)
                    sp.dma_start(h_dram[bass.ds(q, 1)].rearrange("a p c -> (a p) c"), H[par][:].rearrange("p t d -> p (t d)")).then_inc(h_out[par], 16)
                for u in range(2):
                    early_rows(u, u)
                    indices(2 * u + 1, u)
                with sp.Fori(0, NP // 2 - 1) as c:
                    for u in range(2):
                        back(c * 4 + 2 * u, 0)
                        early_rows(c * 2 + u + 2, u)
                        put(sp, gathered[u], (c + 1) * (16 * CT))
                        indices(c * 4 + 2 * u + 5, u)
                        back(c * 4 + 2 * u + 1, 1)
                for u in range(2):
                    back(2 * (NP - 2 + u), 0)
                    sp.wait_ge(gathered[u], NP // 2 * 16 * CT)
                    indices(2 * NP + u, u)
                    back(2 * (NP - 2 + u) + 1, 1)
                with sp.Fori(NP, CHUNKS // 2 - 1) as k:
                    for u in range(2):
                        put(sp, gathered[u], (k - (NP // 2 - 1)) * (16 * CT))
                        indices(k * 2 + u + 2, u)
                        back(k * 2 + u, u)
                for par in range(2):
                    back(CHUNKS - 2 + par, par)
                for u in range(2):
                    sp.wait_ge(h_out[u], 16 * (CHUNKS // 2) + 1)
                with sp.Fori(0, CHUNKS // 2) as k:
                    for par in range(2):
                        q = k * 2 + par
                        put(sp, S["less_bound"], q + 1)
                        put(sp, S["less_bound2"], q + 1)
                        sp.dma_start(G[par][:].rearrange("p t d -> p (t d)"), h_dram[bass.ds(q, 1)].rearrange("a p c -> (a p) c")).then_inc(h_in[par], 16)

            def pool_2(pool):
                pool.wait_ge(S["credits"], 1)

                def gather(u, times, used):
                    put(pool, rec_in[u], times * 16 + 16)
                    for k in range(CT):
                        if k % 4 == 0 and used is not None:
                            put(pool, S["h_done"], used + (k // 4 + 1))
                        nc.gpsimd.indirect_dma_start(G[u][:, k, :], None, q_dram,
                                                     bass.IndirectOffsetOnAxis(ap=gi[u][:, k:k + 1], axis=0)).then_inc(gathered[u], 16)
                gather(0, 0, None)
                gather(1, 0, None)
                with pool.Fori(1, NP // 2) as c:
                    for u in range(2):
                        gather(u, c, c * 20 + (10 * u - 5))
                with pool.Fori(NP // 2, (CHUNKS - NP) // 2) as c:
                    for u in range(2):
                        gather(u, c, c * 10 + (u + NP) * 5)
                for u in range(2):
                    pool.wait_ge(gathered[u], 16 * CT * ((CHUNKS - NP) // 2))
                pool.wait_ge(S["bound_ready"], 1)
                with pool.Fori(0, CHUNKS // 2) as k:
                    for par in range(2):
                        put(pool, h_in[par], k * 16 + 16)
                        put(pool, S["z_done"], k * 2 + par + 1)
                        nc.gpsimd.tensor_tensor(H[par][:, 0:PT, :], G[par][:, 0:PT, :], neg_g[:].unsqueeze(1).to_broadcast([P, PT, D]), ALU.subtract).then_inc(S["less_bound"], 1)

            def pe_2(pe):
                pe.wait_ge(S["p3_done"], 1)
                nc.tensor.matmul(st[:, :], ones_f[:], zero_f[:], start=True, stop=False)

                def chunk_stats(of, par):
                    pe.wait_ge(S["summed"], of + 3)
                    nc.tensor.matmul(st[:, 0:2 * D], ones_f[:], col_sum[par][:].rearrange("p a d -> p (a d)"), start=False, stop=False).then_inc(S["stat_done"], 1)

                def front(q, par, r):
                    pe.wait_ge(S["hot2"], q + 1)
                    pe.wait_ge(S["as_done"], q + 3)
                    for g in range(3):
                        pe.wait_ge(S["oht_ready"], q * 3 + g + 1)
                        for k in range(TURNS[g]):
                            n = START[g] + k
                            of = hotb[:, n, :] if n < CT else parts[:, (n - CT) * 4:(n - CT) * 4 + 4, :].rearrange("p a b -> p (a b)")
                            last = nc.tensor.transpose(tb[g][:, k * P:(k + 1) * P], of, identb[:])
                        last.then_inc(S["turned"], 1)

                def back(q, par, r, early=False):
                    pe.wait_ge(S["oht_ready"], q * 3 + 6)
                    b = r

                    for g in range(5):
                        pe.wait_ge(S["h_done"], q * 5 + g + 9)
                        bank = ph[(par + g) % 2]
                        for k in range(GROUPS[g]):
                            n = 4 * g + k
                            to = bank[:, k * P:(k + 1) * P]
                            nc.tensor.matmul(to, turn_sb[par][:, CT + g, :], wsz[:, k, :], start=True, stop=False)
                            for m in range(3):
                                last = nc.tensor.matmul(to, turn_sb[par][:, n, :], p3[:, bass.ds(b, 1), m, :].rearrange("p a d -> p (a d)"), start=False, stop=m == 2)
                        last.then_inc(S["mm_done"], 1)
                        if g == 1:
                            chunk_stats(q - 2, par)
                drive(pe, front, back)
                chunk_stats(CHUNKS - 2, 0)
                chunk_stats(CHUNKS - 1, 1)
                nc.tensor.matmul(st[:, :], ones_f[:], zero_f[:], start=False, stop=True).then_inc(S["stats_ready"], 1)
                with pe.Fori(0, B) as k:
                    pe.wait_ge(S["sum_taken"], k + 1)
                    for par in range(2):
                        pe.wait_ge(S["z_done"], k * 2 + par + 3)
                        pe.wait_ge(S["own_done"], k * 2 + par + 1)
                        for n in range(CT):
                            last = nc.tensor.matmul(pS[:, 0:D + 1], hotf[par][:, n, :], zb[par][:, n, 0:D + 1],
                                                    start=par == 0 and n == 0, stop=par == 1 and n == CT - 1)
                        last.then_inc(S["z_used"], 1)

            def act_2(act):
                act.wait_ge(S["recs_in"], 16)
                nc.scalar.activation(gi_all[:], recs.bitcast(I32)[:, :, 0], ACT.Copy).then_inc(S["copied"], 1)
                act.wait_ge(S["credits"], 1)

                def front(q, par, r):
                    act.wait_ge(S["mm_done"], q * 5 + 5)
                    for g in range(3):
                        act.wait_ge(S["turned"], q * 3 + g + 4)
                        w = TURNS[g] * P
                        nc.scalar.activation(turn_sb[par][:, START[g]:START[g] + TURNS[g], :].rearrange("p a b -> p (a b)"), tb[g][:, 0:w], ACT.Copy).then_inc(S["oht_ready"], 1)

                def back(q, par, r, early=False):
                    act.wait_ge(S["h_done"], q * 5 + 15)
                    act.wait_ge(S["summed"], q + 1)
                    nc.scalar.activation(hotf[par][:], H[par][:], ACT.Square).then_inc(S["squared"], 1)
                drive(act, front, back)
                act.wait_ge(S["bn_sqrt"], 1)
                nc.scalar.activation(bt[1][:], bt[0][:], ACT.Sqrt).then_inc(S["bn_rooted"], 1)
                def positive(q, par):
                    act.wait_ge(S["less_bound"], q + 3)
                    act.wait_ge(S["less_bound2"], q + 3)
                    act.wait_ge(S["z_used"], q + 1)
                    nc.scalar.activation(zb[par][:, :, 0:D], H[par][:], ACT.Relu).then_inc(S["z_done"], 1)
                positive(0, 0)
                positive(1, 1)
                with act.Fori(0, B - 1) as k:
                    act.wait_ge(S["z_used"], k * 2 + 3)
                    positive(k * 2 + 2, 0)
                    act.wait_ge(S["z_used"], k * 2 + 4)
                    nc.scalar.activation(s_all[:, bass.ds(k, 1), 0:D + 1].rearrange("p a d -> p (a d)"), pS[:, 0:D + 1], ACT.Copy).then_inc(S["sum_taken"], 1)
                    positive(k * 2 + 3, 1)
                for k in (B - 1,):
                    act.wait_ge(S["z_used"], k * 2 + 4)
                    nc.scalar.activation(s_all[:, bass.ds(k, 1), 0:D + 1].rearrange("p a d -> p (a d)"), pS[:, 0:D + 1], ACT.Copy).then_inc(S["sum_taken"], 1)

            def dve_2(dve):
                c = [0]

                def link(ins):
                    c[0] += 1
                    ins.then_inc(S["dv2"], 1)
                    dve.wait_ge(S["dv2"], c[0])
                for n, k in (("as_done", 2), ("h_done", 10), ("turned", 3), ("oht_ready", 3), ("mm_done", 10), ("squared", 1),
                             ("summed", 1), ("z_done", 2), ("less_bound", 2), ("less_bound2", 2), ("z_used", 2), ("sum_taken", 1), ("hout0", 1), ("hout1", 1)):
                    handle = {"hout0": h_out[0], "hout1": h_out[1]}.get(n) or S[n]
                    for _ in range(k):
                        V.memset(dummy2[:], 0.0).then_inc(handle, 1)
                        dve.wait_ge(handle, _ + 1)
                link(V.memset(parts[:], 0.0)); link(V.memset(zero_f[:], 0.0))
                for u in range(2):
                    link(V.memset(zb[u][:], 1.0)); link(V.memset(col_sum[u][:], 0.0))
                link(V.memset(hotf[1][:], 0.0))
                link(V.memset(dummy2[:], 0.0))
                V.memset(dummy2[:], 0.0).then_inc(S["credits"], 1)
                dve.wait_ge(S["credits"], 1)

                def split3(outs, of, r0, r1):
                    link(V.tensor_copy(outs[0], of))
                    link(V.tensor_tensor(r0, of, outs[0], ALU.subtract))
                    link(V.tensor_copy(outs[1], r0))
                    link(V.tensor_tensor(r1, r0, outs[1], ALU.subtract))
                    link(V.tensor_copy(outs[2], r1))
                wb = [hotb[:, u, :] for u in range(3)]
                split3(wb, wrep[:], wt[0][:], wt[1][:])
                link(V.tensor_scalar(wt[2][:], wb[0], masks[:, 0:1], None, ALU.mult))
                link(V.scalar_tensor_tensor(out=wt[3][:], in0=wb[1], scalar=masks[:, 1:2], in1=wt[2][:], op0=ALU.mult, op1=ALU.add))
                link(V.scalar_tensor_tensor(out=wt[2][:], in0=wb[2], scalar=masks[:, 2:3], in1=wt[3][:], op0=ALU.mult, op1=ALU.add))
                for k in range(4):
                    link(V.tensor_scalar(wsz[:, k, :], wt[2][:], masks[:, 3 + k:4 + k], None, ALU.mult))
                dve.wait_ge(S["recs_in"], 16)
                dve.wait_ge(S["p_in"], 16)
                for b7 in range(0, B, 7):
                    blocks = slice(b7, b7 + 7)
                    split3([p3[:, blocks, m, :] for m in range(3)], p_stage[:, blocks, :], H[0][:, 0:7, :], H[1][:, 0:7, :])
                V.memset(dummy2[:], 0.0).then_inc(S["p3_done"], 1)
                dve.wait_ge(S["p3_done"], 1)
                c0 = c[0]

                def link_of(q, n, ins):
                    ins.then_inc(S["dv2"], 1)
                    dve.wait_ge(S["dv2"], q * 4 + (c0 + n))
                attrs = lambda q: recs[:, bass.ds(q * CT, CT), 2:4]
                thrice = lambda ap: ap.unsqueeze(2).to_broadcast([P, CT, 3, 2])
                part = lambda i: parts[:, 0:CT, 6 * i:6 * i + 6].rearrange("p t (j c) -> p t j c", j=3)

                def one_hots(q):
                    dve.wait_ge(S["turned"], q * 3 + 3)
                    V.tensor_tensor(hotb[:], iota_lo[:].unsqueeze(1).to_broadcast([P, CT, P]), recs[:, bass.ds(q * CT, CT), 1:2].to_broadcast([P, CT, P]), ALU.is_equal).then_inc(S["hot2"], 1)

                def attribute_parts(q):
                    link_of(q, 1, V.tensor_copy(part(0), thrice(attrs(q))))
                    link_of(q, 2, V.tensor_tensor(res[0][:], attrs(q), parts[:, 0:CT, 0:2], ALU.subtract))
                    link_of(q, 3, V.tensor_copy(part(1), thrice(res[0][:])))
                    link_of(q, 4, V.tensor_tensor(res[1][:], res[0][:], parts[:, 0:CT, 6:8], ALU.subtract))
                    V.tensor_copy(part(2), thrice(res[1][:])).then_inc(S["as_done"], 1)

                def back(q, par, r, rows, landed, count, ahead=True):
                    dve.wait_ge(landed, count)
                    dve.wait_ge(h_out[par], r * 16 + 1)
                    for g in range(5):
                        w = GROUPS[g] * P
                        dve.wait_ge(S["mm_done"], q * 5 + g + 11)
                        tiles = slice(4 * g, 4 * g + GROUPS[g])
                        V.tensor_tensor(H[par][:, tiles, :], ph[(par + g) % 2][:, 0:w].rearrange("p (t d) -> p t d", d=D), rows[:, tiles, 0:D], ALU.add).then_inc(S["h_done"], 1)
                        if ahead and g == 1:
                            one_hots(q + 2)
                            attribute_parts(q + 2)
                    sum_squares(q - 1, 1 - par)
                    dve.wait_ge(S["stat_done"], q + 1)
                    dve.wait_ge(S["h_done"], q * 5 + 15)
                    V.tensor_reduce(out=col_sum[par][:, 0, :], in_=H[par][:].rearrange("p t d -> p d t"), op=ALU.add, axis=AX)

                def sum_squares(of, par):
                    dve.wait_ge(S["squared"], of + 2)
                    V.tensor_reduce(out=col_sum[par][:, 1, :], in_=hotf[par][:].rearrange("p t d -> p d t"), op=ALU.add, axis=AX).then_inc(S["summed"], 1)
                for q in range(2):
                    one_hots(q)
                    attribute_parts(q)
                with dve.Fori(0, NP // 2) as quad:
                    for u in range(2):
                        k = quad * 2 + u
                        back(k * 2, 0, k, zb[u], S[f"early_back{u}"], quad * 16 + 16)
                        back(k * 2 + 1, 1, k, G[u], gathered[u], (quad + 1) * (16 * CT))
                with dve.Fori(NP, CHUNKS // 2 - 1) as k:
                    for u in range(2):
                        back(k * 2 + u, u, k, G[u], gathered[u], (k - (NP // 2 - 1)) * (16 * CT))
                for u in range(2):
                    back(CHUNKS - 2 + u, u, CHUNKS // 2 - 1, G[u], gathered[u], (CHUNKS - NP) // 2 * 16 * CT, ahead=False)
                sum_squares(CHUNKS - 1, 1)
                c[0] = c0 + 4 * CHUNKS
                dve.wait_ge(S["stats_ready"], 1)
                mean, e2, t2 = bt[2], bt[3], neg_g
                for u, to in ((0, mean), (1, e2)):
                    link(V.tensor_copy(to[:], st[:, u * D:(u + 1) * D]))
                    link(V.tensor_scalar(to[:], to[:], 1.0 / EDGES, None, ALU.mult))
                link(V.tensor_tensor(t2[:], mean[:], mean[:], ALU.mult))
                link(V.tensor_tensor(e2[:], e2[:], t2[:], ALU.subtract))
                link(V.tensor_scalar(bt[0][:], e2[:], 0.0, BN_EPS, ALU.max, ALU.add))
                V.memset(dummy2[:], 0.0).then_inc(S["bn_sqrt"], 1)
                dve.wait_ge(S["bn_rooted"], 1)
                newton(link, alpha[:], bt[0][:], bt[1][:])
                link(V.tensor_tensor(bt[1][:], vec[:, 1, :], sgn[:], ALU.mult))
                link(V.tensor_scalar(bt[1][:], bt[1][:], 1e-20, None, ALU.max))
                link(V.tensor_tensor(alpha[:], alpha[:], bt[1][:], ALU.mult))
                link(V.reciprocal(bt[1][:], alpha[:]))
                link(V.tensor_tensor(bt[1][:], bt[1][:], vec[:, 2, :], ALU.mult))
                link(V.tensor_tensor(neg_g[:], mean[:], bt[1][:], ALU.subtract))
                V.memset(dummy2[:], 0.0).then_inc(S["bound_ready"], 1)
                with dve.Fori(0, CHUNKS // 2) as k:
                    for par in range(2):
                        q = k * 2 + par
                        dve.wait_ge(h_in[par], k * 16 + 16)
                        dve.wait_ge(S["z_done"], q + 1)
                        V.tensor_tensor(H[par][:, PT:, :], G[par][:, PT:, :], neg_g[:].unsqueeze(1).to_broadcast([P, CT - PT, D]), ALU.subtract).then_inc(S["less_bound2"], 1)
                        dve.wait_ge(S["z_used"], q + 1)
                        V.tensor_tensor(hotf[par][:], iota_lo[:].unsqueeze(1).to_broadcast([P, CT, P]),
                                        recs[:, bass.ds(q * CT, CT), 1:2].to_broadcast([P, CT, P]), ALU.is_equal).then_inc(S["own_done"], 1)
            phase_two = (sp_2, pool_2, pe_2, act_2, dve_2)

        three = ExitStack()
        with three:
            sb, ps = mk(three)
            x1 = sb("x1", [P, B, D])
            dinv_row = sb("dinv_row", [P, ROWS]); dinv_col = sb("dinv_col", [P, B]); dc = [sb(f"dc{u}", [P, B]) for u in range(2)]; dr = [sb(f"dr{u}", [B, P]) for u in range(3)]
            g3 = [sb(f"g3_{u}", [P, B, 3, D], BF16) for u in range(2)]
            ring = [ring_raw[:, u * 3584:(u + 1) * 3584].rearrange("p (b d) -> p b d", b=7) for u in range(7)]
            s_in = s_all
            w2 = sb("w2", [P, D]); cw = sb("cw", [P, 3, D]); cb = sb("cb", [P, 3]); ident_f = sb("ident_f", [P, P])
            ta, tcn, tsq, ts, ga, gb, gc, xn = (sb(n, [P, 4, D]) for n in ("ta", "tcn", "tsq", "ts", "ga", "gb", "gc", "xn")); xT4 = sb("xT4", [P, 512])
            tT = sb("tT", [P, 512]); yt = tT; hT = xT4
            sm = [sb(f"sm{u}", [P, 4]) for u in range(6)]
            pa = ps("pa", [P, 512]); pb = ps("pb", [P, 512]); pg = ps("pg", [P, 512])
            py = [ps(f"py{u}", [P, 512]) for u in range(2)]
            dummy3 = sb("dummy3", [P, 1])
            NG = 13
            widths = [(j, 4) for j in range(12)] + [(12, 1)]
            loads3 = [(w2[:], t["w2"]), (ident_f[:], t["ident_f"]), (dr[0][:], deg_dram.rearrange("a (b p) -> (a b) p", p=P)),
                      (dc[0][:], deg_dram.rearrange("a (b p) -> p (a b)", p=P)),
                      (x_in, t["x"].rearrange("(b p) d -> p b d", p=P)), (cb[:], t["cbT"])]
            loads3 += [(cw[:, c, :], t[f"cw{c}"]) for c in range(3)]

            def fl(ap):
                return ap.rearrange("p a b -> p (a b)")

            def sp_3(sp):
                for to, of in loads3:
                    sp.dma_start(to, of, allow_slow_non_contiguous=True).then_inc(S["x_in"], 16)
                sp.wait_ge(S["dinv_made"], 1)
                sp.dma_start(dinv_dram.rearrange("a (b p) -> (a b) p", p=P), dr[1][:]).then_inc(S["dinv_out"], 16)
                sp.wait_ge(S["dinv_out"], 16)
                sp.dma_start(dinv_row[:], dinv_dram.to_broadcast([P, ROWS])).then_inc(S["dinv_in"], 16)
                sp.wait_ge(S["node_done"], NG)
                sp.wait_ge(S["credits3"], 1)

                def strip_loads(c, j, w):
                    for i in range(7):
                        put(sp, S["chunk_used"], (j + 13 * c) * 7 + i + 1)
                        sp.dma_start(ring[i][:, :, 0:w], at_dram[bass.ds(j, 1), :, 7 * i:7 * i + 7, 0:w].rearrange("a p b d -> (a p) b d")).then_inc(a_in[i], 16)
                for c in range(3):
                    with sp.Fori(0, 12) as j:
                        strip_loads(c, j, STRIP)
                    strip_loads(c, 12, P)

            def pool_3(pool):
                pool.wait_ge(S["node_done"], NG)

            def pe_3(pe):
                pe.wait_ge(S["x_in"], 16 * len(loads3))
                def a_group(j, nb):
                    pe.wait_ge(S["s_scaled"], j + 1)
                    for m in range(nb):
                        last = nc.tensor.transpose(pa[:, m * P:(m + 1) * P], ts[:, m, :], ident_f[:])
                    last.then_inc(S["s_turned"], 1)
                    pe.wait_ge(S["s_copied"], j + 1)
                    for m in range(nb):
                        last = nc.tensor.matmul(pb[:, m * P:(m + 1) * P], tT[:, m * P:(m + 1) * P], w2[:], start=True, stop=True)
                    last.then_inc(S["s_made"], 1)

                def b_group(j, nb):
                    pe.wait_ge(S["x_normed"], j + 1)
                    for m in range(nb):
                        last = nc.tensor.transpose(py[0][:, m * P:(m + 1) * P], xn[:, m, :], ident_f[:])
                    last.then_inc(S["x_turned"], 1)
                    pe.wait_ge(S["x_copied"], j + 1)
                    for m in range(nb):
                        last = nc.tensor.matmul(pg[:, m * P:(m + 1) * P], xT4[:, m * P:(m + 1) * P], cw[:, 0, :], start=True, stop=True)
                    last.then_inc(S["x_made"], 1)
                a_group(0, 4)
                with pe.Fori(0, 11) as j:
                    a_group(j + 1, 4)
                    b_group(j, 4)
                a_group(12, 1)
                b_group(11, 4)
                b_group(12, 1)

                pe.wait_ge(S["credits3"], 1)

                def tail(c, n, nb):
                    pe.wait_ge(S["bias_done"], n + 1)
                    pe.wait_ge(S["g_taken"], n + 1)
                    for m in range(nb):
                        sl = slice(m * P, (m + 1) * P)
                        if c < 2:
                            last = nc.tensor.matmul(pg[:, sl], hT[:, sl], cw[:, c + 1, :], start=True, stop=True)
                        else:
                            last = nc.tensor.transpose(pg[:, sl], hT[:, sl], ident_f[:])
                    last.then_inc(S["tail_done"], 1)

                def strip(c, j, par, w, has_tail):
                    n = j + 13 * c
                    pe.wait_ge(S["y_taken"], n + 1)
                    for i in range(7):
                        pe.wait_ge(a_in[i], (n + 1) * 16)
                        for m in range(7):
                            for k in range(3):
                                last = nc.tensor.matmul(py[par][:, 0:w], g3[c % 2][:, 7 * i + m, k, :], ring[i][:, m, 0:w],
                                                        start=i == m == k == 0, stop=i == m == 6 and k == 2)
                        last.then_inc(S["chunk_used"], 1)
                        if i == 1 and has_tail:
                            tail(c, n - 1, 4)
                for c in range(3):
                    pe.wait_ge(S["g_taken"], 13 * c + 1)
                    strip(c, 0, c % 2, STRIP, False)
                    with pe.Fori(0, 5) as k:
                        for h in range(2):
                            strip(c, k * 2 + (1 + h), (c + 1 + h) % 2, STRIP, True)
                    strip(c, 11, (c + 11) % 2, STRIP, True)
                    strip(c, 12, (c + 12) % 2, P, True)
                    tail(c, 13 * c + 12, 1)

            def act_3(act):
                act.wait_ge(S["root_a"], 1)
                nc.scalar.activation(dr[2][:], dr[0][:], ACT.Sqrt)
                nc.scalar.activation(dc[1][:], dc[0][:], ACT.Sqrt).then_inc(S["root_b"], 1)

                def a_group(j, nb):
                    act.wait_ge(S["s_turned"], j + 1)
                    nc.scalar.activation(tT[:, 0:nb * P], pa[:, 0:nb * P], ACT.Copy).then_inc(S["s_copied"], 1)

                def b_group(j, nb):
                    act.wait_ge(S["ln_ask"], j + 1)
                    nc.scalar.activation(sm[3][:], sm[2][:], ACT.Sqrt).then_inc(S["ln_root"], 1)
                    act.wait_ge(S["x_normed"], j + 1)
                    nc.scalar.activation(x1[:, bass.ds(j * 4, nb), :], xn[:, 0:nb, :], ACT.Copy)
                    act.wait_ge(S["x_turned"], j + 1)
                    nc.scalar.activation(xT4[:, 0:nb * P], py[0][:, 0:nb * P], ACT.Copy).then_inc(S["x_copied"], 1)
                a_group(0, 4)
                with act.Fori(0, 11) as j:
                    a_group(j + 1, 4)
                    b_group(j, 4)
                a_group(12, 1)
                b_group(11, 4)
                b_group(12, 1)

                def post(c, j, nb):
                    n = j + 13 * c
                    w = nb * P
                    act.wait_ge(S["yt_ready"], n + 1)
                    nc.scalar.activation(hT[:, 0:w], yt[:, 0:w], ACT.Relu if c < 2 else ACT.Identity, bias=cb[:, c:c + 1]).then_inc(S["bias_done"], 1)
                    if c == 2:
                        act.wait_ge(S["ln_ask"], j + 14)
                        nc.scalar.activation(sm[3][:], sm[2][:], ACT.Sqrt).then_inc(S["ln_root"], 1)
                        put(act, S["out_ready"], j + 1)
                        act.dma_start(out[bass.ds(j * 512, w), :].rearrange("(b p) d -> p b d", p=P), ta[:, 0:nb, :]).then_inc(S["out_sent"], 16)
                for c in range(3):
                    with act.Fori(0, 12) as j:
                        post(c, j, 4)
                    post(c, 12, 1)
                act.wait_ge(S["out_sent"], 16 * 13 + 1)

            def dve_3(dve):
                c3 = [0]

                def link(ins):
                    c3[0] += 1
                    ins.then_inc(S["dv3"], 1)
                    dve.wait_ge(S["dv3"], c3[0])
                dve.wait_ge(S["x_in"], 16 * len(loads3))
                for n, k in (("chunk_used", 7), ("y_taken", 2), ("g_taken", 0), ("out_sent", 1)):
                    for _ in range(k):
                        V.memset(dummy3[:], 0.0).then_inc(S[n], 1)
                        dve.wait_ge(S[n], _ + 1)
                V.memset(dummy3[:], 0.0).then_inc(S["root_a"], 1)
                dve.wait_ge(S["root_a"], 1)
                dve.wait_ge(S["root_b"], 1)
                newton(link, dr[1][:], dr[0][:], dr[2][:])
                V.memset(dummy3[:], 0.0).then_inc(S["dinv_made"], 1)
                dve.wait_ge(S["dinv_made"], 1)
                newton(link, dinv_col[:], dc[0][:], dc[1][:])
                base0 = c3[0]

                def bc(ap, nb):
                    return ap[:, 0:nb].unsqueeze(2).to_broadcast([P, nb, D])

                def norm(lk, nb, ask_at):
                    norm_a(lk, nb)
                    norm_b(lk, nb, ask_at)

                def norm_a(lk, nb):
                    A, C, Q = ta[:, 0:nb, :], tcn[:, 0:nb, :], tsq[:, 0:nb, :]
                    lk(V.tensor_reduce(out=sm[0][:, 0:nb], in_=A, op=ALU.add, axis=AX))
                    lk(V.tensor_scalar(sm[0][:, 0:nb], sm[0][:, 0:nb], 1.0 / D, None, ALU.mult))
                    lk(V.tensor_tensor(C, A, bc(sm[0], nb), ALU.subtract))
                    lk(V.tensor_tensor(Q, C, C, ALU.mult))
                    lk(V.tensor_reduce(out=sm[1][:, 0:nb], in_=Q, op=ALU.add, axis=AX))
                    V.tensor_scalar(sm[2][:, 0:nb], sm[1][:, 0:nb], 1.0 / D, LN_EPS, ALU.mult, ALU.add).then_inc(S["ln_ask"], 1)

                def norm_b(lk, nb, ask_at):
                    dve.wait_ge(S["ln_root"], ask_at)
                    newton(lk, sm[4][:, 0:nb], sm[2][:, 0:nb], sm[3][:, 0:nb])
                NORM = 10

                def scale_split(lk, to, j, nb):
                    G0, R0, R1 = ga[:, 0:nb, :], gb[:, 0:nb, :], gc[:, 0:nb, :]
                    dst = lambda m: to[:, bass.ds(j * 4, nb), m, :]
                    lk(V.tensor_tensor(G0, pg[:, 0:nb * P].rearrange("p (a b) -> p a b", a=nb), dinv_col[:, bass.ds(j * 4, nb)].unsqueeze(2).to_broadcast([P, nb, D]), ALU.mult))
                    lk(V.tensor_copy(dst(0), G0))
                    lk(V.tensor_tensor(R0, G0, dst(0), ALU.subtract))
                    lk(V.tensor_copy(dst(1), R0))
                    lk(V.tensor_tensor(R1, R0, dst(1), ALU.subtract))
                    lk(V.tensor_copy(dst(2), R1))
                SPLIT = 6
                K = 6 + NORM + SPLIT

                def node_groups(j, nb, next_nb, before, k0):
                    k = [0]

                    def lk(ins):
                        k[0] += 1
                        ins.then_inc(S["dv3"], 1)
                        dve.wait_ge(S["dv3"], j * K + (k0 + k[0]))
                    A = ta[:, 0:nb, :]
                    blocks = bass.ds(j * 4, nb)
                    cnt = s_in[:, blocks, D:D + 1]
                    lk(V.tensor_tensor(tcn[:, 0:nb, :], cnt.to_broadcast([P, nb, D]), vec[:, 3:4, :].to_broadcast([P, nb, D]), ALU.mult))
                    lk(V.tensor_scalar(sm[5][:, 0:nb], cnt.rearrange("p a b -> p (a b)"), 1.0, None, ALU.add))
                    lk(V.reciprocal(sm[4][:, 0:nb], sm[5][:, 0:nb]))
                    dve.wait_ge(S["s_made"], j + 1)
                    lk(V.tensor_tensor(tsq[:, 0:nb, :], tcn[:, 0:nb, :], pb[:, 0:nb * P].rearrange("p (a b) -> p a b", a=nb), ALU.add))
                    if next_nb:
                        start_group(j + 1, next_nb)
                    lk(V.tensor_tensor(tcn[:, 0:nb, :], tsq[:, 0:nb, :], bc(sm[4], nb), ALU.mult))
                    lk(V.scalar_tensor_tensor(out=A, in0=x_in[:, blocks, :], scalar=2.0, in1=tcn[:, 0:nb, :], op0=ALU.mult, op1=ALU.add))
                    norm_a(lk, nb)
                    if before is not None:
                        dve.wait_ge(S["x_made"], j)
                        scale_split(lk, g3[0], before, 4)
                    norm_b(lk, nb, j + 1)
                    V.tensor_tensor(xn[:, 0:nb, :], tcn[:, 0:nb, :], bc(sm[4], nb), ALU.mult).then_inc(S["x_normed"], 1)
                    dve.wait_ge(S["x_normed"], j + 1)
                    return k[0]

                def start_group(j, nb):
                    V.tensor_tensor(ts[:, 0:nb, :], s_in[:, bass.ds(j * 4, nb), 0:D], alpha[:].unsqueeze(1).to_broadcast([P, nb, D]), ALU.mult).then_inc(S["s_scaled"], 1)
                start_group(0, 4)
                used = node_groups(0, 4, 4, None, base0)
                shift_k = base0 + used - K
                with dve.Fori(1, 11) as j:
                    assert node_groups(j, 4, 4, j - 1, shift_k) == K
                node_groups(11, 4, 1, 10, shift_k)
                node_groups(12, 1, 0, 11, shift_k)
                c3[0] = shift_k + 13 * K
                dve.wait_ge(S["x_made"], 13)
                scale_split(link, g3[0], 12, 1)
                dve.wait_ge(S["dinv_in"], 16)
                for _ in range(NG):
                    V.memset(dummy3[:], 0.0).then_inc(S["node_done"], 1)
                    dve.wait_ge(S["node_done"], _ + 1)
                V.memset(dummy3[:], 0.0).then_inc(S["g_taken"], 1)
                dve.wait_ge(S["g_taken"], 1)
                V.memset(dummy3[:], 0.0).then_inc(S["credits3"], 1)
                dve.wait_ge(S["credits3"], 1)
                base1 = c3[0]

                def post(c, j, par, nb):
                    n = j + 13 * c
                    w = nb * P
                    k = [0]
                    per = SPLIT if c < 2 else NORM + 1
                    start = base1 + (c * 13 * SPLIT)

                    def lk(ins):
                        k[0] += 1
                        ins.then_inc(S["dv3"], 1)
                        dve.wait_ge(S["dv3"], j * per + (start + k[0]))
                    dve.wait_ge(S["chunk_used"], n * 7 + 14)
                    V.tensor_tensor(yt[:, 0:w], py[par][:, 0:w], dinv_row[:, bass.ds(j * 512, w)], ALU.mult).then_inc(S["yt_ready"], 1)
                    dve.wait_ge(S["yt_ready"], n + 1)
                    V.memset(dummy3[:], 0.0).then_inc(S["y_taken"], 1)
                    dve.wait_ge(S["tail_done"], n + 1)
                    if c < 2:
                        scale_split(lk, g3[(c + 1) % 2], j, nb)
                    else:
                        dve.wait_ge(S["out_sent"], j * 16 + 1)
                        lk(V.tensor_tensor(ta[:, 0:nb, :], x1[:, bass.ds(j * 4, nb), :], pg[:, 0:w].rearrange("p (a b) -> p a b", a=nb), ALU.add))
                        norm(lk, nb, j + 14)
                        V.tensor_tensor(ta[:, 0:nb, :], tcn[:, 0:nb, :], bc(sm[4], nb), ALU.mult).then_inc(S["out_ready"], 1)
                        dve.wait_ge(S["out_ready"], j + 1)
                    V.memset(dummy3[:], 0.0).then_inc(S["g_taken"], 1)
                    dve.wait_ge(S["g_taken"], n + 2)
                    assert k[0] == per, (k, per)
                for c in range(3):
                    post(c, 0, c % 2, 4)
                    with dve.Fori(0, 5) as k:
                        for h in range(2):
                            post(c, k * 2 + (1 + h), (c + 1 + h) % 2, 4)
                    post(c, 11, (c + 11) % 2, 4)
                    post(c, 12, (c + 12) % 2, 1)
            phase_three = (sp_3, pool_3, pe_3, act_3, dve_3)

        block = outer.enter_context(nc.Block())

        def run(eng, n, engine):
            phase_one[n](eng)
            barrier(eng, S["phase1"])
            eng.wait_ge(S["fits_ready"], 1)
            eng.nop(nofuse=True)
            fit = nc.values_load(fits[0:1, 0:1], engines=[engine], min_val=0, max_val=1, skip_runtime_bounds_check_because="a comparison's result")
            with eng.If(fit == 1):
                phase_two[n](eng)
                barrier(eng, S["phase2"])
                phase_three[n](eng)
            with eng.Else():
                general[n](eng)

        @block.sync
        def _(sp):
            run(sp, 0, mybir.EngineType.SP)

        @block.gpsimd
        def _(pool):
            run(pool, 1, mybir.EngineType.Pool)

        @block.tensor
        def _(pe):
            run(pe, 2, mybir.EngineType.PE)

        @block.scalar
        def _(act):
            run(act, 3, mybir.EngineType.Activation)

        @block.vector
        def _(dve):
            run(dve, 4, mybir.EngineType.DVE)


def host_arrays(x, src, dst, edge_attr_2, L0_gnn_W1, L0_gnn_b1, L0_gnn_gamma, L0_gnn_beta, L0_gnn_W2, L0_gnn_b2,
                L1_gnn_W0, L1_gnn_b0, L1_gnn_W1, L1_gnn_b1, L1_gnn_W2, L1_gnn_b2):
    import numpy as np

    def cols(a, pad, lead):
        a = np.asarray(a)
        o = np.full((COLS * P,) + a.shape[1:], pad, a.dtype)
        o[:LEAD * P] = lead
        o[LEAD * P:LEAD * P + EDGES] = a
        return np.ascontiguousarray(np.moveaxis(o.reshape((COLS, P) + a.shape[1:]), 0, 1))

    def row(a):
        return np.asarray(a).reshape(1, -1)
    xr = np.zeros((ROWS, D), np.float32)
    xr[:NODES] = np.asarray(x)
    dst_t = cols(dst, NODES - 1, 0)
    p = np.arange(P)
    wrep = np.asarray(L0_gnn_W1)[2 * D + p % 2]
    masks = np.zeros((P, 8), np.float32)
    for j in range(3):
        masks[:, j] = (p % 32 < 18) & ((p % 32) // 2 % 3 == j)
    for k in range(4):
        masks[:, 3 + k] = p // 32 == k
    c = np.arange(COLS)
    above = (STRIP * (c // P + 1)).astype(np.float32)[None]
    least = (STRIP * np.maximum(-(-(c - (IT * UT - 1)) // P), 0)).astype(np.float32)[None]
    return dict(
        src_t=cols(src, B * P, B * P), dst_t=dst_t, d0_row=np.ascontiguousarray(dst_t[0:1]),
        attr_t=np.ascontiguousarray(cols(edge_attr_2, 0, 0)[:, LEAD:LEAD + RT * RC]),
        iotak=np.tile(np.arange(B, dtype=np.float32), (P, 1)), iota_lo=np.tile(np.arange(P, dtype=np.float32), (P, 1)).astype(np.float16),
        iota_key=np.tile(np.arange(SPAN * B, dtype=np.float32), (P, 1)).astype(np.float16),
        upper=np.triu(np.ones((P, P), np.float32), 1).astype(np.float16), ident_h=np.eye(P, dtype=np.float16),
        ident_f=np.eye(P, dtype=np.float32), empty=np.tile(np.array([np.array(ROWS - 1, np.int32).view(np.float32), -1, 0, 0], np.float32), (P, SLOTS)),
        x=xr, xT=np.ascontiguousarray(xr.T), w1=np.asarray(L0_gnn_W1), wrep=wrep, masks=masks,
        b1=row(L0_gnn_b1), gamma=row(L0_gnn_gamma), beta=row(L0_gnn_beta), b2=row(L0_gnn_b2), w2=np.asarray(L0_gnn_W2),
        cw0=np.asarray(L1_gnn_W0), cw1=np.asarray(L1_gnn_W1), cw2=np.asarray(L1_gnn_W2),
        cb0=row(L1_gnn_b0), cb1=row(L1_gnn_b1), cb2=row(L1_gnn_b2),
        lower=np.tril(np.ones((P, P), np.float32), -1), src=np.asarray(src).reshape(-1, 1), dst=np.asarray(dst).reshape(-1, 1), attr=np.asarray(edge_attr_2),
        least=least, above=above,
        cbT=np.ascontiguousarray(np.stack([np.asarray(L1_gnn_b0), np.asarray(L1_gnn_b1), np.asarray(L1_gnn_b2)], 1)))


def kernel(**inputs):
    import numpy as np
    import concourse.bacc as bacc
    from concourse.bass_utils import run_bass_kernel_spmd
    arrays = {"in_" + k: np.ascontiguousarray(v) for k, v in host_arrays(**inputs).items()}
    nc = bacc.Bacc("TRN2", target_bir_lowering=False, num_devices=1)
    t = {k[3:]: nc.dram_tensor(k, v.shape, mybir.dt.from_np(v.dtype), kind="ExternalInput").ap() for k, v in arrays.items()}
    out = nc.dram_tensor("out", (ROWS, D), F32, kind="ExternalOutput").ap()
    build(nc, t, out)
    r = run_bass_kernel_spmd(nc, [arrays], core_ids=[0])
    return r.results[0]["out"][:NODES]
```
